# Optimizing a Trainium2 kernel written in Bass

```python
import numpy as np
import jax
import jax.numpy as jnp

def _softmax(x, axis=-1):
    return jax.nn.softmax(x, axis=axis)

def _gelu(x):
    return jax.nn.gelu(x, approximate=True)

def _silu(x):
    return jax.nn.silu(x)

def _sigmoid(x):
    return jax.nn.sigmoid(x)

def _layernorm(x, axis=-1, eps=1e-05):
    m = jnp.mean(x, axis=axis, keepdims=True)
    v = jnp.var(x, axis=axis, keepdims=True)
    return (x - m) / jnp.sqrt(v + eps)

def _scatter_add(tgt, idx, src, axis=0):
    return tgt.at[idx].add(src)

def _segment_sum(src, seg, n):
    return jax.ops.segment_sum(src, seg, n)
kernel_name = 'mk_adaln_ffn_d4_seqx_r8_ed7787'

def setup_inputs(seed: int=0):
    np.random.seed(seed)
    _w = jnp.asarray

    def _rec_inputs():
        import jax
        import jax.numpy as jnp
        _rk = jax.random.key(seed)
        x = -7.109e-05 + 0.9999 * jax.random.normal(jax.random.fold_in(_rk, 1), (64, 32, 256), jnp.float32)
        _lenS = 32 - jax.random.randint(jax.random.fold_in(_rk, 7), (64,), 0, max(1, 32 // 4) + 1, jnp.int32)
        _lenS2 = 32 - jax.random.randint(jax.random.fold_in(_rk, 8), (64,), 0, max(1, 32 // 4) + 1, jnp.int32)
        itok_B_1_198 = jax.random.randint(jax.random.fold_in(_rk, 11), (64,), 1, 199, jnp.int32)
        itok_B_0_6 = jax.random.randint(jax.random.fold_in(_rk, 12), (64,), 0, 7, jnp.int32)
        itok_Bx257_0_4111 = jax.random.randint(jax.random.fold_in(_rk, 13), (64, 257), 0, 514, jnp.int32)
        itok_B_37_3939 = jax.random.randint(jax.random.fold_in(_rk, 14), (64,), 37, 3940, jnp.int32)
        itok_B_0_3 = jax.random.randint(jax.random.fold_in(_rk, 15), (64,), 0, 4, jnp.int32)
        return (x, itok_B_1_198, itok_B_0_6, itok_Bx257_0_4111, itok_B_37_3939, itok_B_0_3)
    x, itok_B_1_198, itok_B_0_6, itok_Bx257_0_4111, itok_B_37_3939, itok_B_0_3 = _rec_inputs()

    def _L0_cond_setup():
        import jax, jax.numpy as jnp
        import numpy as np
        B, C, T = (128, 32, 256)
        S, D = (200, 32)
        key = jax.random.key(seed)
        k1, k2, k3 = jax.random.split(key, 3)
        x = jax.random.normal(k1, (B, C, T), dtype=jnp.float32)
        conditions = jax.random.randint(k2, (B,), 0, S, dtype=jnp.int64)
        weights = jax.random.normal(k3, (S, C, D), dtype=jnp.float32) / jnp.sqrt(jnp.float32(C))
        return {'x': x, 'conditions': conditions, 'weights': weights}
    _L0_cond_all = _L0_cond_setup()
    _L0_cond_in = {k: v for k, v in _L0_cond_all.items() if k in ('weights',)}
    del _L0_cond_all

    def _L0_ffn_setup():
        import jax, jax.numpy as jnp
        import numpy as np
        B, S, D, H = (4, 256, 256, 1024)

        def fwht(x):
            orig_shape = x.shape
            n = orig_shape[-1]
            x = x.reshape(-1, n)
            h = 1
            while h < n:
                xb = x.reshape(-1, n // (2 * h), 2, h)
                a = xb[:, :, 0, :]
                b = xb[:, :, 1, :]
                x = jnp.stack([a + b, a - b], axis=2).reshape(-1, n)
                h *= 2
            scale = jnp.asarray(1.0 / np.sqrt(n), dtype=x.dtype)
            return (x * scale).reshape(orig_shape)
        key = jax.random.key(seed)
        kx, k1, k2, k3 = jax.random.split(key, 4)
        x = jax.random.normal(kx, (B, S, D), dtype=jnp.float32)
        W1 = jax.random.normal(k1, (H, D), dtype=jnp.float32) * (1.0 / np.sqrt(D))
        W2 = jax.random.normal(k2, (D, H), dtype=jnp.float32) * (1.0 / np.sqrt(H))
        W3 = jax.random.normal(k3, (H, D), dtype=jnp.float32) * (1.0 / np.sqrt(D))
        return {'x': x, 'W1': W1, 'W2': W2, 'W3': W3}
    _L0_ffn_all = _L0_ffn_setup()
    _L0_ffn_in = {k: v for k, v in _L0_ffn_all.items() if k in ('W1', 'W2', 'W3')}
    del _L0_ffn_all

    def _L1_cond_setup():
        import jax, jax.numpy as jnp
        import numpy as np
        B, T, D_IN, D_OUT = (16, 256, 256, 256)
        N_ADAPTERS, RANK = (8, 16)
        key = jax.random.key(seed)
        k_x, k_w, k_a, k_b, k_s, k_idx = jax.random.split(key, 6)
        x = jax.random.normal(k_x, (B, T, D_IN), dtype=jnp.float32)
        W = jax.random.normal(k_w, (D_OUT, D_IN), dtype=jnp.float32) * (1.0 / np.sqrt(D_IN))
        A = jax.random.normal(k_a, (N_ADAPTERS, RANK, D_IN), dtype=jnp.float32) * 0.02
        Bm = jax.random.normal(k_b, (N_ADAPTERS, D_OUT, RANK), dtype=jnp.float32) * 0.02
        scalings = jnp.ones((N_ADAPTERS,), dtype=jnp.float32)
        adapter_idx = jax.random.randint(k_idx, (B,), 0, N_ADAPTERS, dtype=jnp.int32)
        return {'x': x, 'W': W, 'A': A, 'Bm': Bm, 'scalings': scalings, 'adapter_idx': adapter_idx}
    _L1_cond_all = _L1_cond_setup()
    _L1_cond_in = {k: v for k, v in _L1_cond_all.items() if k in ('W', 'A', 'Bm', 'scalings')}
    del _L1_cond_all

    def _L1_ffn_setup():
        import jax, jax.numpy as jnp
        import numpy as np
        NUM_EXPERTS = 32
        TOP_K = 4
        HIDDEN = 256
        INTER = 96
        key = jax.random.key(seed)
        k1, k2, k3, k4 = jax.random.split(key, 4)
        hidden_states = jax.random.normal(k1, (4, 64, HIDDEN), dtype=jnp.float32)
        gate = jax.random.normal(k2, (HIDDEN, NUM_EXPERTS), dtype=jnp.float32) * 0.02
        gate_up_proj = jax.random.normal(k3, (NUM_EXPERTS, HIDDEN, 2 * INTER), dtype=jnp.float32) * 0.02
        down_proj = jax.random.normal(k4, (NUM_EXPERTS, INTER, HIDDEN), dtype=jnp.float32) * 0.02
        return {'hidden_states': hidden_states, 'gate': gate, 'gate_up_proj': gate_up_proj, 'down_proj': down_proj}
    _L1_ffn_all = _L1_ffn_setup()
    _L1_ffn_in = {k: v for k, v in _L1_ffn_all.items() if k in ('gate', 'gate_up_proj', 'down_proj')}
    del _L1_ffn_all

    def _L2_cond_setup():
        import jax, jax.numpy as jnp
        import numpy as np
        H, G, HD = (8, 4, 32)
        GSZ = H // G
        BLOCK = 16
        WINDOW = 128
        SCALE = 256.0 ** (-0.5)
        EPS = 1e-06
        THETA = 10000.0
        B, T, D = (16, 4, 256)
        NBLK = 257

        def _rms(x, scale):
            var = jnp.mean(x * x, axis=-1, keepdims=True)
            return x * jax.lax.rsqrt(var + EPS) * (1.0 + scale)

        def _rope(x, pos):
            half = HD // 2
            inv = 1.0 / THETA ** (jnp.arange(half, dtype=jnp.float32) / half)
            ang = pos[:, :, None].astype(jnp.float32) * inv
            cos = jnp.cos(ang)[:, None, :, :]
            sin = jnp.sin(ang)[:, None, :, :]
            x1, x2 = (x[..., :half], x[..., half:])
            return jnp.concatenate([x1 * cos - x2 * sin, x2 * cos + x1 * sin], axis=-1)
        key = jax.random.key(seed)
        ks = jax.random.split(key, 10)
        inv_d = 1.0 / np.sqrt(D)
        return {'x': jax.random.normal(ks[0], (B, T, D), jnp.float32), 'Wq': jax.random.normal(ks[1], (H * HD, D), jnp.float32) * inv_d, 'Wk': jax.random.normal(ks[2], (G * HD, D), jnp.float32) * inv_d, 'Wv': jax.random.normal(ks[3], (G * HD, D), jnp.float32) * inv_d, 'Wo': jax.random.normal(ks[4], (D, H * HD), jnp.float32) * inv_d, 'q_norm_scale': jax.random.normal(ks[5], (HD,), jnp.float32) * 0.02, 'k_norm_scale': jax.random.normal(ks[6], (HD,), jnp.float32) * 0.02, 'k_blocks': jax.random.normal(ks[7], (B * NBLK, G, BLOCK, HD), jnp.float32), 'v_blocks': jax.random.normal(ks[8], (B * NBLK, G, BLOCK, HD), jnp.float32), 'block_tables': jnp.arange(B * NBLK, dtype=jnp.int32).reshape(B, NBLK), 'kv_lens': jax.random.randint(ks[9], (B,), 0, 512, dtype=jnp.int32)}
    _L2_cond_all = _L2_cond_setup()
    _L2_cond_in = {k: v for k, v in _L2_cond_all.items() if k in ('Wq', 'Wk', 'Wv', 'Wo', 'q_norm_scale', 'k_norm_scale', 'k_blocks', 'v_blocks')}
    del _L2_cond_all

    def _L2_ffn_setup():
        import jax, jax.numpy as jnp
        import numpy as np
        B, S, D = (4, 512, 256)
        DFF = 4 * D
        SKIP = 0.125
        key = jax.random.key(seed)
        ks = jax.random.split(key, 4)
        s_in = 1.0 / np.sqrt(D).astype(np.float32)
        s_ff = 1.0 / np.sqrt(DFF).astype(np.float32)
        return {'x': jax.random.normal(ks[0], (B, S, D), jnp.float32), 'Wr': jax.random.normal(ks[1], (D, 1), jnp.float32) * s_in, 'br': jnp.zeros((1,), jnp.float32), 'W1': jax.random.normal(ks[2], (D, DFF), jnp.float32) * s_in, 'b1': jnp.zeros((DFF,), jnp.float32), 'W2': jax.random.normal(ks[3], (DFF, D), jnp.float32) * s_ff, 'b2': jnp.zeros((D,), jnp.float32)}
    _L2_ffn_all = _L2_ffn_setup()
    _L2_ffn_in = {k: v for k, v in _L2_ffn_all.items() if k in ('Wr', 'br', 'W1', 'b1', 'W2', 'b2')}
    del _L2_ffn_all

    def _L3_cond_setup():
        import jax, jax.numpy as jnp
        import numpy as np
        B, S, D_IN, D_OUT, R, E = (8, 256, 256, 256, 16, 4)
        key = jax.random.key(seed)
        ks = jax.random.split(key, 7)
        x = jax.random.normal(ks[0], (B, S, D_IN), dtype=jnp.float32)
        W_base = jax.random.normal(ks[1], (D_OUT, D_IN), dtype=jnp.float32) * 0.02
        Wt = jax.random.normal(ks[2], (D_IN, D_IN), dtype=jnp.float32) * 0.02
        A = jax.random.normal(ks[3], (E, R, D_IN), dtype=jnp.float32) * 0.02
        B_w = jax.random.normal(ks[4], (E, D_OUT, R), dtype=jnp.float32) * 0.02
        Wp = jax.random.normal(ks[5], (D_OUT, D_OUT), dtype=jnp.float32) * 0.02
        scaling = jnp.ones((E,), dtype=jnp.float32)
        adapter_idx = jax.random.randint(ks[6], (B,), 0, E)
        return {'x': x, 'W_base': W_base, 'Wt': Wt, 'A': A, 'B_w': B_w, 'Wp': Wp, 'scaling': scaling, 'adapter_idx': adapter_idx}
    _L3_cond_all = _L3_cond_setup()
    _L3_cond_in = {k: v for k, v in _L3_cond_all.items() if k in ('W_base', 'Wt', 'A', 'B_w', 'Wp', 'scaling')}
    del _L3_cond_all

    def _L3_ffn_setup():
        import jax, jax.numpy as jnp
        import numpy as np
        H = 256
        E = 8
        TOP_K = 2
        I_MOE = 176
        I_SH = 704
        BS, NT = (2, 64)
        key = jax.random.key(seed)
        ks = jax.random.split(key, 7)
        s = lambda d: (1.0 / np.sqrt(d)).astype(np.float32)
        return {'hidden_states': jax.random.normal(ks[0], (BS, NT, H), jnp.float32), 'gate_w': jax.random.normal(ks[1], (E, H), jnp.float32) * s(H), 'w1': jax.random.normal(ks[2], (E, 2 * I_MOE, H), jnp.float32) * s(H), 'w2': jax.random.normal(ks[3], (E, H, I_MOE), jnp.float32) * s(I_MOE), 'shared_gate_up_w': jax.random.normal(ks[4], (2 * I_SH, H), jnp.float32) * s(H), 'shared_down_w': jax.random.normal(ks[5], (H, I_SH), jnp.float32) * s(I_SH), 'shared_gate_w': jax.random.normal(ks[6], (1, H), jnp.float32) * s(H)}
    _L3_ffn_all = _L3_ffn_setup()
    _L3_ffn_in = {k: v for k, v in _L3_ffn_all.items() if k in ('gate_w', 'w1', 'w2', 'shared_gate_up_w', 'shared_down_w', 'shared_gate_w')}
    del _L3_ffn_all
    return {'x': x, 'itok_B_1_198': itok_B_1_198, 'itok_B_0_6': itok_B_0_6, 'itok_Bx257_0_4111': itok_Bx257_0_4111, 'itok_B_37_3939': itok_B_37_3939, 'itok_B_0_3': itok_B_0_3, 'L0_cond_weights': _L0_cond_in['weights'], 'L0_ffn_W1': _L0_ffn_in['W1'], 'L0_ffn_W2': _L0_ffn_in['W2'], 'L0_ffn_W3': _L0_ffn_in['W3'], 'L1_cond_W': _L1_cond_in['W'], 'L1_cond_A': _L1_cond_in['A'], 'L1_cond_Bm': _L1_cond_in['Bm'], 'L1_cond_scalings': _L1_cond_in['scalings'], 'L1_ffn_gate': _L1_ffn_in['gate'], 'L1_ffn_gate_up_proj': _L1_ffn_in['gate_up_proj'], 'L1_ffn_down_proj': _L1_ffn_in['down_proj'], 'L2_cond_Wq': _L2_cond_in['Wq'], 'L2_cond_Wk': _L2_cond_in['Wk'], 'L2_cond_Wv': _L2_cond_in['Wv'], 'L2_cond_Wo': _L2_cond_in['Wo'], 'L2_cond_q_norm_scale': _L2_cond_in['q_norm_scale'], 'L2_cond_k_norm_scale': _L2_cond_in['k_norm_scale'], 'L2_cond_k_blocks': _L2_cond_in['k_blocks'], 'L2_cond_v_blocks': _L2_cond_in['v_blocks'], 'L2_ffn_Wr': _L2_ffn_in['Wr'], 'L2_ffn_br': _L2_ffn_in['br'], 'L2_ffn_W1': _L2_ffn_in['W1'], 'L2_ffn_b1': _L2_ffn_in['b1'], 'L2_ffn_W2': _L2_ffn_in['W2'], 'L2_ffn_b2': _L2_ffn_in['b2'], 'L3_cond_W_base': _L3_cond_in['W_base'], 'L3_cond_Wt': _L3_cond_in['Wt'], 'L3_cond_A': _L3_cond_in['A'], 'L3_cond_B_w': _L3_cond_in['B_w'], 'L3_cond_Wp': _L3_cond_in['Wp'], 'L3_cond_scaling': _L3_cond_in['scaling'], 'L3_ffn_gate_w': _L3_ffn_in['gate_w'], 'L3_ffn_w1': _L3_ffn_in['w1'], 'L3_ffn_w2': _L3_ffn_in['w2'], 'L3_ffn_shared_gate_up_w': _L3_ffn_in['shared_gate_up_w'], 'L3_ffn_shared_down_w': _L3_ffn_in['shared_down_w'], 'L3_ffn_shared_gate_w': _L3_ffn_in['shared_gate_w']}

def reference(x, itok_B_1_198, itok_B_0_6, itok_Bx257_0_4111, itok_B_37_3939, itok_B_0_3, L0_cond_weights, L0_ffn_W1, L0_ffn_W2, L0_ffn_W3, L1_cond_W, L1_cond_A, L1_cond_Bm, L1_cond_scalings, L1_ffn_gate, L1_ffn_gate_up_proj, L1_ffn_down_proj, L2_cond_Wq, L2_cond_Wk, L2_cond_Wv, L2_cond_Wo, L2_cond_q_norm_scale, L2_cond_k_norm_scale, L2_cond_k_blocks, L2_cond_v_blocks, L2_ffn_Wr, L2_ffn_br, L2_ffn_W1, L2_ffn_b1, L2_ffn_W2, L2_ffn_b2, L3_cond_W_base, L3_cond_Wt, L3_cond_A, L3_cond_B_w, L3_cond_Wp, L3_cond_scaling, L3_ffn_gate_w, L3_ffn_w1, L3_ffn_w2, L3_ffn_shared_gate_up_w, L3_ffn_shared_down_w, L3_ffn_shared_gate_w):
    import jax
    import jax.numpy as jnp

    def _L0_cond_ref(x, conditions, weights):
        import jax, jax.numpy as jnp
        import numpy as np
        B, C, T = (128, 32, 256)
        S, D = (200, 32)
        w = weights[conditions]
        return jnp.einsum('bct,bcd->bdt', x, w)

    def _L0_ffn_ref(x, W1, W2, W3):
        import jax, jax.numpy as jnp
        import numpy as np
        B, S, D, H = (4, 256, 256, 1024)

        def fwht(x):
            orig_shape = x.shape
            n = orig_shape[-1]
            x = x.reshape(-1, n)
            h = 1
            while h < n:
                xb = x.reshape(-1, n // (2 * h), 2, h)
                a = xb[:, :, 0, :]
                b = xb[:, :, 1, :]
                x = jnp.stack([a + b, a - b], axis=2).reshape(-1, n)
                h *= 2
            scale = jnp.asarray(1.0 / np.sqrt(n), dtype=x.dtype)
            return (x * scale).reshape(orig_shape)
        up_gate = jnp.einsum('bsd,hd->bsh', x, W1)
        up_lin = jnp.einsum('bsd,hd->bsh', x, W3)
        hidden = jax.nn.silu(up_gate) * up_lin
        hidden = fwht(hidden)
        out = jnp.einsum('bsh,dh->bsd', hidden, W2)
        return out

    def _L1_cond_ref(x, W, A, Bm, scalings, adapter_idx):
        import jax, jax.numpy as jnp
        import numpy as np
        B, T, D_IN, D_OUT = (16, 256, 256, 256)
        N_ADAPTERS, RANK = (8, 16)
        H = jnp.einsum('btd,od->bto', x, W)
        A_b = A[adapter_idx]
        B_b = Bm[adapter_idx]
        s_b = scalings[adapter_idx]
        xa = jnp.einsum('btd,brd->btr', x, A_b)
        delta = jnp.einsum('btr,bor->bto', xa, B_b)
        delta = jax.lax.stop_gradient(delta * s_b[:, None, None])
        return H + delta

    def _L1_ffn_ref(hidden_states, gate, gate_up_proj, down_proj):
        import jax, jax.numpy as jnp
        import numpy as np
        NUM_EXPERTS = 32
        TOP_K = 4
        HIDDEN = 256
        INTER = 96
        batch_size = hidden_states.shape[0]
        x = hidden_states.reshape(-1, HIDDEN)
        num_tokens = x.shape[0]
        router_logits = jnp.einsum('TD,DE->TE', x, gate)
        routing_weights = jax.nn.softmax(router_logits.astype(jnp.float32), axis=-1)
        top_k_weights, top_k_indices = jax.lax.top_k(routing_weights, TOP_K)
        top_k_weights = top_k_weights / top_k_weights.sum(axis=-1, keepdims=True)
        top_k_weights = top_k_weights.astype(x.dtype)
        router_weights = jnp.zeros((num_tokens, NUM_EXPERTS), dtype=x.dtype)
        token_indices = jnp.broadcast_to(jnp.arange(num_tokens)[:, None], top_k_indices.shape)
        router_weights = router_weights.at[token_indices, top_k_indices].set(top_k_weights)
        gate_up = jnp.einsum('TD,EDF->TEF', x, gate_up_proj)
        g, u = jnp.split(gate_up, 2, axis=-1)
        gated = u * jax.nn.silu(g)
        next_states = jnp.einsum('TEF,EFD->TED', gated, down_proj)
        next_states = (next_states * router_weights[..., None]).sum(axis=1)
        return next_states.reshape(batch_size, -1, HIDDEN)

    def _L2_cond_ref(x, Wq, Wk, Wv, Wo, q_norm_scale, k_norm_scale, k_blocks, v_blocks, block_tables, kv_lens):
        import jax, jax.numpy as jnp
        import numpy as np
        H, G, HD = (8, 4, 32)
        GSZ = H // G
        BLOCK = 16
        WINDOW = 128
        SCALE = 256.0 ** (-0.5)
        EPS = 1e-06
        THETA = 10000.0
        B, T, D = (16, 4, 256)
        NBLK = 257

        def _rms(x, scale):
            var = jnp.mean(x * x, axis=-1, keepdims=True)
            return x * jax.lax.rsqrt(var + EPS) * (1.0 + scale)

        def _rope(x, pos):
            half = HD // 2
            inv = 1.0 / THETA ** (jnp.arange(half, dtype=jnp.float32) / half)
            ang = pos[:, :, None].astype(jnp.float32) * inv
            cos = jnp.cos(ang)[:, None, :, :]
            sin = jnp.sin(ang)[:, None, :, :]
            x1, x2 = (x[..., :half], x[..., half:])
            return jnp.concatenate([x1 * cos - x2 * sin, x2 * cos + x1 * sin], axis=-1)
        Bx, Tx, _ = x.shape
        q = jnp.einsum('btd,od->bto', x, Wq).reshape(Bx, Tx, H, HD).transpose(0, 2, 1, 3)
        k = jnp.einsum('btd,od->bto', x, Wk).reshape(Bx, Tx, G, HD).transpose(0, 2, 1, 3)
        v = jnp.einsum('btd,od->bto', x, Wv).reshape(Bx, Tx, G, HD).transpose(0, 2, 1, 3)
        q = _rms(q, q_norm_scale)
        k = _rms(k, k_norm_scale)
        pos = kv_lens[:, None] + jnp.arange(Tx, dtype=jnp.int32)
        q = _rope(q, pos)
        k = _rope(k, pos)
        slot = pos // BLOCK
        off = pos % BLOCK
        blk = jnp.take_along_axis(block_tables, slot, axis=1)
        k_blocks = k_blocks.at[blk, :, off, :].set(k.transpose(0, 2, 1, 3))
        v_blocks = v_blocks.at[blk, :, off, :].set(v.transpose(0, 2, 1, 3))
        k_all = k_blocks[block_tables].transpose(0, 2, 1, 3, 4).reshape(Bx, G, -1, HD)
        v_all = v_blocks[block_tables].transpose(0, 2, 1, 3, 4).reshape(Bx, G, -1, HD)
        S = k_all.shape[2]
        qg = q.reshape(Bx, G, GSZ, Tx, HD)
        scores = jnp.einsum('bghtd,bgsd->bghts', qg, k_all) * SCALE
        kpos = jnp.arange(S, dtype=jnp.int32)
        allowed = (kpos[None, None, :] <= pos[:, :, None]) & (kpos[None, None, :] > pos[:, :, None] - WINDOW)
        scores = jnp.where(allowed[:, None, None, :, :], scores, -jnp.inf)
        p = jax.nn.softmax(scores, axis=-1)
        o = jnp.einsum('bghts,bgsd->bghtd', p, v_all).reshape(Bx, H, Tx, HD)
        o = o.transpose(0, 2, 1, 3).reshape(Bx, Tx, H * HD)
        return jnp.einsum('bto,do->btd', o, Wo)

    def _L2_ffn_ref(x, Wr, br, W1, b1, W2, b2):
        import jax, jax.numpy as jnp
        import numpy as np
        B, S, D = (4, 512, 256)
        DFF = 4 * D
        SKIP = 0.125
        Bs, Ss, Ds = x.shape
        k = max(int(Ss * SKIP), 1)
        logits = (x @ Wr + br)[..., 0]
        weights, idx = jax.lax.top_k(logits, k)
        perm = jnp.argsort(idx, axis=1)
        tokens = jnp.take_along_axis(idx, perm, axis=1)
        fx = jnp.take_along_axis(x, tokens[..., None], axis=1)
        h = jax.nn.gelu(fx @ W1 + b1, approximate=False)
        out_l = h @ W2 + b2
        tw = jax.nn.softmax(weights, axis=1)
        rw = jnp.take_along_axis(tw, perm, axis=1)
        xw = rw[..., None] * out_l
        bidx = jnp.arange(Bs)[:, None]
        return x.at[bidx, tokens].add(xw)

    def _L3_cond_ref(x, W_base, Wt, A, B_w, Wp, scaling, adapter_idx):
        import jax, jax.numpy as jnp
        import numpy as np
        B, S, D_IN, D_OUT, R, E = (8, 256, 256, 256, 16, 4)
        base = jnp.einsum('bsi,oi->bso', x, W_base)
        h = jnp.einsum('bsi,ji->bsj', x, Wt)
        Ab = A[adapter_idx]
        Bb = B_w[adapter_idx]
        sc = scaling[adapter_idx]
        z = jnp.einsum('bsj,brj->bsr', h, Ab)
        l = jnp.einsum('bsr,bor->bso', z, Bb)
        lora_out = jnp.einsum('bso,po->bsp', l, Wp) * sc[:, None, None]
        return base + lora_out

    def _L3_ffn_ref(hidden_states, gate_w, w1, w2, shared_gate_up_w, shared_down_w, shared_gate_w):
        import jax, jax.numpy as jnp
        import numpy as np
        H = 256
        E = 8
        TOP_K = 2
        I_MOE = 176
        I_SH = 704
        BS, NT = (2, 64)
        bs, nt, h = hidden_states.shape
        x = hidden_states.reshape(-1, h)
        T = x.shape[0]
        gu = x @ shared_gate_up_w.T
        g, u = jnp.split(gu, 2, axis=-1)
        shared = jax.nn.silu(g) * u @ shared_down_w.T
        shared = jax.nn.sigmoid(x @ shared_gate_w.T) * shared
        logits = x @ gate_w.T
        probs = jax.nn.softmax(logits.astype(jnp.float32), axis=-1)
        top_w, top_i = jax.lax.top_k(probs, TOP_K)
        top_w = top_w / jnp.sum(top_w, axis=-1, keepdims=True)
        combine = jnp.zeros((T, E), top_w.dtype).at[jnp.arange(T)[:, None], top_i].set(top_w)
        gu_e = jnp.einsum('th,eih->tei', x, w1)
        ge, ue = jnp.split(gu_e, 2, axis=-1)
        he = jax.nn.silu(ge) * ue
        ye = jnp.einsum('tei,ehi->teh', he, w2)
        out = jnp.einsum('teh,te->th', ye, combine.astype(x.dtype)) + shared
        return out.reshape(bs, nt, h)
    x = x + _L0_ffn_ref(_L0_cond_ref(x, itok_B_1_198, L0_cond_weights), L0_ffn_W1, L0_ffn_W2, L0_ffn_W3)
    x = x + _L1_ffn_ref(_L1_cond_ref(x, L1_cond_W, L1_cond_A, L1_cond_Bm, L1_cond_scalings, itok_B_0_6), L1_ffn_gate, L1_ffn_gate_up_proj, L1_ffn_down_proj)
    x = x + _L2_ffn_ref(_L2_cond_ref(x, L2_cond_Wq, L2_cond_Wk, L2_cond_Wv, L2_cond_Wo, L2_cond_q_norm_scale, L2_cond_k_norm_scale, L2_cond_k_blocks, L2_cond_v_blocks, itok_Bx257_0_4111, itok_B_37_3939), L2_ffn_Wr, L2_ffn_br, L2_ffn_W1, L2_ffn_b1, L2_ffn_W2, L2_ffn_b2)
    x = x + _L3_ffn_ref(_L3_cond_ref(x, L3_cond_W_base, L3_cond_Wt, L3_cond_A, L3_cond_B_w, L3_cond_Wp, L3_cond_scaling, itok_B_0_3), L3_ffn_gate_w, L3_ffn_w1, L3_ffn_w2, L3_ffn_shared_gate_up_w, L3_ffn_shared_down_w, L3_ffn_shared_gate_w)
    return x

_drawn_inputs = setup_inputs


def setup_inputs(seed=0):
    import zlib

    import numpy as np

    out = dict(_drawn_inputs(seed))
    spreads = {'L1_cond_scalings': (1.0, 0.2),
     'L2_ffn_b1': (0.0, 0.1),
     'L2_ffn_b2': (0.0, 0.1),
     'L3_cond_scaling': (1.0, 0.2)}
    factors = {}
    for name, (base, spread) in spreads.items():
        noise = np.random.default_rng([zlib.crc32(name.encode()), seed]).standard_normal(out[name].shape)
        drawn = base * np.exp(spread * noise) if base else spread * noise
        out[name] = jnp.asarray(drawn.astype(out[name].dtype))
    for name, factor in factors.items():
        out[name] = (out[name] * factor).astype(out[name].dtype)
    return out
```

```python
from contextlib import ExitStack

import numpy as np

import concourse.bass as bass
from concourse import mybir

ALU = mybir.AluOpType
ACT = mybir.ActivationFunctionType
F32 = mybir.dt.float32
BF16 = mybir.dt.bfloat16
I32 = mybir.dt.int32
X = mybir.AxisListType.X

P = 128
B, S, D = 64, 32, 256
T = B * S
KD = D // P
NT = T // P
CH = 512
NCH = T // CH
TPC = CH // P
BPT, BPC = P // S, CH // S
H0 = 1024
E1, K1, F1 = 32, 4, 96
E3, K3, F3, FS = 8, 2, 176, 704
R = 16
G, GS, HD = 4, 2, 32
BLOCK, WINDOW, NBLK, NROWS = 16, 128, 257, 4112
WB = WINDOW // BLOCK + S // BLOCK + 1
WK = WB * BLOCK
NEWB = S // BLOCK + 1
SEGS = NEWB * B
WG = 8
WGR = WG * WB
ROW = BLOCK * 2 * G * HD
KW = G * HD
SEL = 4
H2 = 1024
EPS = 1e-6
FAR = float(2 ** 17)
MASKED = -1e30


def pieces(total):
    return [min(P, total - a) for a in range(0, total, P)]


class Moe:

    def __init__(self, experts, chosen, shared, rank, total, step0, chunk0, acc0, piece0):
        self.E, self.K, self.Z = experts, chosen, rank
        self.EW = experts + shared
        self.shared = shared
        self.total = total
        self.widths = pieces(total)
        self.M = len(self.widths)
        self.step0, self.chunk0, self.acc0, self.piece0 = step0, chunk0, acc0, piece0
        self.links = 18 if shared else 16


M0 = H0 // P
L1 = Moe(E1, K1, 0, 8 * R, E1 * F1, NCH * M0, 0, NCH, 0)
L3 = Moe(E3, K3, 1, 4 * R, E3 * F3 + FS, NCH * (M0 + L1.M), NCH, 3 * NCH, NCH * L1.M)
N1, N3 = L1.total, L3.total
TAIL_LINKS = 17
O_CREDIT = 16
MAGIC = 1.5 * 2 ** 23
TWO_PI_HI = 6.28125
TWO_PI_LO = float(2 * np.pi - 6.28125)


def constants():
    p = np.arange(P)
    t = p % S
    had = np.array([[1.0]])
    while had.shape[0] < P:
        had = np.block([[had, had], [had, -had]])
    half = HD // 2
    inv = (np.float32(1.0) / (np.float32(10000.0) ** (np.arange(half, dtype=np.float32) / np.float32(half))))
    seg_j, seg_b = np.repeat(np.arange(NEWB), B), np.tile(np.arange(B), NEWB)
    c = np.arange(WK)
    sel_t, sel_b = np.repeat(np.arange(TPC), BPT * SEL), np.tile(np.repeat(np.arange(BPT), SEL), TPC)

    def rows(x):
        return np.broadcast_to(np.asarray(x, np.float32).reshape(1, -1), (P, np.size(x)))

    late = {
        "ident": np.eye(P),
        "had": had / 32.0,
        "restart32": rows((np.arange(TPC * E1) % E1) != 0),
        "restart8": rows((np.arange(TPC * E3) % E3) != 0),
        "samebatch": (p[:, None] // S) == (p[None, :] // S),
        "own": t[:, None] == np.arange(S)[None, :],
        "before": np.arange(S)[None, :] < t[:, None],
        "place": (sel_b[None, None, :] == (p // S)[:, None, None])
        & (sel_t[None, None, :] == np.arange(TPC)[None, :, None]),
        "rank": rows(np.tile(np.arange(SEL), TPC * BPT)),
        "rowt": t[:, None],
        "ones": np.ones((P, P)),
    }
    first = {
        "slots": rows(np.arange(NBLK)),
        "segid": rows(1 + np.arange(SEGS)),
        "prio": rows(seg_b * 4 + seg_j + 1),
        "off": rows(np.arange(BLOCK)),
        "win": rows(np.arange(WB) - WINDOW // BLOCK),
        "myprio": np.stack([(p % B) * 4 + p // B + 1, (p % B) * 4 + 3], axis=1),
        "shift": rows(np.arange(NEWB * BLOCK)[None, :] - np.arange(S)[:, None]),
        "key": rows(c),
        "keyless": c[None, :] - t[:, None],
        "inv": rows(inv),
    }

    def sels(L, owner):
        x = np.zeros((P, L.M * P), np.float32)
        for j in range(3):
            x[j * L.EW + owner, np.arange(L.total)] = 1
        return x

    tsel = np.stack([((p[:, None] // S) == q) & ((p[:, None] % S) == (p[None, :] % S)) for q in range(BPT)], 1)
    cast = {
        "identb": np.eye(P),
        "tselb": tsel,
        "sel1": sels(L1, np.arange(N1) // F1),
        "sel3": sels(L3, np.minimum(np.arange(N3) // F3, E3)),
    }

    def pack(d):
        at, out, o = {}, [], 0
        for name, x in d.items():
            x = np.asarray(x, np.float32).reshape(P, -1)
            at[name] = (o, x.shape[1])
            o += x.shape[1]
            out.append(x)
        return at, np.ascontiguousarray(np.concatenate(out, axis=1))

    return pack(late), pack(first), pack(cast)


class Chain:

    def __init__(self, eng, sem, base=0):
        self.eng, self.sem, self.base, self.n = eng, sem, base, 0

    def link(self, ins):
        self.n += 1
        ins.then_inc(self.sem, 1)
        self.eng.wait_ge(self.sem, self.base + self.n)


def build(nc, a):
    (late_at, _), (first_at, _), (cast_at, _) = constants()
    with ExitStack() as ctx:
        def sb(name, shape, dt=F32):
            return ctx.enter_context(nc.sbuf_tensor(name, shape, dt))

        def sem(name):
            return ctx.enter_context(nc.semaphore(name))

        ps = ctx.enter_context(nc.psum_tensor("ps", [P, 8, 512], F32))

        newblk = nc.dram_tensor("newblk", (SEGS, ROW), F32).ap()
        tab_d = nc.dram_tensor("tab_d", (B, WB), F32).ap()
        dest_d = nc.dram_tensor("dest_d", (B, NEWB * BLOCK), F32).ap()
        tok_d = nc.dram_tensor("tok_d", (B, S), I32).ap()

        xT = sb("xT", [P, KD, T])
        yT = sb("yT", [P, KD, T])
        qT = yT
        big = sb("big", [P, 2 * KD * N3 + L3.M * D])
        l1_gate = big[:, 0:KD * N1].rearrange("p (k n) -> p k n", k=KD)
        l1_up = big[:, KD * N1:2 * KD * N1].rearrange("p (k n) -> p k n", k=KD)
        l3_gate = big[:, 0:KD * N3].rearrange("p (k n) -> p k n", k=KD)
        l3_up = big[:, KD * N3:2 * KD * N3].rearrange("p (k n) -> p k n", k=KD)
        l3_down = big[:, 2 * KD * N3:].rearrange("p (m n) -> p m n", n=D)
        stage = big[:, 0:2 * ROW].rearrange("p (j n) -> p j n", j=2)
        rest = big[:, 2 * ROW:]
        early = sb("early", [P, 12288])
        l0_w1 = early[:, 0:2048].rearrange("p (k n) -> p k n", k=KD)
        l0_w3 = early[:, 2048:4096].rearrange("p (k n) -> p k n", k=KD)
        l0_down = early[:, 4096:6144].rearrange("p (m n) -> p m n", n=D)
        w2mix = early[:, 6144:8192].rearrange("p (c n) -> p c n", n=D)
        xrows = early[:, 8192:12288].rearrange("p (i n) -> p i n", n=D)
        l1_down = early[:, 6144:12288].rearrange("p (m n) -> p m n", n=D)
        kvw = early[:, 0:ROW].rearrange("p (o n) -> p o n", o=BLOCK)
        kv2 = early[:, ROW:2 * ROW].rearrange("p (s h b n) -> p s h b n", s=2, h=2, b=BPT)
        scr = early[:, 2 * ROW:3 * ROW]
        qkn = scr[:, 0:1536]
        sqr = scr[:, 1536:3072]
        kvrow = scr[:, 3072:4096].rearrange("p (t n) -> p t n", t=TPC)
        KTs = scr[:, 0:352].rearrange("p (s n) -> p s n", s=2)
        Pex = scr[:, 352:1056].rearrange("p (s h n) -> p s h n", s=2, h=2)
        Pn = scr[:, 1056:1760].rearrange("p (s h n) -> p s h n", s=2, h=2)
        PTs = scr[:, 1760:2784].rearrange("p (s h n) -> p s h n", s=2, h=2)
        Qbd = scr[:, 3072:4096].rearrange("p (s b n) -> p s b n", s=2, b=2)
        acol = scr[:, 2784:2800].rearrange("p (a s h) -> p a s h", a=4, s=2)
        mid = sb("mid", [P, 6144])
        F = {n: mid[:, 3072 + o:3072 + o + w] for n, (o, w) in first_at.items()}
        first_n = sum(w for _, w in first_at.values())
        assert 3072 + first_n <= 6144
        seen = mid[:, 0:3072]
        wqkv = mid[:, 0:1024].rearrange("p (k n) -> p k n", k=KD)
        wo = mid[:, 1024:1536].rearrange("p (g n) -> p g n", g=GS)
        w21 = mid[:, 1536:3584].rearrange("p (k n) -> p k n", k=KD)
        w22 = mid[:, 3584:5632].rearrange("p (m n) -> p m n", n=D)

        late = sb("late", [P, sum(w for _, w in late_at.values())])
        C = {n: late[:, o:o + w] for n, (o, w) in late_at.items()}
        ident = C["ident"]
        identb = sb("identb", [P, P], BF16)
        tselb = sb("tselb", [P, BPT, P], BF16)
        selb = sb("selb", [P, L1.M * P], BF16)
        maskb = sb("maskb", [P, NT * WK], BF16)
        cosb = sb("cosb", [P, NT, HD // 2])
        sinb = sb("sinb", [P, NT, HD // 2])
        gain = sb("gain", [P, (G * GS + G) * HD])
        wr = sb("wr", [P, D])
        b21 = sb("b21", [P, H2 // P])
        b22 = sb("b22", [1, D])
        br = sb("br", [P, 1])
        small1 = sb("small1", [P, KD, D + P + L1.EW])
        b1s = sb("b1s", [P, D])
        small3 = sb("small3", [P, KD, D + L3.EW])
        work = sb("work", [P, 2560])
        silu = work[:, 0:1024].rearrange("p (s n) -> p s n", s=2)
        hid = work[:, 1024:2048].rearrange("p (s n) -> p s n", s=2)
        prod = work[:, 2048:2560]
        wdiag = work[:, 0:2048].rearrange("p (i n) -> p i n", n=P)
        raw3 = work[:, 0:1280].rearrange("p (k n) -> p k n", k=KD)
        ycur = sb("ycur", [P, KD, CH])
        oT = ycur
        ytok = work[:, 0:1024].rearrange("p (t n) -> p t n", t=TPC)
        ywr = scr[:, 0:1024].rearrange("p (t n) -> p t n", t=TPC)
        hT2 = work[:, 1024:1536].rearrange("p (m n) -> p m n", n=TPC * BPT * SEL)
        pwT = prod
        fx = scr[:, 1024:1152].rearrange("p (d n) -> p d n", d=KD)
        outl = scr[:, 1152:1408]
        pick = scr[:, 1408:1664].rearrange("p (t n) -> p t n", t=TPC)
        pickw = scr[:, 1664:1920].rearrange("p (t n) -> p t n", t=TPC)
        lcol = scr[:, 2800:2864].rearrange("p (a t) -> p a t", t=TPC)
        lex = scr[:, 2864:2884].rearrange("p (t n) -> p t n", t=TPC)
        lexe = scr[:, 2884:2904].rearrange("p (t n) -> p t n", t=TPC)
        zm = sb("zm", [P, CH])
        awt = sb("awt", [P, KD, 64])
        wpb = sb("wpb", [64, D])
        top8 = sb("top8", [P, TPC, 8])
        rt = [sb(f"rt{i}", [P, TPC * L1.EW]) for i in range(6)]
        rcol = sb("rcol", [P, 5, TPC])
        parts = sb("parts", [P, TPC * 3 * L1.EW], BF16)
        partsT = sb("partsT", [3 * L1.EW, CH], BF16)
        kcol = sb("kcol", [P, 2, TPC * 12])

        wrows = prod.rearrange("p (i n) -> p i n", i=NT)
        cond_i = sb("cond_i", [P, NT], I32)
        cond_f = sb("cond_f", [P, NT])
        cond_x = sb("cond_x", [P, NT], I32)
        adapt_i = zm[:, 0:2 * B].bitcast(I32).rearrange("p (l b) -> p l b", l=2)
        adapt_f = zm[:, 2 * B:4 * B].rearrange("p (l b) -> p l b", l=2)
        adapt_s = sb("adapt_s", [P, 4])
        amask = sb("amask", [P, 2, B])
        bt_i = rest[:, 0:257].bitcast(I32)
        bt_f = rest[:, 257:514]
        diag4 = rest[:, 514:770].rearrange("p (j b) -> p j b", j=4)
        rowinfo = rest[:, 770:1026]
        ix = rest[:, 1026:1090]
        cmpt = rest[:, 1090:1090 + 3072]
        eqt = rest[:, 4162:4354]
        dest = rest[:, 4354:4402]
        kv_i = sb("kv_i", [P, NT + 1], I32)
        kv_f = sb("kv_f", [P, 4, NT + 1])
        win_i = sb("win_i", [BPT * WB, NT], I32)
        new_i = sb("new_i", [BPT * WB, NT], I32)
        tok_i = sb("tok_i", [P, NT], I32)
        seg_i = sb("seg_i", [P, 2], I32)
        cur_i = sb("cur_i", [P, 3 * TPC], I32)
        blkw = sb("blkw", [BPT * WB, NT])

        names = ("late cast x xrows cond w0 w2 small1 big1 down1 ints first small2 small2b l2w raw3 big3 sel3 kvt "
                 "condidx condx wrows wzero wdiag y0 y0s mix had down0 castb "
                 "gu_ready w_ready silu_ready prod_ready hid_ready acc_ready acc_used z_ready zm_ready "
                 "y_ready ycur_ready lg_ready shifted exp_ready parts_ready partsT_ready partsT_used "
                 "chain1 chain3 chain2 prep amask tabst tabld destst destld tokst tokld seggot segst rowps "
                 "rowsb trig angles fold folds foldg xs_ready qkv_ready squared ssq_ready root_ready v_ready "
                 "normed gained rot_ready roped qps_ready qsb_ready scattered ropesteps qklinks "
                 "curidx curidx2 gold0 gold1 gnew0 gnew1 shuf0 shuf1 kt_ps kt_sb qbd_ready s_ps nb_ready p_ready rr_ready pn_ready "
                 "pt_ps pt_sb o_ps o_sb qzero ytok_ps ytok_sb ldiag_ready lrow_ps lex_ready lexe_ready "
                 "pick_ready fx_ps fx_sb pwt_ps pwt_sb h_ps h_sb outl_ps outl_sb fin_ready fint_ps fint_sb s_out "
                 "stdlinks mlinks qkv_end passed").split()
        s = {n: sem(n) for n in names}


        def pe_gate_up(m, w, gate, up, rhs):
            for bank, weights in ((m % 2, gate), (2 + m % 2, up)):
                for k in range(KD):
                    last = nc.tensor.matmul(ps[0:w, bank, :], weights[:, k, m * P:m * P + w], rhs[k],
                                            start=(k == 0), stop=(k == KD - 1))
            last.then_inc(s["gu_ready"], 1)

        def pe_down(pe, m, w, down, step, last_m):
            pe.wait_ge(s["hid_ready"], step + m + 1)
            for d in range(KD):
                last = nc.tensor.matmul(ps[:, 6 + d, :], down[0:w, m, d * P:(d + 1) * P], hid[0:w, m % 2, :],
                                        start=(m == 0), stop=(m == last_m))
            if m == last_m:
                last.then_inc(s["acc_ready"], 1)

        def act_silu(act, m, w, step):
            act.wait_ge(s["gu_ready"], step + m + 1)
            nc.scalar.activation(silu[0:w, m % 2, :], ps[0:w, m % 2, :], ACT.Silu).then_inc(s["silu_ready"], 1)

        def dve_residual(dve, tc, acc0):
            dve.wait_ge(s["acc_ready"], tc + acc0 + 1)
            for d in range(KD):
                cols = xT[:, d, bass.ds(tc * CH, CH)]
                last = nc.vector.tensor_tensor(cols, ps[:, 6 + d, :], cols, ALU.add)
            last.then_inc(s["acc_used"], 1)


        def moe_pe(pe, L, tc, wbase, wa, wb, router, gate, up, down):
            step, n, piece = tc * L.M + L.step0, tc + L.chunk0, tc * L.M + L.piece0
            xc = [xT[:, k, bass.ds(tc * CH, CH)] for k in range(KD)]
            for k in range(KD):
                last = nc.tensor.matmul(ps[0:L.Z, 0, :], wa[:, k, :], xc[k], start=(k == 0), stop=(k == KD - 1))
            last.then_inc(s["z_ready"], 1)
            for d in range(KD):
                for k in range(KD):
                    nc.tensor.matmul(ps[:, 2 + d, :], wbase[:, k, d * P:(d + 1) * P], xc[k],
                                     start=(k == 0), stop=False)
            pe.wait_ge(s["zm_ready"], n + 1)
            for d in range(KD):
                last = nc.tensor.matmul(ps[:, 2 + d, :], wb[0:L.Z, d * P:(d + 1) * P], zm[0:L.Z, :],
                                        start=False, stop=True)
            last.then_inc(s["y_ready"], 1)
            pe.wait_ge(s["ycur_ready"], n + 1)
            for t in range(TPC):
                for k in range(KD):
                    last = nc.tensor.matmul(ps[:, 4, t * L.EW:(t + 1) * L.EW], ycur[:, k, t * P:(t + 1) * P],
                                            router[:, k, :], start=(k == 0), stop=(k == KD - 1))
            last.then_inc(s["lg_ready"], 1)
            rhs = [ycur[:, k, :] for k in range(KD)]

            def spread(m):
                w = L.widths[m]
                nc.tensor.matmul(ps[0:w, 4 + m % 2, :], selb[0:3 * L.EW, m * P:m * P + w], partsT[0:3 * L.EW, :],
                                 start=True, stop=True).then_inc(s["w_ready"], 1)

            for m in range(L.M):
                pe_gate_up(m, L.widths[m], gate, up, rhs)
                if m == 1:
                    pe.wait_ge(s["parts_ready"], n + 1)
                    half = ps[:, 5, :].bitcast(BF16)
                    for t in range(TPC):
                        last = nc.tensor.transpose(half[0:3 * L.EW, t * P:(t + 1) * P],
                                                   parts[:, t * 3 * L.EW:(t + 1) * 3 * L.EW], identb[:, :])
                    last.then_inc(s["partsT_ready"], 1)
                    pe.wait_ge(s["partsT_used"], n + 1)
                    spread(0)
                if m >= 1:
                    spread(m)
                    pe_down(pe, m - 1, L.widths[m - 1], down, step, L.M - 1)
            pe_down(pe, L.M - 1, L.widths[-1], down, step, L.M - 1)
            pe.wait_ge(s["acc_used"], tc + L.acc0 + 1)

        def moe_act(act, L, tc):
            step, n = tc * L.M + L.step0, tc + L.chunk0
            act.wait_ge(s["y_ready"], n + 1)
            for d in range(KD):
                last = nc.scalar.activation(ycur[:, d, :], ps[:, 2 + d, :], ACT.Copy)
            last.then_inc(s["ycur_ready"], 1)
            act.wait_ge(s["shifted"], n + 1)
            last = nc.scalar.activation(rt[1][:, 0:TPC * L.E], rt[0][:, 0:TPC * L.E], ACT.Exp)
            if L.shared:
                last = nc.scalar.activation(rcol[:, 3, :], rcol[:, 4, :], ACT.Exp, scale=-1.0)
            last.then_inc(s["exp_ready"], 1)
            act_silu(act, 0, L.widths[0], step)
            act_silu(act, 1, L.widths[1], step)
            act.wait_ge(s["partsT_ready"], n + 1)
            nc.scalar.activation(partsT[0:3 * L.EW, :], ps[:, 5, :].bitcast(BF16)[0:3 * L.EW, 0:CH],
                                 ACT.Copy).then_inc(s["partsT_used"], 1)
            for m in range(2, L.M):
                act_silu(act, m, L.widths[m], step)

        def moe_dve(dve, L, li, tc, chain_sem):
            step, n, piece = tc * L.M + L.step0, tc + L.chunk0, tc * L.M + L.piece0
            dve.wait_ge(s["z_ready"], n + 1)
            nc.vector.tensor_tensor(
                zm[0:L.Z, :].rearrange("p (b s) -> p b s", s=S),
                ps[0:L.Z, 0, :].rearrange("p (b s) -> p b s", s=S),
                amask[0:L.Z, li, bass.ds(tc * BPC, BPC)].unsqueeze(2).broadcast_to([L.Z, BPC, S]),
                ALU.mult).then_inc(s["zm_ready"], 1)
            E, EW = L.E, L.EW
            flat = TPC * E

            def tiles(x, e=E):
                return x[:, 0:TPC * e].rearrange("p (t e) -> p t e", t=TPC)

            def over(col, e=E):
                return col.broadcast_to([P, TPC, e])

            ch = Chain(dve, chain_sem, tc * L.links)
            lg = tiles(ps[:, 4, :], EW)[:, :, 0:E]
            dve.wait_ge(s["lg_ready"], n + 1)
            nc.vector.sem_inc(s["passed"], 1)
            for t in range(TPC):
                last = nc.vector.max(top8[:, t, :], lg[:, t, :])
            ch.link(last)
            if L.shared:
                nc.vector.tensor_copy(rcol[:, 4, :], tiles(ps[:, 4, :], EW)[:, :, E])
            nc.vector.tensor_tensor(tiles(rt[0]), lg, over(top8[:, :, 0:1]), ALU.subtract)\
                .then_inc(s["shifted"], 1)
            ch.link(nc.vector.tensor_tensor(tiles(rt[2]), lg, over(top8[:, :, L.K - 1:L.K]), ALU.is_gt))
            ch.link(nc.vector.tensor_tensor(tiles(rt[3]), lg, over(top8[:, :, L.K - 1:L.K]), ALU.is_equal))
            ch.link(nc.vector.tensor_reduce(rcol[:, 0, :], tiles(rt[2]), X, ALU.add))
            ch.link(nc.vector.tensor_tensor_scan(rt[4][:, 0:flat], C["restart%d" % E][:, 0:flat], rt[3][:, 0:flat],
                                                 0.0, ALU.mult, ALU.add))
            ch.link(nc.vector.tensor_tensor(tiles(rt[5]), tiles(rt[4]), over(rcol[:, 0, :].unsqueeze(2)), ALU.add))
            ch.link(nc.vector.scalar_tensor_tensor(rt[4][:, 0:flat], rt[5][:, 0:flat], float(L.K), rt[3][:, 0:flat],
                                                   ALU.is_le, ALU.mult))
            ch.link(nc.vector.tensor_tensor(rt[3][:, 0:flat], rt[2][:, 0:flat], rt[4][:, 0:flat], ALU.add))
            dve.wait_ge(s["exp_ready"], n + 1)
            ch.link(nc.vector.tensor_tensor(rt[2][:, 0:flat], rt[1][:, 0:flat], rt[3][:, 0:flat], ALU.mult))
            ch.link(nc.vector.tensor_reduce(rcol[:, 1, :], tiles(rt[2]), X, ALU.add))
            ch.link(nc.vector.reciprocal(rcol[:, 2, :], rcol[:, 1, :]))
            weights = tiles(rt[5], EW)
            ch.link(nc.vector.tensor_tensor(weights[:, :, 0:E], tiles(rt[2]), over(rcol[:, 2, :].unsqueeze(2)),
                                            ALU.mult))
            if L.shared:
                ch.link(nc.vector.tensor_scalar(rcol[:, 0, :], rcol[:, 3, :], 1.0, None, ALU.add))
                ch.link(nc.vector.reciprocal(weights[:, :, E:EW], rcol[:, 0, :].unsqueeze(2)))
            part = [parts[:, 0:TPC * 3 * EW].rearrange("p (t j e) -> p t j e", t=TPC, j=3)[:, :, j, :]
                    for j in range(3)]
            ch.link(nc.vector.tensor_copy(part[0], weights))
            ch.link(nc.vector.tensor_tensor(tiles(rt[0], EW), weights, part[0], ALU.subtract))
            ch.link(nc.vector.tensor_copy(part[1], tiles(rt[0], EW)))
            ch.link(nc.vector.tensor_tensor(tiles(rt[2], EW), tiles(rt[0], EW), part[1], ALU.subtract))
            nc.vector.tensor_copy(part[2], tiles(rt[2], EW)).then_inc(s["parts_ready"], 1)
            assert ch.n == L.links, ch.n

            for m, w in enumerate(L.widths):
                dve.wait_ge(s["silu_ready"], step + m + 1)
                nc.vector.tensor_tensor(silu[0:w, m % 2, :], silu[0:w, m % 2, :], ps[0:w, 2 + m % 2, :],
                                        ALU.mult).then_inc(s["prod_ready"], 1)
                dve.wait_ge(s["prod_ready"], piece + m + 1)
                dve.wait_ge(s["w_ready"], piece + m + 1)
                nc.vector.tensor_tensor(hid[0:w, m % 2, :], silu[0:w, m % 2, :], ps[0:w, 4 + m % 2, :], ALU.mult)\
                    .then_inc(s["hid_ready"], 1)

        rows16 = newblk.rearrange("s (o n) -> (s o) n", n=2 * KW)
        SC = 1.0 / 16.0
        block = ctx.enter_context(nc.Block())

        @block.sync
        def _(sp):
            sp.dma_start(cond_i[:, :], a["cond"]).then_inc(s["cond"], 16)
            sp.dma_start(late[:, :], a["late"]).then_inc(s["late"], 16)
            sp.dma_start(kv_i[:, :], a["kv"]).then_inc(s["ints"], 16)
            sp.dma_start(bt_i[0:B, :], a["tables"]).then_inc(s["ints"], 16)
            sp.dma_start(mid[:, 3072:3072 + first_n], a["first"]).then_inc(s["first"], 16)
            sp.dma_start(l0_down, a["w2"]).then_inc(s["w2"], 16)
            sp.dma_start(xrows, a["xrows"]).then_inc(s["xrows"], 16)
            sp.dma_start(early[:, 0:4096], a["w13"]).then_inc(s["w0"], 16)
            sp.dma_start(xT[:, :, :], a["xT"]).then_inc(s["x"], 16)
            for dst, name in ((small1, "small1"), (b1s, "b1"), (small3, "small3"), (adapt_i, "adapt"),
                              (adapt_s, "adapt_s")):
                sp.dma_start(dst if dst is adapt_i else dst[:], a[name]).then_inc(s["small1"], 16)
            for dst, name in ((gain, "gain"), (wr, "wr"), (b21, "b21"), (b22, "b22"), (br, "br")):
                sp.dma_start(dst[:], a[name]).then_inc(s["small2"], 16)
            sp.wait_ge(s["tabst"], 1)
            sp.dma_start(tab_d, ix[0:B, 16:16 + WB]).then_inc(s["tabld"], 16)
            sp.wait_ge(s["tabld"], 16)
            with nc.allow_non_contiguous_dma(reason="704 words"):
                sp.dma_start(blkw[:, :], tab_d.rearrange("(g b) i -> (b i) g", b=BPT)).then_inc(s["tabld"], 16)
            sp.wait_ge(s["destst"], 1)
            for j in range(NEWB):
                src = dest[(j % 2) * B:(j % 2 + 1) * B, (j // 2) * BLOCK:(j // 2 + 1) * BLOCK]
                sp.dma_start(dest_d[:, j * BLOCK:(j + 1) * BLOCK], src).then_inc(s["destld"], 16)
            sp.wait_ge(s["destld"], 16 * NEWB)
            sp.dma_start(rest[0:B, 4402:4450], dest_d).then_inc(s["destld"], 16)
            sp.wait_ge(s["tokst"], 1)
            sp.dma_start(tok_d, rest[0:B, 4450:4482].bitcast(I32)).then_inc(s["tokld"], 16)
            sp.wait_ge(s["tokld"], 16)
            with nc.allow_non_contiguous_dma(reason="2048 words"):
                sp.dma_start(tok_i[:, :], tok_d.rearrange("(i b) t -> (b t) i", b=BPT)).then_inc(s["tokld"], 16)
            sp.wait_ge(s["seggot"], 32)
            sp.dma_start(newblk[0:P, :], stage[:, 0, :]).then_inc(s["segst"], 16)
            sp.dma_start(newblk[P:SEGS, :], stage[0:B, 1, :]).then_inc(s["segst"], 16)
            sp.wait_ge(s["had"], 1)
            sp.dma_start(l1_down, a["down1"]).then_inc(s["down1"], 16)
            sp.wait_ge(s["segst"], 32)
            sp.wait_ge(s["prep"], 1)
            sp.dma_start(l1_gate, a["gate1"]).then_inc(s["big1"], 16)
            sp.dma_start(l1_up, a["up1"]).then_inc(s["big1"], 16)
            sp.dma_start(mid[:, 0:5632], a["l2w"]).then_inc(s["l2w"], 16)
            sp.wait_ge(s["acc_used"], 2 * NCH)
            sp.dma_start(big[:, 0:2 * KD * N3], a["gu3"]).then_inc(s["big3"], 16)
            sp.dma_start(l3_down, a["down3"]).then_inc(s["big3"], 16)
            with sp.Fori(0, NCH) as tc:
                for t in range(TPC):
                    slot = t % 2
                    sp.wait_ge(s["gnew0" if slot == 0 else "gnew1"], (tc * 2 + t // 2 + 1) * 16)
                    nc.sync.sem_inc(s["passed"], 1)
                    sp.wait_ge(s["o_ps"], tc * BPC + (O_CREDIT + BPT * (t - 1)))
                    for q in range(BPT):
                        for h, (i0, i1) in enumerate(((0, 6), (6, WB))):
                            sp.dma_start(kv2[0:(i1 - i0) * BLOCK, slot, h, q, :],
                                         kvw[slot * 64 + q * WB + i0:slot * 64 + q * WB + i1, :, :])\
                                .then_inc(s["shuf0" if slot == 0 else "shuf1"], 16)
            sp.wait_ge(s["acc_used"], 3 * NCH)
            sp.dma_start(raw3, a["raw3"]).then_inc(s["raw3"], 16)
            with sp.Fori(0, NCH) as tc:
                sp.wait_ge(s["acc_used"], tc + 3 * NCH + 1)
                sp.dma_start(a["out"][:, :, bass.ds(tc * CH, CH)], xT[:, :, bass.ds(tc * CH, CH)])\
                    .then_inc(s["s_out"], 16)
            sp.wait_ge(s["s_out"], 16 * NCH)

        @block.gpsimd
        def _(pool):
            def gather(out, src, idx, signal, **kw):
                nc.gpsimd.indirect_dma_start(
                    out=out, out_offset=None, in_=src, in_offset=bass.IndirectOffsetOnAxis(ap=idx, axis=0), **kw
                ).then_inc(signal, 16)

            nc.gpsimd.memset(work[:, 0:2048], 0.0).then_inc(s["wzero"], 1)
            pool.wait_ge(s["condx"], 1)
            for i in range(NT):
                gather(wrows[:, i, :], a["cond_w"], cond_x[:, i:i + 1], s["wrows"])
            o1, o2 = cast_at["identb"][0], cast_at["sel1"][0]
            pool.dma_start(identb[:, :], a["cast"][:, o1:o1 + P]).then_inc(s["castb"], 16)
            pool.dma_start(tselb[:, :, :], a["cast"][:, o1 + P:o2].rearrange("p (q n) -> p q n", q=BPT))\
                .then_inc(s["castb"], 16)
            pool.dma_start(selb[:, :], a["cast"][:, o2:o2 + L1.M * P]).then_inc(s["castb"], 16)
            pool.wait_ge(s["condidx"], 1)
            gather(stage[:, 0, :], a["cache"], seg_i[:, 0:1], s["seggot"])
            gather(stage[0:B, 1, :], a["cache"], seg_i[0:B, 1:2], s["seggot"])

            pool.wait_ge(s["segst"], 32)
            pool.wait_ge(s["tokld"], 32)
            with pool.Fori(0, NCH) as tc:
                nc.gpsimd.tensor_copy(cur_i[:, 0:TPC], tok_i[:, bass.ds(tc * TPC, TPC)]).then_inc(s["curidx"], 1)
                pool.wait_ge(s["curidx"], tc + 1)
                pool.wait_ge(s["roped"], tc + 1)
                pool.wait_ge(s["v_ready"], tc + 1)
                nc.gpsimd.sem_inc(s["passed"], 1)
                for t in range(TPC):
                    nc.gpsimd.indirect_dma_start(
                        out=rows16, out_offset=bass.IndirectOffsetOnAxis(ap=cur_i[:, t:t + 1], axis=0),
                        in_=kvrow[:, t, :], in_offset=None, bounds_check=SEGS * BLOCK - 1, oob_is_err=False,
                    ).then_inc(s["scattered"], 16)
                pool.wait_ge(s["scattered"], (tc + 1) * (16 * TPC))
                nc.gpsimd.sem_inc(s["passed"], 1)

            pool.wait_ge(s["scattered"], 16 * NT)
            pool.wait_ge(s["qkv_end"], 1)
            nc.gpsimd.memset(Qbd, 0.0).then_inc(s["qzero"], 1)
            pool.wait_ge(s["qzero"], 1)
            o3 = cast_at["sel3"][0]
            pool.dma_start(selb[:, 0:L3.M * P], a["cast"][:, o3:o3 + L3.M * P]).then_inc(s["sel3"], 16)

            def old_blocks(t):
                slot = t % 2
                gather(early[slot * 64:slot * 64 + BPT * WB, 0:ROW], a["cache"], cur_i[0:BPT * WB, 4 + t:5 + t],
                       s["gold0" if slot == 0 else "gold1"])

            def new_blocks(tc, t):
                slot = t % 2
                pool.wait_ge(s["gold0" if slot == 0 else "gold1"], (tc * 2 + t // 2 + 1) * 16)
                nc.gpsimd.sem_inc(s["passed"], 1)
                gather(early[slot * 64:slot * 64 + BPT * WB, 0:ROW], newblk, cur_i[0:BPT * WB, 8 + t:9 + t],
                       s["gnew0" if slot == 0 else "gnew1"], bounds_check=SEGS - 1, oob_is_err=False)

            with pool.Fori(0, NCH) as tc:
                nc.gpsimd.tensor_copy(cur_i[0:BPT * WB, 4:8], win_i[:, bass.ds(tc * TPC, TPC)])
                nc.gpsimd.tensor_copy(cur_i[0:BPT * WB, 8:12], new_i[:, bass.ds(tc * TPC, TPC)])\
                    .then_inc(s["curidx2"], 1)
                pool.wait_ge(s["curidx2"], tc + 1)
                nc.gpsimd.sem_inc(s["passed"], 1)
                for t in range(TPC):
                    if t >= 2:
                        pool.wait_ge(s["shuf0" if t % 2 == 0 else "shuf1"], (tc * 2 + t // 2) * (16 * 2 * BPT))
                        nc.gpsimd.sem_inc(s["passed"], 1)
                    old_blocks(t)
                    if t >= 1:
                        new_blocks(tc, t - 1)
                new_blocks(tc, TPC - 1)
                pool.wait_ge(s["shuf0"], (tc * 2 + 2) * (16 * 2 * BPT))
                pool.wait_ge(s["shuf1"], (tc * 2 + 2) * (16 * 2 * BPT))
                nc.gpsimd.sem_inc(s["passed"], 1)

        @block.scalar
        def _(act):
            act.wait_ge(s["folds"], 1)
            nc.scalar.activation(sinb[:], sinb[:], ACT.Sin)
            nc.scalar.activation(cosb[:], cosb[:], ACT.Sin).then_inc(s["trig"], 1)
            for g in range(0, 8, 2):
                act.wait_ge(s["y0"], g + 1)
                nc.scalar.activation(yT[:, g % 2, (g // 2) * CH:(g // 2 + 1) * CH], ps[:, g, :], ACT.Copy)\
                    .then_inc(s["y0s"], 1)
            act.wait_ge(s["had"], 1)
            nc.scalar.activation(l0_down, ps[:, 0:4, :], ACT.Copy).then_inc(s["down0"], 1)
            with act.Fori(0, NCH) as tc:
                for m in range(M0):
                    act_silu(act, m, P, tc * M0)
            with act.Fori(0, NCH) as tc:
                moe_act(act, L1, tc)

            with act.Fori(0, NCH) as tc:
                act.wait_ge(s["acc_used"], 2 * NCH)
                nc.scalar.activation(ycur[:, :, :], xT[:, :, bass.ds(tc * CH, CH)], ACT.Copy)\
                    .then_inc(s["xs_ready"], 1)
                act.wait_ge(s["qkv_ready"], tc + 1)
                nc.scalar.activation(sqr.rearrange("p (t n) -> p t n", t=TPC), ps[:, 0:4, 0:384], ACT.Square)\
                    .then_inc(s["squared"], 1)
                nc.scalar.activation(kvrow[:, :, KW:2 * KW], ps[:, 0:4, 384:512], ACT.Copy).then_inc(s["v_ready"], 1)
                act.wait_ge(s["ssq_ready"], tc + 1)
                nc.scalar.activation(kcol[:, 0, :], kcol[:, 1, :], ACT.Sqrt).then_inc(s["root_ready"], 1)
                act.wait_ge(s["qps_ready"], tc + 1)
                nc.scalar.activation(qT[:, :, bass.ds(tc * CH, CH)], ps[:, 4:6, :], ACT.Copy)\
                    .then_inc(s["qsb_ready"], 1)
                act.wait_ge(s["scattered"], (tc + 1) * (16 * TPC))
            act.wait_ge(s["qsb_ready"], NCH)
            nc.scalar.activation(rcol[:, 3, :], rcol[:, 1, :], ACT.Copy).then_inc(s["qkv_end"], 1)

            def keys_out(tc, n):
                act.wait_ge(s["kt_ps"], tc * BPC + (n + 1))
                nc.scalar.activation(KTs[:, n % 2, :], ps[:, n % 2, 0:WK], ACT.Copy).then_inc(s["kt_sb"], 1)

            def exponentials(tc, n):
                act.wait_ge(s["nb_ready"], tc * BPC + (n + 1))
                for h in range(2):
                    last = nc.scalar.activation(Pex[:, n % 2, h, :], ps[:, 2 + n % 2, h * WK:(h + 1) * WK], ACT.Exp,
                                                bias=acol[:, 1, n % 2, h:h + 1], scale=SC,
                                                accum_out=acol[:, 2, n % 2, h:h + 1])
                last.then_inc(s["p_ready"], 1)

            def probs_out(tc, n):
                act.wait_ge(s["pt_ps"], tc * BPC + (n + 1))
                nc.scalar.activation(PTs[0:96, n % 2, 0, :], ps[0:96, 4 + n % 2, 0:256], ACT.Copy)
                nc.scalar.activation(PTs[0:80, n % 2, 1, :], ps[0:80, 4 + n % 2, 256:512], ACT.Copy)\
                    .then_inc(s["pt_sb"], 1)

            with act.Fori(0, NCH) as tc:
                for n in range(BPC + 2):
                    if n < BPC:
                        keys_out(tc, n)
                    if 1 <= n <= BPC:
                        exponentials(tc, n - 1)
                    if n >= 2:
                        probs_out(tc, n - 2)
                act.wait_ge(s["ytok_ps"], tc + 1)
                nc.scalar.activation(ytok.rearrange("p (a b) n -> p a (b n)", a=2), ps[:, 0:2, :], ACT.Copy)\
                    .then_inc(s["ytok_sb"], 1)
                act.wait_ge(s["lex_ready"], tc + 1)
                nc.scalar.activation(lexe, lex, ACT.Exp).then_inc(s["lexe_ready"], 1)
                act.wait_ge(s["fx_ps"], tc + 1)
                nc.scalar.activation(fx, ps[:, 3, 0:128].rearrange("p (d n) -> p d n", d=KD), ACT.Copy)\
                    .then_inc(s["fx_sb"], 1)
                act.wait_ge(s["pwt_ps"], tc + 1)
                nc.scalar.activation(pwT[0:64, :], ps[0:64, 4, :], ACT.Copy).then_inc(s["pwt_sb"], 1)
                act.wait_ge(s["h_ps"], tc + 1)
                for m in range(H2 // P):
                    last = nc.scalar.activation(hT2[:, m, :], ps[:, 5, m * 64:(m + 1) * 64], ACT.Gelu,
                                                bias=b21[:, m:m + 1])
                last.then_inc(s["h_sb"], 1)
                act.wait_ge(s["outl_ps"], tc + 1)
                nc.scalar.activation(outl[0:64, :], ps[0:64, 0, 0:256], ACT.Copy).then_inc(s["outl_sb"], 1)

            act.wait_ge(s["fin_ready"], 1)
            nc.scalar.activation(awt[:, :, :], ps[:, 0, 0:128].rearrange("p (k n) -> p k n", k=KD), ACT.Copy)
            nc.scalar.activation(wpb[:, :], ps[0:64, 1, 0:256], ACT.Copy).then_inc(s["fint_sb"], 1)
            with act.Fori(0, NCH) as tc:
                moe_act(act, L3, tc)

        @block.vector
        def _(dve):
            ch = Chain(dve, s["chain1"])
            dve.wait_ge(s["cond"], 16)
            ch.link(nc.vector.tensor_copy(cond_f[:, :], cond_i[:, :]))
            dve.wait_ge(s["late"], 16)
            nc.vector.tensor_scalar(cond_x[:, :], cond_f[:, :], float(S), C["rowt"], ALU.mult, ALU.add)\
                .then_inc(s["condx"], 1)

            dve.wait_ge(s["ints"], 32)
            dve.wait_ge(s["first"], 16)
            kv, off0, hi, slot0 = (kv_f[:, j, :] for j in range(4))
            ch.link(nc.vector.tensor_copy(kv, kv_i[:, :]))
            ch.link(nc.vector.tensor_scalar(off0, kv, 1.0 / BLOCK, -0.5 + 0.5 / BLOCK, ALU.mult, ALU.add))
            ch.link(nc.vector.tensor_scalar(hi, off0, MAGIC, None, ALU.add))
            ch.link(nc.vector.tensor_scalar(slot0, hi, MAGIC, None, ALU.subtract))
            ch.link(nc.vector.scalar_tensor_tensor(off0, slot0, -float(BLOCK), kv, ALU.mult, ALU.add))
            ang, turns, fold, wrap = (ycur[:, j // 2, (j % 2) * 256:(j % 2 + 1) * 256] for j in range(4))
            pos = kv_f[:, 2, 0:NT]
            ch.link(nc.vector.tensor_scalar(pos, kv[:, 0:NT], C["rowt"], None, ALU.add))
            ch.link(nc.vector.tensor_tensor(ang.rearrange("p (i f) -> p i f", i=NT),
                                            pos.unsqueeze(2).broadcast_to([P, NT, HD // 2]),
                                            F["inv"].unsqueeze(1).broadcast_to([P, NT, HD // 2]), ALU.mult))
            ch.link(nc.vector.tensor_scalar(turns, ang, float(1 / (2 * np.pi)), None, ALU.mult))
            ch.link(nc.vector.tensor_scalar(turns, turns, MAGIC, None, ALU.add))
            ch.link(nc.vector.tensor_scalar(turns, turns, MAGIC, None, ALU.subtract))
            ch.link(nc.vector.scalar_tensor_tensor(fold, turns, -TWO_PI_HI, ang, ALU.mult, ALU.add))
            ch.link(nc.vector.scalar_tensor_tensor(ang, turns, -TWO_PI_LO, fold, ALU.mult, ALU.add))
            edge = 3.1415925
            sin_f = sinb[:].rearrange("p i f -> p (i f)")
            cos_f = cosb[:].rearrange("p i f -> p (i f)")
            ch.link(nc.vector.tensor_scalar(sin_f, ang, edge, -edge, ALU.min, ALU.max))
            ch.link(nc.vector.tensor_scalar(wrap, ang, float(np.pi / 2), -float(2 * np.pi), ALU.is_gt, ALU.mult))
            ch.link(nc.vector.scalar_tensor_tensor(fold, ang, float(np.pi / 2), wrap, ALU.add, ALU.add))
            nc.vector.tensor_scalar(cos_f, fold, edge, -edge, ALU.min, ALU.max).then_inc(s["folds"], 1)

            slots, tab = ix[0:B, 0:WB], ix[0:B, 16:16 + WB]
            ch.link(nc.vector.tensor_copy(bt_f[0:B, :], bt_i[0:B, :]))
            ch.link(nc.vector.tensor_scalar(slots, F["win"][0:B, :], slot0[0:B, NT:NT + 1], 0.0, ALU.add, ALU.max))
            ch.link(nc.vector.tensor_scalar(slots, slots, float(NBLK - 1), None, ALU.min))
            for i in range(WB):
                ch.link(nc.vector.scalar_tensor_tensor(cmpt[0:B, i * NBLK:(i + 1) * NBLK], F["slots"][0:B, :],
                                                       slots[:, i:i + 1], bt_f[0:B, :], ALU.is_equal, ALU.mult,
                                                       accum_out=tab[:, i:i + 1]))
            i0 = WINDOW // BLOCK
            segf = ix[:, 32:34]
            nc.vector.tensor_copy(segf[0:B, 0:1], tab[:, i0:i0 + 1]).then_inc(s["tabst"], 1)
            nc.vector.tensor_copy(segf[B:P, 0:1], tab[:, i0 + 1:i0 + 2])
            ch.link(nc.vector.tensor_copy(segf[0:B, 1:2], tab[:, i0 + 2:i0 + 3]))
            nc.vector.tensor_copy(seg_i[:, 0:1], segf[:, 0:1])
            nc.vector.tensor_copy(seg_i[0:B, 1:2], segf[0:B, 1:2]).then_inc(s["condidx"], 1)
            idB = ident[0:B, 0:B]
            ch.link(nc.vector.tensor_tensor(diag4[0:B, 0:NEWB, :], idB.unsqueeze(1).broadcast_to([B, NEWB, B]),
                                            tab[:, i0:i0 + NEWB].unsqueeze(2).broadcast_to([B, NEWB, B]), ALU.mult))
            nc.vector.tensor_scalar(diag4[0:B, NEWB, :], idB, off0[0:B, NT:NT + 1], None, ALU.mult)\
                .then_inc(s["rowps"], 1)
            dve.wait_ge(s["rowsb"], 1)
            ch.link(nc.vector.tensor_copy(rowinfo, ps[:, 7, 0:256]))
            segblk, offrow = rowinfo[:, 0:SEGS], rowinfo[:, SEGS:SEGS + B]
            v = seen.rearrange("p (o j b) -> p o j b", o=BLOCK, j=NEWB)
            prio = F["prio"].rearrange("p (j b) -> p j b", j=NEWB)

            def over_o(x):
                return x.unsqueeze(1).broadcast_to([P, BLOCK, B])

            offs = F["off"].unsqueeze(2).broadcast_to([P, BLOCK, B])
            ch.link(nc.vector.tensor_copy(v[:, :, 1, :], over_o(prio[:, 1, :])))
            ch.link(nc.vector.tensor_tensor(v[:, :, 0, :], over_o(offrow), offs, ALU.is_le))
            ch.link(nc.vector.tensor_tensor(v[:, :, 2, :], over_o(offrow), offs, ALU.is_gt))
            ch.link(nc.vector.tensor_tensor(v[:, :, 0, :], v[:, :, 0, :], over_o(prio[:, 0, :]), ALU.mult))
            ch.link(nc.vector.tensor_tensor(v[:, :, 2, :], v[:, :, 2, :], over_o(prio[:, 2, :]), ALU.mult))
            win, last_seg, col = ix[:, 40:56], ix[:, 56:57], ix[:, 57:58]
            for st, rows in enumerate((P, B)):
                ch.link(nc.vector.tensor_scalar(eqt[0:rows, :], segblk[0:rows, :], segf[0:rows, st:st + 1], None,
                                                ALU.is_equal))
                ch.link(nc.vector.tensor_tensor(cmpt[0:rows, :].rearrange("p (o n) -> p o n", o=BLOCK),
                                                seen[0:rows, :].rearrange("p (o n) -> p o n", o=BLOCK),
                                                eqt[0:rows, :].unsqueeze(1).broadcast_to([rows, BLOCK, SEGS]),
                                                ALU.mult))
                ch.link(nc.vector.tensor_reduce(win[0:rows, :], cmpt[0:rows, :].rearrange("p (o n) -> p o n", o=BLOCK),
                                                X, ALU.max))
                ch.link(nc.vector.tensor_tensor(cmpt[0:rows, 0:SEGS], eqt[0:rows, :], F["segid"][0:rows, :], ALU.mult))
                ch.link(nc.vector.tensor_reduce(last_seg[0:rows, :], cmpt[0:rows, 0:SEGS], X, ALU.max))
                ch.link(nc.vector.tensor_scalar(col[0:rows, :], last_seg[0:rows, :], float(BLOCK), -BLOCK - FAR,
                                                ALU.mult, ALU.add))
                ch.link(nc.vector.tensor_scalar(eqt[0:rows, 0:BLOCK], F["off"][0:rows, :], col[0:rows, :], None,
                                                ALU.add))
                ch.link(nc.vector.scalar_tensor_tensor(cmpt[0:rows, 0:BLOCK], win[0:rows, :],
                                                       F["myprio"][0:rows, st:st + 1], eqt[0:rows, 0:BLOCK],
                                                       ALU.is_equal, ALU.mult))
                ch.link(nc.vector.tensor_scalar(dest[0:rows, st * BLOCK:(st + 1) * BLOCK], cmpt[0:rows, 0:BLOCK], FAR,
                                                None, ALU.add))
            nc.vector.tensor_copy(ix[:, 58:59], ix[:, 56:57]).then_inc(s["destst"], 1)
            dve.wait_ge(s["tabld"], 32)
            WR = BPT * WB
            nc.vector.tensor_copy(win_i[:, :], blkw[:, :])
            wide = cmpt[0:WR, :].rearrange("p (g n) -> p g n", g=NT)
            ch.link(nc.vector.tensor_tensor(wide, segblk[0:WR, :].unsqueeze(1).broadcast_to([WR, NT, SEGS]),
                                            blkw[:, :].unsqueeze(2).broadcast_to([WR, NT, SEGS]), ALU.is_equal))
            ch.link(nc.vector.tensor_tensor(wide, wide, F["segid"][0:WR, :].unsqueeze(1).broadcast_to([WR, NT, SEGS]),
                                            ALU.mult))
            ch.link(nc.vector.tensor_reduce(ix[0:WR, 0:NT], wide, X, ALU.max))
            ch.link(nc.vector.tensor_scalar(ix[0:WR, 16:32], ix[0:WR, 0:NT], 0.0, FAR, ALU.is_equal, ALU.mult))
            ch.link(nc.vector.scalar_tensor_tensor(new_i[:, :], ix[0:WR, 0:NT], -1.0, ix[0:WR, 16:32], ALU.add,
                                                   ALU.add))
            dve.wait_ge(s["destld"], 16 * (NEWB + 1))
            toks = cmpt[0:B, 0:S * NEWB * BLOCK].rearrange("p (t u) -> p t u", t=S)
            ch.link(nc.vector.scalar_tensor_tensor(
                toks, F["shift"][0:B, :].rearrange("p (t u) -> p t u", t=S), off0[0:B, NT:NT + 1],
                rest[0:B, 4402:4450].unsqueeze(1).broadcast_to([B, S, NEWB * BLOCK]), ALU.is_equal, ALU.mult))
            ch.link(nc.vector.tensor_reduce(eqt[0:B, 0:S], toks, X, ALU.add))
            nc.vector.tensor_copy(rest[0:B, 4450:4482].bitcast(I32), eqt[0:B, 0:S]).then_inc(s["tokst"], 1)
            hi, least = kv_f[:, 2, :], kv_f[:, 3, :]
            ch.link(nc.vector.tensor_scalar(hi, off0, float(WINDOW), None, ALU.add))
            ch.link(nc.vector.tensor_tensor(least, hi, kv, ALU.subtract))

            def per_tile(x):
                return x[:, 0:NT].unsqueeze(2).broadcast_to([P, NT, WK])

            def per_key(x):
                return x.unsqueeze(1).broadcast_to([P, NT, WK])

            ma = cmpt[:, 0:NT * WK].rearrange("p (i c) -> p i c", i=NT)
            mb = seen[:, 0:NT * WK].rearrange("p (i c) -> p i c", i=NT)
            ch.link(nc.vector.tensor_tensor(ma, per_key(F["keyless"]), per_tile(off0), ALU.is_gt))
            ch.link(nc.vector.tensor_tensor(mb, per_key(F["keyless"]), per_tile(hi), ALU.is_le))
            ch.link(nc.vector.tensor_tensor(ma, ma, mb, ALU.mult))
            ch.link(nc.vector.tensor_tensor(mb, per_key(F["key"]), per_tile(least), ALU.is_ge))
            ch.link(nc.vector.tensor_tensor(ma, ma, mb, ALU.mult))
            dve.wait_ge(s["tokld"], 32)
            nc.vector.tensor_scalar(maskb[:, :], cmpt[:, 0:NT * WK], -MASKED, MASKED, ALU.mult, ALU.add)\
                .then_inc(s["prep"], 1)

            dve.wait_ge(s["w2"], 16)
            for step, (src, dst) in enumerate(((l0_down, w2mix), (w2mix, l0_down), (l0_down, w2mix))):
                r = 4 >> step
                si, di = (z.rearrange("p (a h r) n -> p a h (r n)", h=2, r=r) for z in (src, dst))
                nc.vector.tensor_tensor(di[:, :, 0, :], si[:, :, 0, :], si[:, :, 1, :], ALU.add)
                last = nc.vector.tensor_tensor(di[:, :, 1, :], si[:, :, 0, :], si[:, :, 1, :], ALU.subtract)
                if step < 2:
                    ch.link(last)
            last.then_inc(s["mix"], 1)
            dve.wait_ge(s["wrows"], 16 * NT)
            dve.wait_ge(s["wzero"], 1)
            for q in range(BPT):
                r = slice(q * S, (q + 1) * S)
                last = nc.vector.tensor_copy(wdiag[r, :, r], wrows[r, :, :])
            last.then_inc(s["wdiag"], 1)
            for g in range(1, 8, 2):
                dve.wait_ge(s["y0"], g + 1)
                nc.vector.tensor_copy(yT[:, g % 2, (g // 2) * CH:(g // 2 + 1) * CH], ps[:, g, :])\
                    .then_inc(s["y0s"], 1)
            dve.wait_ge(s["small1"], 80)
            ch.link(nc.vector.tensor_copy(adapt_f, adapt_i))
            for li in range(2):
                ch.link(nc.vector.tensor_scalar(amask[:, li, :], adapt_f[:, li, :], adapt_s[:, 2 * li + 1:2 * li + 2],
                                                adapt_s[:, 2 * li:2 * li + 1], ALU.is_equal, ALU.mult))

            dve.wait_ge(s["x"], 16)
            with dve.Fori(0, NCH) as tc:
                for m in range(M0):
                    dve.wait_ge(s["silu_ready"], tc * M0 + (m + 1))
                    nc.vector.tensor_tensor(hid[:, m % 2, :], silu[:, m % 2, :], ps[:, 2 + m % 2, :], ALU.mult)\
                        .then_inc(s["hid_ready"], 1)
                dve_residual(dve, tc, 0)
            with dve.Fori(0, NCH) as tc:
                moe_dve(dve, L1, 0, tc, s["stdlinks"])
                dve_residual(dve, tc, L1.acc0)

            dve.wait_ge(s["trig"], 1)
            dve.wait_ge(s["small2"], 80)
            nc.vector.tensor_scalar(gain[:, :], gain[:, :], 1.0, None, ALU.add).then_inc(s["gained"], 1)
            dve.wait_ge(s["gained"], 1)
            NH = G * GS + G

            with dve.Fori(0, NCH) as tc:
                ch = Chain(dve, s["qklinks"], tc * 7)
                dve.wait_ge(s["squared"], tc + 1)
                ch.link(nc.vector.tensor_reduce(kcol[:, 0, :], sqr.rearrange("p (h d) -> p h d", d=HD), X, ALU.add))
                nc.vector.tensor_scalar(kcol[:, 1, :], kcol[:, 0, :], 1.0 / HD, EPS, ALU.mult, ALU.add)\
                    .then_inc(s["ssq_ready"], 1)
                dve.wait_ge(s["root_ready"], tc + 1)
                ch.link(nc.vector.reciprocal(kcol[:, 1, :], kcol[:, 0, :]))
                qk4 = qkn.rearrange("p (t h d) -> p t h d", t=TPC, d=HD)
                for t in range(TPC):
                    last = nc.vector.tensor_tensor(
                        qk4[:, t, :, :], ps[:, t, 0:384].rearrange("p (h d) -> p h d", d=HD),
                        kcol[:, 1, t * NH:(t + 1) * NH].unsqueeze(2).broadcast_to([P, NH, HD]), ALU.mult)
                ch.link(last)
                qk3 = qkn.rearrange("p (t n) -> p t n", t=TPC)
                ch.link(nc.vector.tensor_tensor(qk3, qk3, gain[:, :].unsqueeze(1).broadcast_to([P, TPC, NH * HD]),
                                                ALU.mult))

                def trig(table):
                    return table[:, bass.ds(tc * TPC, TPC), :].unsqueeze(2).broadcast_to([P, TPC, NH, HD // 2])

                def temp(x):
                    return x.rearrange("p (t h d) -> p t h d", t=TPC, d=HD // 2)

                low, high = qk4[:, :, :, 0:HD // 2], qk4[:, :, :, HD // 2:HD]
                tmp = [temp(sqr[:, 0:768]), temp(sqr[:, 768:1536]), temp(work[:, 0:768]), temp(work[:, 1024:1792])]
                nc.vector.tensor_tensor(tmp[0], low, trig(cosb), ALU.mult)
                nc.vector.tensor_tensor(tmp[1], high, trig(sinb), ALU.mult)
                nc.vector.tensor_tensor(tmp[2], high, trig(cosb), ALU.mult)
                ch.link(nc.vector.tensor_tensor(tmp[3], low, trig(sinb), ALU.mult))
                k4 = kvrow[:, :, 0:KW].rearrange("p t (g d) -> p t g d", g=G)
                nq = G * GS
                nc.vector.tensor_tensor(low[:, :, 0:nq, :], tmp[0][:, :, 0:nq, :], tmp[1][:, :, 0:nq, :], ALU.subtract)
                nc.vector.tensor_tensor(high[:, :, 0:nq, :], tmp[2][:, :, 0:nq, :], tmp[3][:, :, 0:nq, :], ALU.add)
                ch.link(nc.vector.tensor_tensor(k4[:, :, :, 0:HD // 2], tmp[0][:, :, nq:, :], tmp[1][:, :, nq:, :],
                                                ALU.subtract))
                ch.link(nc.vector.tensor_tensor(k4[:, :, :, HD // 2:], tmp[2][:, :, nq:, :], tmp[3][:, :, nq:, :],
                                                ALU.add))
                nc.vector.tensor_copy(kcol[:, 0, 0:1], kcol[:, 1, 0:1]).then_inc(s["roped"], 1)
                assert ch.n == 7

            def block_diagonals(tc, n):
                if n >= 4:
                    dve.wait_ge(s["s_ps"], tc * BPC + (n - 2))
                q = Qbd[:, (n // 2) % 2, :, :].rearrange("p b (g h t) -> p b g h t", g=G, h=GS)
                for g in range(G):
                    rows = slice(g * HD, (g + 1) * HD)
                    src = qT[rows, :, bass.ds(tc * CH + n * S, 2 * S)].rearrange("p h (b t) -> p b h t", b=2)
                    last = nc.vector.tensor_copy(q[rows, :, g, :, :], src)
                last.then_inc(s["qbd_ready"], 2)

            def normalise(tc, n):
                dve.wait_ge(s["rr_ready"], tc * BPC + (n + 1))
                for h in range(2):
                    last = nc.vector.tensor_scalar(Pn[:, n % 2, h, :], Pex[:, n % 2, h, :],
                                                   acol[:, 3, n % 2, h:h + 1], None, ALU.mult)
                last.then_inc(s["pn_ready"], 1)

            def maxima(tc, n):
                dve.wait_ge(s["s_ps"], tc * BPC + (n + 1))
                nc.vector.tensor_reduce(acol[:, 0, n % 2, :],
                                        ps[:, 2 + n % 2, 0:2 * WK].rearrange("p (h c) -> p h c", h=2), X, ALU.max)\
                    .then_inc(s["mlinks"], 1)
                dve.wait_ge(s["mlinks"], tc * BPC + (n + 1))
                nc.vector.tensor_scalar(acol[:, 1, n % 2, :], acol[:, 0, n % 2, :], -SC, None, ALU.mult)\
                    .then_inc(s["nb_ready"], 1)

            def sums(tc, n):
                dve.wait_ge(s["p_ready"], tc * BPC + (n + 1))
                nc.vector.reciprocal(acol[:, 3, n % 2, :], acol[:, 2, n % 2, :]).then_inc(s["rr_ready"], 1)

            def values_out(tc, n):
                dve.wait_ge(s["o_ps"], tc * BPC + (O_CREDIT + n + 1))
                nc.vector.tensor_copy(oT[:, :, n * S:(n + 1) * S],
                                      ps[:, 6 + n % 2, 0:GS * S].rearrange("p (h t) -> p h t", h=GS))\
                    .then_inc(s["o_sb"], 1)

            dve.wait_ge(s["qzero"], 1)
            with dve.Fori(0, NCH) as tc:
                block_diagonals(tc, 0)
                for n in range(1, BPC + 3):
                    if n <= BPC:
                        maxima(tc, n - 1)
                    if n >= 3:
                        values_out(tc, n - 3)
                    if n % 2 == 1 and n + 1 < BPC:
                        block_diagonals(tc, n + 1)
                    if n <= BPC:
                        sums(tc, n - 1)
                        normalise(tc, n - 1)
                ch = Chain(dve, s["chain2"], tc * TAIL_LINKS)
                dve.wait_ge(s["ytok_sb"], tc + 1)
                ch.link(nc.vector.tensor_tensor(ywr, ytok, wr[:, :].unsqueeze(1).broadcast_to([P, TPC, D]), ALU.mult))
                ch.link(nc.vector.tensor_reduce(lcol[:, 0, :], ywr, X, ALU.add))
                ch.link(nc.vector.tensor_scalar(lcol[:, 1, :], lcol[:, 0, :], br[:, 0:1], None, ALU.add))

                def r3(x):
                    return x[:, 0:P].rearrange("p (t e) -> p t e", t=TPC)

                def const(x):
                    return x.unsqueeze(1).broadcast_to([P, TPC, S])

                def over(x, n=S):
                    return x.unsqueeze(2).broadcast_to([P, TPC, n])

                nc.vector.tensor_tensor(r3(rt[0]), const(C["own"]), over(lcol[:, 1, :]), ALU.mult)\
                    .then_inc(s["ldiag_ready"], 1)
                dve.wait_ge(s["lrow_ps"], tc + 1)
                nc.vector.sem_inc(s["passed"], 1)
                lrow = ps[:, 2, 0:P]
                for t in range(TPC):
                    nc.vector.max(top8[:, t, :], lrow[:, t * S:(t + 1) * S])
                ch.link(nc.vector.tensor_tensor(r3(rt[1]), r3(lrow), const(C["own"]), ALU.mult))
                ch.link(nc.vector.tensor_reduce(lcol[:, 2, :], r3(rt[1]), X, ALU.add))
                nc.vector.tensor_tensor(lex[:, :, 0:SEL], top8[:, :, 0:SEL],
                                        top8[:, :, 0:1].broadcast_to([P, TPC, SEL]), ALU.subtract)
                nc.vector.tensor_tensor(lex[:, :, SEL:SEL + 1], lcol[:, 2, :].unsqueeze(2), top8[:, :, 0:1],
                                        ALU.subtract).then_inc(s["lex_ready"], 1)
                ch.link(nc.vector.tensor_tensor(r3(rt[2]), r3(lrow), over(lcol[:, 2, :]), ALU.is_gt))
                ch.link(nc.vector.tensor_tensor(r3(rt[3]), r3(lrow), over(lcol[:, 2, :]), ALU.is_equal))
                ch.link(nc.vector.tensor_tensor(r3(rt[4]), r3(rt[3]), const(C["before"]), ALU.mult))
                ch.link(nc.vector.tensor_tensor(r3(rt[3]), r3(rt[4]), r3(rt[2]), ALU.add))
                ch.link(nc.vector.tensor_reduce(lcol[:, 3, :], r3(rt[3]), X, ALU.add))
                NP = TPC * BPT * SEL
                pk = pick[:, :, :]
                rank3 = C["rank"].unsqueeze(1).broadcast_to([P, TPC, NP])
                place3 = C["place"].rearrange("p (t n) -> p t n", t=TPC)
                ch.link(nc.vector.tensor_tensor(pickw, rank3, over(lcol[:, 3, :], NP), ALU.is_equal))
                ch.link(nc.vector.tensor_tensor(pk, pickw, place3, ALU.mult))
                dve.wait_ge(s["lexe_ready"], tc + 1)
                ch.link(nc.vector.tensor_reduce(lcol[:, 4, :], lexe[:, :, 0:SEL], X, ALU.add))
                ch.link(nc.vector.reciprocal(lcol[:, 5, :], lcol[:, 4, :]))
                ch.link(nc.vector.tensor_tensor(lcol[:, 6, :], lcol[:, 5, :], lexe[:, :, SEL], ALU.mult))
                ch.link(nc.vector.tensor_tensor(pickw, pk, over(lcol[:, 6, :], NP), ALU.mult))
                ch.link(nc.vector.tensor_copy(lcol[:, 7, :], lcol[:, 6, :]))
                nc.vector.tensor_copy(lcol[:, 7, :], lcol[:, 6, :]).then_inc(s["pick_ready"], 1)
                assert ch.n == TAIL_LINKS, ch.n
                dve_residual(dve, tc, 2 * NCH)

            with dve.Fori(0, NCH) as tc:
                moe_dve(dve, L3, 1, tc, s["chain3"])
                dve_residual(dve, tc, L3.acc0)

        @block.tensor
        def _(pe):
            nc.tensor.sem_inc(s["o_ps"], O_CREDIT)
            pe.wait_ge(s["rowps"], 1)
            nc.tensor.matmul(ps[:, 7, 0:256], C["ones"][0:B, :], diag4[0:B, :, :], start=True, stop=True)\
                .then_inc(s["rowsb"], 1)
            pe.wait_ge(s["prep"], 1)
            pe.wait_ge(s["xrows"], 16)
            pe.wait_ge(s["wdiag"], 1)
            for c in range(NCH):
                for d in range(KD):
                    for t in range(TPC):
                        i = c * TPC + t
                        last = nc.tensor.matmul(ps[:, 2 * c + d, t * P:(t + 1) * P],
                                                xrows[:, i, d * P:(d + 1) * P], wdiag[:, i, :], start=True, stop=True)
                    last.then_inc(s["y0"], 1)
            pe.wait_ge(s["mix"], 1)
            pe.wait_ge(s["y0s"], 8)
            for c in range(4):
                last = nc.tensor.matmul(ps[:, c, :], C["had"], w2mix[:, 2 * c:2 * c + 2, :], start=True, stop=True)
            last.then_inc(s["had"], 1)
            pe.wait_ge(s["down0"], 1)
            pe.wait_ge(s["w0"], 16)
            with pe.Fori(0, NCH) as tc:
                rhs = [yT[:, k, bass.ds(tc * CH, CH)] for k in range(KD)]
                for m in range(M0):
                    pe_gate_up(m, P, l0_w1, l0_w3, rhs)
                    if m >= 1:
                        pe_down(pe, m - 1, P, l0_down, tc * M0, M0 - 1)
                pe_down(pe, M0 - 1, P, l0_down, tc * M0, M0 - 1)
                pe.wait_ge(s["acc_used"], tc + 1)
            pe.wait_ge(s["small1"], 80)
            pe.wait_ge(s["castb"], 48)
            pe.wait_ge(s["down1"], 16)
            pe.wait_ge(s["big1"], 32)
            with pe.Fori(0, NCH) as tc:
                moe_pe(pe, L1, tc, small1[:, :, 0:D], small1[:, :, D:D + P], b1s, small1[:, :, D + P:],
                       l1_gate, l1_up, l1_down)
            pe.wait_ge(s["l2w"], 16)
            with pe.Fori(0, NCH) as tc:
                pe.wait_ge(s["xs_ready"], tc + 1)
                for t in range(TPC):
                    for k in range(KD):
                        last = nc.tensor.matmul(ps[:, t, :], ycur[:, k, t * P:(t + 1) * P], wqkv[:, k, :],
                                                start=(k == 0), stop=(k == KD - 1))
                last.then_inc(s["qkv_ready"], 1)
                pe.wait_ge(s["roped"], tc + 1)
                pe.wait_ge(s["v_ready"], tc + 1)
                for t in range(TPC):
                    for h in range(GS):
                        last = nc.tensor.transpose(ps[:, 4 + h, t * P:(t + 1) * P],
                                                   qkn.rearrange("p (t n) -> p t n", t=TPC)[:, t, h * P:(h + 1) * P],
                                                   ident)
                last.then_inc(s["qps_ready"], 1)
            pe.wait_ge(s["qsb_ready"], NCH)

            def keys(tc, n):
                t, q = n // BPT, n % BPT
                if q == 0:
                    pe.wait_ge(s["shuf0" if t % 2 == 0 else "shuf1"], (tc * 2 + t // 2 + 1) * (16 * 2 * BPT))
                nc.tensor.transpose(ps[:, n % 2, 0:96], kv2[0:96, t % 2, 0, q, 0:KW], ident[0:96, 0:96])
                nc.tensor.transpose(ps[:, n % 2, 96:WK], kv2[0:80, t % 2, 1, q, 0:KW], ident[0:80, 0:80])\
                    .then_inc(s["kt_ps"], 1)

            def scores(tc, n):
                pe.wait_ge(s["kt_sb"], tc * BPC + (n + 1))
                pe.wait_ge(s["qbd_ready"], tc * BPC + (n + 1))
                for h in range(2):
                    out = ps[:, 2 + n % 2, h * WK:(h + 1) * WK]
                    nc.tensor.matmul(out, Qbd[:, (n // 2) % 2, n % 2, h * P:(h + 1) * P], KTs[:, n % 2, :], start=True, stop=False)
                    last = nc.tensor.matmul(out, tselb[:, n % BPT, :],
                                            maskb[:, bass.ds(tc * (TPC * WK) + (n // BPT) * WK, WK)],
                                            start=False, stop=True)
                last.then_inc(s["s_ps"], 1)

            def probs(tc, n):
                pe.wait_ge(s["pn_ready"], tc * BPC + (n + 1))
                bank = ps[:, 4 + n % 2, :]
                for h in range(2):
                    nc.tensor.transpose(bank[0:96, h * P:(h + 1) * P], Pn[:, n % 2, h, 0:96], ident)
                for h in range(2):
                    last = nc.tensor.transpose(bank[0:80, 256 + h * P:256 + (h + 1) * P], Pn[:, n % 2, h, 96:WK],
                                               ident)
                last.then_inc(s["pt_ps"], 1)

            def values(tc, n):
                t, q = n // BPT, n % BPT
                pe.wait_ge(s["pt_sb"], tc * BPC + (n + 1))
                if n >= 2:
                    pe.wait_ge(s["o_sb"], tc * BPC + (n - 1))
                for g in range(G):
                    for h, r in ((0, 96), (1, 80)):
                        last = nc.tensor.matmul(ps[g * HD:(g + 1) * HD, 6 + n % 2, 0:GS * S],
                                                kv2[0:r, t % 2, h, q, KW + g * HD:KW + (g + 1) * HD],
                                                PTs[0:r, n % 2, h, g * GS * S:(g + 1) * GS * S],
                                                start=(h == 0), stop=(h == 1))
                last.then_inc(s["o_ps"], 1)

            with pe.Fori(0, NCH) as tc:
                for n in range(BPC + 3):
                    if n < BPC:
                        keys(tc, n)
                    if 1 <= n <= BPC:
                        scores(tc, n - 1)
                    if 2 <= n < BPC + 2:
                        probs(tc, n - 2)
                    if n >= 3:
                        values(tc, n - 3)
                pe.wait_ge(s["o_sb"], tc * BPC + BPC)
                for t in range(TPC):
                    for h in range(GS):
                        last = nc.tensor.matmul(ps[:, t // 2, (t % 2) * D:(t % 2 + 1) * D],
                                                oT[:, h, t * P:(t + 1) * P], wo[:, h, :],
                                                start=(h == 0), stop=(h == GS - 1))
                last.then_inc(s["ytok_ps"], 1)
                for d in range(KD):
                    for h in range(GS):
                        nc.tensor.matmul(ps[:, 6 + d, :], wo[:, h, d * P:(d + 1) * P], oT[:, h, :],
                                         start=(h == 0), stop=False)
                pe.wait_ge(s["ldiag_ready"], tc + 1)
                nc.tensor.matmul(ps[:, 2, 0:P], C["samebatch"], rt[0][:, 0:P], start=True, stop=True)\
                    .then_inc(s["lrow_ps"], 1)
                pe.wait_ge(s["pick_ready"], tc + 1)
                NP = TPC * BPT * SEL
                for d in range(KD):
                    for t in range(TPC):
                        last = nc.tensor.matmul(ps[:, 3, d * NP:(d + 1) * NP], ytok[:, t, d * P:(d + 1) * P],
                                                pick[:, t, :], start=(t == 0), stop=(t == TPC - 1))
                last.then_inc(s["fx_ps"], 1)
                for t in range(TPC):
                    last = nc.tensor.transpose(ps[0:NP, 4, t * P:(t + 1) * P], pickw[:, t, :], ident)
                last.then_inc(s["pwt_ps"], 1)
                pe.wait_ge(s["fx_sb"], tc + 1)
                for m in range(H2 // P):
                    for k in range(KD):
                        last = nc.tensor.matmul(ps[:, 5, m * NP:(m + 1) * NP], w21[:, k, m * P:(m + 1) * P],
                                                fx[:, k, :], start=(k == 0), stop=(k == KD - 1))
                last.then_inc(s["h_ps"], 1)
                pe.wait_ge(s["h_sb"], tc + 1)
                for m in range(H2 // P):
                    nc.tensor.matmul(ps[0:NP, 0, 0:D], hT2[:, m, :], w22[:, m, :], start=(m == 0), stop=False)
                nc.tensor.matmul(ps[0:NP, 0, 0:D], C["ones"][0:1, 0:NP], b22[0:1, :], start=False, stop=True)\
                    .then_inc(s["outl_ps"], 1)
                pe.wait_ge(s["outl_sb"], tc + 1)
                pe.wait_ge(s["pwt_sb"], tc + 1)
                for d in range(KD):
                    last = nc.tensor.matmul(ps[:, 6 + d, :], outl[0:NP, d * P:(d + 1) * P], pwT[0:NP, :],
                                            start=False, stop=True)
                last.then_inc(s["acc_ready"], 1)
                pe.wait_ge(s["acc_used"], tc + 2 * NCH + 1)

            pe.wait_ge(s["raw3"], 16)
            aT, wt, bn, wpT = raw3[:, :, 0:64], raw3[:, :, 64:320], raw3[:, :, 320:384], raw3[:, :, 384:640]
            for i in range(KD):
                for k in range(KD):
                    nc.tensor.matmul(ps[:, 0, i * 64:(i + 1) * 64], wt[:, k, i * P:(i + 1) * P], aT[:, k, :],
                                     start=(k == 0), stop=(k == KD - 1))
            for k in range(KD):
                last = nc.tensor.matmul(ps[0:64, 1, 0:D], bn[:, k, :], wpT[:, k, :], start=(k == 0),
                                        stop=(k == KD - 1))
            last.then_inc(s["fin_ready"], 1)
            pe.wait_ge(s["fint_sb"], 1)
            pe.wait_ge(s["big3"], 32)
            pe.wait_ge(s["sel3"], 16)
            with pe.Fori(0, NCH) as tc:
                moe_pe(pe, L3, tc, small3[:, :, 0:D], awt, wpb, small3[:, :, D:], l3_gate, l3_up, l3_down)


def kernel(**inputs):
    import numpy as _np
    import concourse.bacc as _bacc
    from concourse import mybir as _mybir
    from concourse.bass_utils import run_bass_kernel_spmd as _run

    v = {k: _np.asarray(x) for k, x in inputs.items()}

    def fold(w):
        return w.reshape(KD, P, -1).transpose(1, 0, 2)

    def tokens(x):
        return _np.repeat(x, S).reshape(NT, P).T

    x = v["x"].reshape(T, D)
    qkv = _np.concatenate([v["L2_cond_Wq"].T.reshape(D, G, GS, HD).transpose(0, 2, 1, 3).reshape(D, -1),
                           v["L2_cond_Wk"].T, v["L2_cond_Wv"].T], axis=1)
    wo = v["L2_cond_Wo"].T.reshape(G, GS, HD, D).transpose(0, 2, 1, 3).reshape(P, GS, D)
    up1 = v["L1_ffn_gate_up_proj"].transpose(1, 0, 2)
    w1 = v["L3_ffn_w1"].transpose(2, 0, 1)
    gu = v["L3_ffn_shared_gate_up_w"].T
    down3 = _np.concatenate([v["L3_ffn_w2"].transpose(0, 2, 1).reshape(E3 * F3, D), v["L3_ffn_shared_down_w"].T,
                             _np.zeros((L3.M * P - N3, D), _np.float32)])
    scal1 = _np.repeat(v["L1_cond_scalings"], R)
    scal3 = _np.tile(_np.repeat(v["L3_cond_scaling"], R), 2)
    row = _np.arange(P) // R
    (_, late), (_, first), (_, cast) = constants()
    kvlen = v["itok_B_37_3939"]
    arrays = {
        "cond": tokens(v["itok_B_1_198"]),
        "kv": _np.concatenate([tokens(kvlen), _np.tile(kvlen, 2)[:, None]], axis=1),
        "tables": v["itok_Bx257_0_4111"],
        "adapt": _np.broadcast_to(_np.stack([v["itok_B_0_6"], v["itok_B_0_3"]])[None], (P, 2, B)),
        "adapt_s": _np.stack([scal1, row.astype(_np.float32), scal3, (row % 4).astype(_np.float32)], axis=1),
        "late": late, "first": first, "cast": cast,
        "xrows": x.reshape(NT, P, D).transpose(1, 0, 2),
        "xT": fold(x.T),
        "cond_w": v["L0_cond_weights"].reshape(-1, S),
        "w13": _np.concatenate([fold(v["L0_ffn_W1"].T).reshape(P, -1), fold(v["L0_ffn_W3"].T).reshape(P, -1)], 1),
        "w2": v["L0_ffn_W2"].T.reshape(M0, P, D).transpose(1, 0, 2),
        "small1": fold(_np.concatenate([v["L1_cond_W"].T, v["L1_cond_A"].reshape(P, D).T, v["L1_ffn_gate"]], 1)),
        "b1": v["L1_cond_Bm"].transpose(0, 2, 1).reshape(P, D),
        "gate1": fold(up1[:, :, :F1].reshape(D, N1)),
        "up1": fold(up1[:, :, F1:].reshape(D, N1)),
        "down1": v["L1_ffn_down_proj"].reshape(L1.M, P, D).transpose(1, 0, 2),
        "cache": _np.concatenate([v["L2_cond_k_blocks"].transpose(0, 2, 1, 3).reshape(NROWS, BLOCK, KW),
                                  v["L2_cond_v_blocks"].transpose(0, 2, 1, 3).reshape(NROWS, BLOCK, KW)],
                                 axis=2).reshape(NROWS, ROW),
        "l2w": _np.concatenate([fold(qkv).reshape(P, -1), wo.reshape(P, -1), fold(v["L2_ffn_W1"]).reshape(P, -1),
                                v["L2_ffn_W2"].reshape(H2 // P, P, D).transpose(1, 0, 2).reshape(P, -1)], axis=1),
        "gq": v["L2_cond_q_norm_scale"], "gk": v["L2_cond_k_norm_scale"],
        "wr": _np.broadcast_to(v["L2_ffn_Wr"].reshape(1, D), (P, D)),
        "b21": v["L2_ffn_b1"].reshape(H2 // P, P).T,
        "b22": v["L2_ffn_b2"].reshape(1, D),
        "br": _np.broadcast_to(v["L2_ffn_br"].reshape(1, 1), (P, 1)),
        "small3": fold(_np.concatenate([v["L3_cond_W_base"].T, v["L3_ffn_gate_w"].T, v["L3_ffn_shared_gate_w"].T], 1)),
        "raw3": fold(_np.concatenate([v["L3_cond_A"].reshape(64, D).T, v["L3_cond_Wt"],
                                      v["L3_cond_B_w"].transpose(1, 0, 2).reshape(D, 64), v["L3_cond_Wp"].T], 1)),
        "gu3": _np.concatenate([
            fold(_np.concatenate([w1[:, :, :F3].reshape(D, -1), gu[:, :FS]], axis=1)).reshape(P, -1),
            fold(_np.concatenate([w1[:, :, F3:].reshape(D, -1), gu[:, FS:]], axis=1)).reshape(P, -1)], axis=1),
        "down3": down3.reshape(L3.M, P, D).transpose(1, 0, 2),
    }
    arrays["gain"] = _np.broadcast_to(_np.concatenate([_np.tile(arrays.pop("gq"), G * GS),
                                                       _np.tile(arrays.pop("gk"), G)])[None], (P, 384))
    nc = _bacc.Bacc("TRN2", target_bir_lowering=False, num_devices=1)
    sent, a = {}, {}
    for name, x in arrays.items():
        x = _np.ascontiguousarray(x)
        sent[f"in_{name}"] = x
        a[name] = nc.dram_tensor(f"in_{name}", x.shape, _mybir.dt.from_np(x.dtype), kind="ExternalInput").ap()
    a["out"] = nc.dram_tensor("out_x", (P, KD, T), _mybir.dt.float32, kind="ExternalOutput").ap()
    build(nc, a)
    r = _run(nc, [sent], core_ids=[0])
    got = r.results[0]["out_x"]
    return got.transpose(1, 0, 2).reshape(D, T).T.reshape(B, S, D)
```

```python
from contextlib import ExitStack

import numpy as np

import concourse.bass as bass
from concourse import mybir

ALU = mybir.AluOpType
ACT = mybir.ActivationFunctionType
F32 = mybir.dt.float32
BF16 = mybir.dt.bfloat16
FR = mybir.dt.float32r
I32 = mybir.dt.int32
X = mybir.AxisListType.X

P = 128
B, S, D = 64, 32, 256
T = B * S
KD = D // P
NT = T // P
CH = 512
NCH = T // CH
TPC = CH // P
BPT, BPC = P // S, CH // S
H0 = 1024
E1, K1, F1 = 32, 4, 96
E3, K3, F3, FS = 8, 2, 176, 704
R = 16
G, GS, HD = 4, 2, 32
BLOCK, WINDOW, NBLK, NROWS = 16, 128, 257, 4112
WB = WINDOW // BLOCK + S // BLOCK + 1
WK = WB * BLOCK
NEWB = S // BLOCK + 1
SEGS = NEWB * B
WG = 8
WGR = WG * WB
ROW = BLOCK * 2 * G * HD
KW = G * HD
SEL = 4
H2 = 1024
EPS = 1e-6
FAR = float(2 ** 17)
MASKED = -1e30


def pieces(total):
    return [min(P, total - a) for a in range(0, total, P)]


class Moe:

    def __init__(self, experts, chosen, shared, rank, total, step0, chunk0, acc0, piece0, split_down, high0):
        self.E, self.K, self.Z = experts, chosen, rank
        self.EW = experts + shared
        self.RW = self.EW + self.EW % 2
        self.shared = shared
        self.total = total
        self.widths = pieces(total)
        self.M = len(self.widths)
        self.step0, self.chunk0, self.acc0, self.piece0 = step0, chunk0, acc0, piece0
        self.split_down, self.high0 = split_down, high0
        self.links = 18 if shared else 16


M0 = H0 // P
SLOTS = 3
L1 = Moe(E1, K1, 0, 8 * R, E1 * F1, NCH * M0, 0, NCH, 0, False, 0)
L3 = Moe(E3, K3, 1, 4 * R, E3 * F3 + FS, NCH * (M0 + L1.M), NCH, 3 * NCH, NCH * L1.M, True,
         NCH * M0)
N1, N3 = L1.total, L3.total
TAIL_LINKS = 17
O_CREDIT = 16
MAGIC = 1.5 * 2 ** 23
TWO_PI_HI = 6.28125
TWO_PI_LO = float(2 * np.pi - 6.28125)


def constants():
    p = np.arange(P)
    t = p % S
    had = np.array([[1.0]])
    while had.shape[0] < P:
        had = np.block([[had, had], [had, -had]])
    half = HD // 2
    inv = (np.float32(1.0) / (np.float32(10000.0) ** (np.arange(half, dtype=np.float32) / np.float32(half))))
    seg_j, seg_b = np.repeat(np.arange(NEWB), B), np.tile(np.arange(B), NEWB)
    c = np.arange(WK)
    sel_t, sel_b = np.repeat(np.arange(TPC), BPT * SEL), np.tile(np.repeat(np.arange(BPT), SEL), TPC)

    def rows(x):
        return np.broadcast_to(np.asarray(x, np.float32).reshape(1, -1), (P, np.size(x)))

    late = {
        "ident": np.eye(P),
        "had": had / 32.0,
        "restart32": rows((np.arange(TPC * E1) % E1) != 0),
        "restart8": rows((np.arange(TPC * E3) % E3) != 0),
        "samebatch": (p[:, None] // S) == (p[None, :] // S),
        "own": t[:, None] == np.arange(S)[None, :],
        "before": np.arange(S)[None, :] < t[:, None],
        "place": (sel_b[None, None, :] == (p // S)[:, None, None])
        & (sel_t[None, None, :] == np.arange(TPC)[None, :, None]),
        "rank": rows(np.tile(np.arange(SEL), TPC * BPT)),
        "rowt": t[:, None],
        "ones": np.ones((P, P)),
    }
    first = {
        "slots": rows(np.arange(NBLK)),
        "segid": rows(1 + np.arange(SEGS)),
        "prio": rows(seg_b * 4 + seg_j + 1),
        "off": rows(np.arange(BLOCK)),
        "win": rows(np.arange(WB) - WINDOW // BLOCK),
        "myprio": np.stack([(p % B) * 4 + p // B + 1, (p % B) * 4 + 3], axis=1),
        "shift": rows(np.arange(NEWB * BLOCK)[None, :] - np.arange(S)[:, None]),
        "key": rows(c),
        "keyless": c[None, :] - t[:, None],
        "inv": rows(inv),
    }

    def sels(L, owner):
        x = np.zeros((P, L.M * P), np.float32)
        for j in range(3):
            x[j * L.EW + owner, np.arange(L.total)] = 1
        return x

    tsel = np.stack([((p[:, None] // S) == q) & ((p[:, None] % S) == (p[None, :] % S)) for q in range(BPT)], 1)
    cast = {
        "identb": np.eye(P),
        "tselb": tsel,
        "sel1": sels(L1, np.arange(N1) // F1),
        "sel3": sels(L3, np.minimum(np.arange(N3) // F3, E3)),
    }

    def pack(d):
        at, out, o = {}, [], 0
        for name, x in d.items():
            x = np.asarray(x, np.float32).reshape(P, -1)
            at[name] = (o, x.shape[1])
            o += x.shape[1]
            out.append(x)
        return at, np.ascontiguousarray(np.concatenate(out, axis=1))

    return pack(late), pack(first), pack(cast)


class Chain:

    def __init__(self, eng, sem, base=0):
        self.eng, self.sem, self.base, self.n = eng, sem, base, 0

    def link(self, ins):
        self.n += 1
        ins.then_inc(self.sem, 1)
        self.eng.wait_ge(self.sem, self.base + self.n)


def build(nc, a):
    (late_at, _), (first_at, _), (cast_at, _) = constants()
    with ExitStack() as ctx:
        base = {}

        def sb(name, shape, dt=F32):
            base[name] = -(-nc.sbuf_base // 32) * 32
            return ctx.enter_context(nc.sbuf_tensor(name, shape, dt))

        def rounded(name, host, word, shape):
            assert word % 8 == 0
            return nc.alloc_sbuf_tensor_at(name, [P] + shape, FR, offset=base[host] + 4 * word).ap()

        def sem(name):
            return ctx.enter_context(nc.semaphore(name))

        ps = ctx.enter_context(nc.psum_tensor("ps", [P, 8, 512], F32))

        newblk = nc.dram_tensor("newblk", (SEGS, ROW), F32).ap()
        tab_d = nc.dram_tensor("tab_d", (B, WB), F32).ap()
        dest_d = nc.dram_tensor("dest_d", (B, NEWB * BLOCK), F32).ap()
        tok_d = nc.dram_tensor("tok_d", (B, S), I32).ap()

        xT = sb("xT", [P, KD, T])
        yT = sb("yT", [P, KD, T])
        qT = yT
        big = sb("big", [P, 2 * KD * N3 + L3.M * D])
        l1_gate = big[:, 0:KD * N1].rearrange("p (k n) -> p k n", k=KD)
        l1_up = big[:, KD * N1:2 * KD * N1].rearrange("p (k n) -> p k n", k=KD)
        l3_gate = big[:, 0:KD * N3].rearrange("p (k n) -> p k n", k=KD)
        l3_up = big[:, KD * N3:2 * KD * N3].rearrange("p (k n) -> p k n", k=KD)
        l3_down = big[:, 2 * KD * N3:].rearrange("p (m n) -> p m n", n=D)
        stage = big[:, 0:2 * ROW].rearrange("p (j n) -> p j n", j=2)
        rest = big[:, 2 * ROW:]
        early = sb("early", [P, 12288])
        l0_w1 = early[:, 0:2048].rearrange("p (k n) -> p k n", k=KD)
        l0_w3 = early[:, 2048:4096].rearrange("p (k n) -> p k n", k=KD)
        l0_down = early[:, 4096:6144].rearrange("p (m n) -> p m n", n=D)
        w2mix = early[:, 6144:8192].rearrange("p (c n) -> p c n", n=D)
        xrows = early[:, 8192:12288].rearrange("p (i n) -> p i n", n=D)
        l1_down = early[:, 6144:12288].rearrange("p (m n) -> p m n", n=D)
        kvw = early[:, 0:ROW].rearrange("p (o n) -> p o n", o=BLOCK)
        halves = [early[:, ROW:2 * ROW], big[:, 2 * KD * N3:2 * KD * N3 + ROW]]
        kv2 = [x[:, j * (ROW // 2):(j + 1) * (ROW // 2)].rearrange("p (h b n) -> p h b n", h=2, b=BPT)
               for x in halves for j in range(2)]
        scr = early[:, 2 * ROW:3 * ROW]
        qkn = scr[:, 0:1536]
        sqr = scr[:, 1536:3072]
        kvrow = scr[:, 3072:4096].rearrange("p (t n) -> p t n", t=TPC)
        KTs = scr[:, 0:352].rearrange("p (s n) -> p s n", s=2)
        Pex = scr[:, 352:1056].rearrange("p (s h n) -> p s h n", s=2, h=2)
        Pn = scr[:, 1056:1760].rearrange("p (s h n) -> p s h n", s=2, h=2)
        PTs = scr[:, 1760:2784].rearrange("p (s h n) -> p s h n", s=2, h=2)
        Qbd = scr[:, 3072:4096].rearrange("p (s b n) -> p s b n", s=2, b=2)
        acol = scr[:, 2784:2800].rearrange("p (a s h) -> p a s h", a=4, s=2)
        mid = sb("mid", [P, 6144])
        F = {n: mid[:, 3072 + o:3072 + o + w] for n, (o, w) in first_at.items()}
        first_n = sum(w for _, w in first_at.values())
        assert 3072 + first_n <= 6144
        seen = mid[:, 0:3072]
        wqkv = mid[:, 0:1024].rearrange("p (k n) -> p k n", k=KD)
        wo = mid[:, 1024:1536].rearrange("p (g n) -> p g n", g=GS)
        w21 = mid[:, 1536:3584].rearrange("p (k n) -> p k n", k=KD)
        w22 = mid[:, 3584:5632].rearrange("p (m n) -> p m n", n=D)
        l0_high = rounded("l0_high", "early", 8192, [4096])
        l0_low = rounded("l0_low", "early", 0, [4096])
        parts0 = [[[x[:, (2 * i + k) * H0:(2 * i + k + 1) * H0] for x in (l0_high, l0_low)] for k in range(KD)]
                  for i in range(2)]
        l0_down2 = [rounded("l0_downh", "early", 4096, [M0, D]), rounded("l0_downl", "early", 6144, [M0, D])]
        l1_gateh, l1_gatel = rounded("l1_gateh", "early", 0, [KD, N1]), rounded("l1_gatel", "big", 0, [KD, N1])
        l1_uph = [rounded("l1_uph0", "yT", 0, [N1]), rounded("l1_uph1", "mid", 0, [N1])]
        l1_upl = rounded("l1_upl", "big", KD * N1, [KD, N1])
        l3_gateh, l3_gatel = rounded("l3_gateh", "early", 0, [KD, N3]), rounded("l3_gatel", "big", 0, [KD, N3])
        l3_uph, l3_upl = rounded("l3_uph", "early", KD * N3, [KD, N3]), rounded("l3_upl", "big", KD * N3, [KD, N3])
        l3_down2 = [rounded("l3_downh", "mid", 0, [L3.M, D]), rounded("l3_downl", "big", 2 * KD * N3, [L3.M, D])]

        late = sb("late", [P, sum(w for _, w in late_at.values())])
        C = {n: late[:, o:o + w] for n, (o, w) in late_at.items()}
        ident = C["ident"]
        identb = sb("identb", [P, P], BF16)
        tselb = sb("tselb", [P, BPT, P], BF16)
        selb = sb("selb", [P, L1.M * P], BF16)
        maskb = sb("maskb", [P, NT * WK], BF16)
        cosb = sb("cosb", [P, NT, HD // 2])
        sinb = sb("sinb", [P, NT, HD // 2])
        gain = sb("gain", [P, (G * GS + G) * HD])
        wr = sb("wr", [P, D])
        b21 = sb("b21", [P, H2 // P])
        b22 = sb("b22", [1, D])
        br = sb("br", [P, 1])
        small1 = sb("small1", [P, KD, D + P + L1.EW])
        b1s = sb("b1s", [P, D])
        small3 = sb("small3", [P, KD, D + L3.RW])
        work = sb("work", [P, 2560])
        silu = work[:, 0:1536].rearrange("p (s n) -> p s n", s=SLOTS)
        hid = [work[:, 1536:2048], work[:, 2048:2560], mid[:, 4096:4608]]
        hidh = [rounded("hidh0", "work", 1536, [CH]), rounded("hidh1", "work", 2048, [CH]),
                rounded("hidh2", "mid", 4096, [CH])]
        hidh3 = hidh[0:2] + [rounded("hidh3", "yT", 1024, [CH])]
        hidl = rounded("hidl", "mid", 4608, [SLOTS, CH])
        prod = work[:, 2048:2560]
        wdiag = work[:, 0:2048].rearrange("p (i n) -> p i n", n=P)
        raw3 = work[:, 0:1280].rearrange("p (k n) -> p k n", k=KD)
        ycur = sb("ycur", [P, KD, CH])
        yhigh = rounded("yhigh", "ycur", 0, [KD, CH])
        ylow1 = rounded("ylow1", "mid", 3072, [KD, CH])
        ylow3 = rounded("ylow3", "yT", 0, [KD, CH])
        routerh = sb("routerh", [P, KD * L1.EW], FR)
        routerl = sb("routerl", [P, KD * L1.EW], FR)
        oT = ycur
        ytok = work[:, 0:1024].rearrange("p (t n) -> p t n", t=TPC)
        ywr = scr[:, 0:1024].rearrange("p (t n) -> p t n", t=TPC)
        hT2 = work[:, 1024:1536].rearrange("p (m n) -> p m n", n=TPC * BPT * SEL)
        pwT = prod
        fx = scr[:, 1024:1152].rearrange("p (d n) -> p d n", d=KD)
        outl = scr[:, 1152:1408]
        pick = scr[:, 1408:1664].rearrange("p (t n) -> p t n", t=TPC)
        pickw = scr[:, 1664:1920].rearrange("p (t n) -> p t n", t=TPC)
        lcol = scr[:, 2800:2864].rearrange("p (a t) -> p a t", t=TPC)
        lex = scr[:, 2864:2884].rearrange("p (t n) -> p t n", t=TPC)
        lexe = scr[:, 2884:2904].rearrange("p (t n) -> p t n", t=TPC)
        zm = sb("zm", [P, CH])
        awt = sb("awt", [P, KD, 64])
        wpb = sb("wpb", [64, D])
        top8 = sb("top8", [P, TPC, 8])
        rt = [sb(f"rt{i}", [P, TPC * L1.EW]) for i in range(6)]
        rcol = sb("rcol", [P, 5, TPC])
        parts = sb("parts", [P, TPC * 3 * L1.EW], BF16)
        partsT = sb("partsT", [3 * L1.EW, CH], BF16)
        kcol = sb("kcol", [P, 2, TPC * 12])

        wrows = prod.rearrange("p (i n) -> p i n", i=NT)
        cond_i = sb("cond_i", [P, NT], I32)
        cond_f = sb("cond_f", [P, NT])
        cond_x = sb("cond_x", [P, NT], I32)
        adapt_i = zm[:, 0:2 * B].bitcast(I32).rearrange("p (l b) -> p l b", l=2)
        adapt_f = zm[:, 2 * B:4 * B].rearrange("p (l b) -> p l b", l=2)
        adapt_s = sb("adapt_s", [P, 4])
        amask = sb("amask", [P, 2, B])
        bt_i = rest[:, 0:257].bitcast(I32)
        bt_f = rest[:, 257:514]
        diag4 = rest[:, 514:770].rearrange("p (j b) -> p j b", j=4)
        rowinfo = rest[:, 770:1026]
        ix = rest[:, 1026:1090]
        cmpt = rest[:, 1090:1090 + 3072]
        eqt = rest[:, 4162:4354]
        dest = rest[:, 4354:4402]
        kv_i = sb("kv_i", [P, NT + 1], I32)
        kv_f = sb("kv_f", [P, 4, NT + 1])
        win_i = sb("win_i", [BPT * WB, NT], I32)
        new_i = sb("new_i", [BPT * WB, NT], I32)
        tok_i = sb("tok_i", [P, NT], I32)
        seg_i = sb("seg_i", [P, 2], I32)
        cur_i = sb("cur_i", [P, 3 * TPC], I32)
        blkw = sb("blkw", [BPT * WB, NT])

        names = ("late cast x xrows cond w0 w2 small1 big1 down1 ints first small2 small2b l2w raw3 big3 sel3 kvt "
                 "condidx condx wrows wzero wdiag y0 y0s mix had down0 castb "
                 "gu_ready w_ready silu_ready prod_ready hid_ready acc_ready acc_used z_ready zm_ready "
                 "y_ready ycur_ready lg_ready shifted exp_ready parts_ready partsT_ready partsT_used "
                 "chain1 chain3 chain2 prep amask tabst tabld destst destld tokst tokld seggot segst rowps "
                 "rowsb trig angles fold folds foldg xs_ready qkv_ready squared ssq_ready root_ready v_ready "
                 "normed gained rot_ready roped qps_ready qsb_ready scattered ropesteps qklinks "
                 "curidx curidx2 gold0 gold1 gnew0 gnew1 shuf0 shuf1 kt_ps kt_sb qbd_ready s_ps nb_ready p_ready rr_ready pn_ready "
                 "pt_ps pt_sb o_ps o_sb qzero ytok_ps ytok_sb ldiag_ready lrow_ps lex_ready lexe_ready "
                 "pick_ready fx_ps fx_sb pwt_ps pwt_sb h_ps h_sb outl_ps outl_sb fin_ready fint_ps fint_sb s_out "
                 "stdlinks mlinks qkv_end passed ylow_ready hfull_ready hhigh_ready w0h w0l downh1 w1h w1l w3h w3l wqkv gu_done routed3 rowused masked keys").split()
        s = {n: sem(n) for n in names}


        def split_matmul(out, weights, rows, start, stop):
            (wh, wl), (xh, xl) = weights, rows
            for n, (w, x) in enumerate(((wh, xh), (wh, xl), (wl, xh))):
                last = nc.tensor.matmul(out, w, x, start=start and n == 0,
                                        stop=stop and n == 2)
            return last

        def pe_gate_up(m, w, gate, up, ylow=ylow1):
            cols = slice(m * P, m * P + w)
            for bank, weights in ((m % 2, gate), (2 + m % 2, up)):
                for k in range(KD):
                    last = split_matmul(ps[0:w, bank, :], [x[:, cols] for x in weights[k]],
                                        (yhigh[:, k, :], ylow[:, k, :]), k == 0, k == KD - 1)
            last.then_inc(s["gu_ready"], 1)

        def pe_down(pe, m, w, down, split, step, last_m, high=hidh):
            pe.wait_ge(s["hid_ready"], step + m + 1)
            for d in range(KD):
                cols = slice(d * P, (d + 1) * P)
                if not split:
                    last = nc.tensor.matmul(ps[:, 6 + d, :], down[0:w, m, cols], hid[m % SLOTS][0:w, :],
                                            start=(m == 0), stop=(m == last_m))
                else:
                    last = split_matmul(ps[:, 6 + d, :], [x[0:w, m, cols] for x in down],
                                        (high[m % SLOTS][0:w, :], hidl[0:w, m % SLOTS, :]), m == 0, m == last_m)
            if m == last_m:
                last.then_inc(s["acc_ready"], 1)

        def act_high(act, m, w, step, high=hidh):
            act.wait_ge(s["hfull_ready"], step + m + 1)
            nc.scalar.activation(high[m % SLOTS][0:w, :], silu[0:w, m % SLOTS, :], ACT.Copy)\
                .then_inc(s["hhigh_ready"], 1)

        def dve_low(dve, m, w, step, high=hidh):
            dve.wait_ge(s["hhigh_ready"], step + m + 1)
            nc.vector.tensor_tensor(hidl[0:w, m % SLOTS, :], silu[0:w, m % SLOTS, :], high[m % SLOTS][0:w, :],
                                    ALU.subtract).then_inc(s["hid_ready"], 1)

        def act_silu(act, m, w, step):
            act.wait_ge(s["gu_ready"], step + m + 1)
            nc.scalar.activation(silu[0:w, m % SLOTS, :], ps[0:w, m % 2, :], ACT.Silu).then_inc(s["silu_ready"], 1)

        def dve_residual(dve, tc, acc0):
            dve.wait_ge(s["acc_ready"], tc + acc0 + 1)
            for d in range(KD):
                cols = xT[:, d, bass.ds(tc * CH, CH)]
                last = nc.vector.tensor_tensor(cols, ps[:, 6 + d, :], cols, ALU.add)
            last.then_inc(s["acc_used"], 1)


        def moe_pe(pe, L, tc, wbase, wa, wb, gate, up, down):
            step, n, piece = tc * L.M + L.step0, tc + L.chunk0, tc * L.M + L.piece0
            ylow = ylow3 if L.shared else ylow1
            xc = [xT[:, k, bass.ds(tc * CH, CH)] for k in range(KD)]
            for k in range(KD):
                last = nc.tensor.matmul(ps[0:L.Z, 0, :], wa[:, k, :], xc[k], start=(k == 0), stop=(k == KD - 1))
            last.then_inc(s["z_ready"], 1)
            for d in range(KD):
                for k in range(KD):
                    nc.tensor.matmul(ps[:, 2 + d, :], wbase[:, k, d * P:(d + 1) * P], xc[k],
                                     start=(k == 0), stop=False)
            pe.wait_ge(s["zm_ready"], n + 1)
            for d in range(KD):
                last = nc.tensor.matmul(ps[:, 2 + d, :], wb[0:L.Z, d * P:(d + 1) * P], zm[0:L.Z, :],
                                        start=False, stop=True)
            last.then_inc(s["y_ready"], 1)
            pe.wait_ge(s["ylow_ready"], NCH + n + 1)
            for t in range(TPC):
                cols = slice(t * P, (t + 1) * P)
                for k in range(KD):
                    last = split_matmul(ps[:, 4, t * L.RW:(t + 1) * L.RW], (yhigh[:, k, cols], ylow[:, k, cols]),
                                        [x[:, k * L.RW:(k + 1) * L.RW] for x in (routerh, routerl)], k == 0, k == KD - 1)
            last.then_inc(s["lg_ready"], 1)

            def spread(m):
                w = L.widths[m]
                nc.tensor.matmul(ps[0:w, 4 + m % 2, :], selb[0:3 * L.EW, m * P:m * P + w], partsT[0:3 * L.EW, :],
                                 start=True, stop=True).then_inc(s["w_ready"], 1)

            high = hidh3 if L.shared else hidh
            for m in range(L.M):
                if m >= 2:
                    pe.wait_ge(s["prod_ready"], piece + m - 1)
                pe_gate_up(m, L.widths[m], gate, up, ylow)
                if m == 1:
                    pe.wait_ge(s["parts_ready"], n + 1)
                    half = ps[:, 5, :].bitcast(BF16)
                    for t in range(TPC):
                        last = nc.tensor.transpose(half[0:3 * L.EW, t * P:(t + 1) * P],
                                                   parts[:, t * 3 * L.EW:(t + 1) * 3 * L.EW], identb[:, :])
                    last.then_inc(s["partsT_ready"], 1)
                    pe.wait_ge(s["partsT_used"], n + 1)
                    spread(0)
                    spread(1)
                    pe.wait_ge(s["acc_used"], tc + L.acc0)
                if m >= 2:
                    if L.split_down:
                        pe.wait_ge(s["hfull_ready"], tc * L.M + (L.high0 + m - 1))
                    else:
                        pe.wait_ge(s["hid_ready"], step + m - 1)
                    spread(m)
                    pe_down(pe, m - 2, L.widths[m - 2], down, L.split_down, step, L.M - 1, high)
            for m in (L.M - 2, L.M - 1):
                pe_down(pe, m, L.widths[m], down, L.split_down, step, L.M - 1, high)

        def moe_act(act, L, tc):
            step, n = tc * L.M + L.step0, tc + L.chunk0
            act.wait_ge(s["y_ready"], n + 1)
            for d in range(KD):
                last = nc.scalar.activation(yhigh[:, d, :], ps[:, 2 + d, :], ACT.Copy)
            last.then_inc(s["ycur_ready"], 1)
            act.wait_ge(s["shifted"], n + 1)
            last = nc.scalar.activation(rt[1][:, 0:TPC * L.E], rt[0][:, 0:TPC * L.E], ACT.Exp)
            if L.shared:
                last = nc.scalar.activation(rcol[:, 3, :], rcol[:, 4, :], ACT.Exp, scale=-1.0)
            last.then_inc(s["exp_ready"], 1)
            act_silu(act, 0, L.widths[0], step)
            act_silu(act, 1, L.widths[1], step)
            act.wait_ge(s["partsT_ready"], n + 1)
            nc.scalar.activation(partsT[0:3 * L.EW, :], ps[:, 5, :].bitcast(BF16)[0:3 * L.EW, 0:CH],
                                 ACT.Copy).then_inc(s["partsT_used"], 1)
            for m in range(2, L.M):
                if L.split_down:
                    for h in range(0 if m == 2 else m - 1, m):
                        act_high(act, h, L.widths[h], tc * L.M + L.high0, hidh3)
                act_silu(act, m, L.widths[m], step)
            if L.split_down:
                act_high(act, L.M - 1, L.widths[-1], tc * L.M + L.high0, hidh3)

        def moe_dve(dve, L, li, tc, chain_sem):
            step, n, piece = tc * L.M + L.step0, tc + L.chunk0, tc * L.M + L.piece0
            dve.wait_ge(s["z_ready"], n + 1)
            nc.vector.tensor_tensor(
                zm[0:L.Z, :].rearrange("p (b s) -> p b s", s=S),
                ps[0:L.Z, 0, :].rearrange("p (b s) -> p b s", s=S),
                amask[0:L.Z, li, bass.ds(tc * BPC, BPC)].unsqueeze(2).broadcast_to([L.Z, BPC, S]),
                ALU.mult).then_inc(s["zm_ready"], 1)
            dve.wait_ge(s["ycur_ready"], NCH + n + 1)
            ylow = ylow3 if L.shared else ylow1
            for d in range(KD):
                last = nc.vector.tensor_tensor(ylow[:, d, :], ps[:, 2 + d, :], yhigh[:, d, :],
                                               ALU.subtract)
            last.then_inc(s["ylow_ready"], 1)
            E, EW = L.E, L.EW
            flat = TPC * E

            def tiles(x, e=E):
                return x[:, 0:TPC * e].rearrange("p (t e) -> p t e", t=TPC)

            def over(col, e=E):
                return col.broadcast_to([P, TPC, e])

            ch = Chain(dve, chain_sem, tc * L.links)
            lg = tiles(ps[:, 4, :], L.RW)[:, :, 0:E]
            dve.wait_ge(s["lg_ready"], n + 1)
            nc.vector.sem_inc(s["passed"], 1)
            for t in range(TPC):
                last = nc.vector.max(top8[:, t, :], lg[:, t, :])
            ch.link(last)
            if L.shared:
                nc.vector.tensor_copy(rcol[:, 4, :], tiles(ps[:, 4, :], L.RW)[:, :, E])
            nc.vector.tensor_tensor(tiles(rt[0]), lg, over(top8[:, :, 0:1]), ALU.subtract)\
                .then_inc(s["shifted"], 1)
            ch.link(nc.vector.tensor_tensor(tiles(rt[2]), lg, over(top8[:, :, L.K - 1:L.K]), ALU.is_gt))
            ch.link(nc.vector.tensor_tensor(tiles(rt[3]), lg, over(top8[:, :, L.K - 1:L.K]), ALU.is_equal))
            ch.link(nc.vector.tensor_reduce(rcol[:, 0, :], tiles(rt[2]), X, ALU.add))
            ch.link(nc.vector.tensor_tensor_scan(rt[4][:, 0:flat], C["restart%d" % E][:, 0:flat], rt[3][:, 0:flat],
                                                 0.0, ALU.mult, ALU.add))
            ch.link(nc.vector.tensor_tensor(tiles(rt[5]), tiles(rt[4]), over(rcol[:, 0, :].unsqueeze(2)), ALU.add))
            ch.link(nc.vector.scalar_tensor_tensor(rt[4][:, 0:flat], rt[5][:, 0:flat], float(L.K), rt[3][:, 0:flat],
                                                   ALU.is_le, ALU.mult))
            ch.link(nc.vector.tensor_tensor(rt[3][:, 0:flat], rt[2][:, 0:flat], rt[4][:, 0:flat], ALU.add))
            dve.wait_ge(s["exp_ready"], n + 1)
            ch.link(nc.vector.tensor_tensor(rt[2][:, 0:flat], rt[1][:, 0:flat], rt[3][:, 0:flat], ALU.mult))
            ch.link(nc.vector.tensor_reduce(rcol[:, 1, :], tiles(rt[2]), X, ALU.add))
            ch.link(nc.vector.reciprocal(rcol[:, 2, :], rcol[:, 1, :]))
            weights = tiles(rt[5], EW)
            ch.link(nc.vector.tensor_tensor(weights[:, :, 0:E], tiles(rt[2]), over(rcol[:, 2, :].unsqueeze(2)),
                                            ALU.mult))
            if L.shared:
                ch.link(nc.vector.tensor_scalar(rcol[:, 0, :], rcol[:, 3, :], 1.0, None, ALU.add))
                ch.link(nc.vector.reciprocal(weights[:, :, E:EW], rcol[:, 0, :].unsqueeze(2)))
            part = [parts[:, 0:TPC * 3 * EW].rearrange("p (t j e) -> p t j e", t=TPC, j=3)[:, :, j, :]
                    for j in range(3)]
            ch.link(nc.vector.tensor_copy(part[0], weights))
            ch.link(nc.vector.tensor_tensor(tiles(rt[0], EW), weights, part[0], ALU.subtract))
            ch.link(nc.vector.tensor_copy(part[1], tiles(rt[0], EW)))
            ch.link(nc.vector.tensor_tensor(tiles(rt[2], EW), tiles(rt[0], EW), part[1], ALU.subtract))
            nc.vector.tensor_copy(part[2], tiles(rt[2], EW)).then_inc(s["parts_ready"], 1)
            assert ch.n == L.links, ch.n

            for m, w in enumerate(L.widths):
                dve.wait_ge(s["silu_ready"], step + m + 1)
                row = silu[0:w, m % SLOTS, :]
                nc.vector.tensor_tensor(row, row, ps[0:w, 2 + m % 2, :],
                                        ALU.mult).then_inc(s["prod_ready"], 1)
                dve.wait_ge(s["prod_ready"], piece + m + 1)
                dve.wait_ge(s["w_ready"], piece + m + 1)
                if L.split_down:
                    nc.vector.tensor_tensor(row, row, ps[0:w, 4 + m % 2, :], ALU.mult).then_inc(s["hfull_ready"], 1)
                    dve_low(dve, m, w, tc * L.M + L.high0, hidh3)
                else:
                    nc.vector.tensor_tensor(hid[m % SLOTS][0:w, :], row, ps[0:w, 4 + m % 2, :], ALU.mult)\
                        .then_inc(s["hid_ready"], 1)

        rows16 = newblk.rearrange("s (o n) -> (s o) n", n=2 * KW)
        SC = 1.0 / 16.0
        block = ctx.enter_context(nc.Block())

        @block.sync
        def _(sp):
            sp.dma_start(cond_i[:, :], a["cond"]).then_inc(s["cond"], 16)
            sp.dma_start(late[:, :], a["late"]).then_inc(s["late"], 16)
            sp.dma_start(kv_i[:, :], a["kv"]).then_inc(s["ints"], 16)
            sp.dma_start(bt_i[0:B, :], a["tables"]).then_inc(s["ints"], 16)
            sp.dma_start(mid[:, 3072:3072 + first_n], a["first"]).then_inc(s["first"], 16)
            sp.dma_start(l0_down, a["w2"]).then_inc(s["w2"], 16)
            sp.dma_start(xrows, a["xrows"]).then_inc(s["xrows"], 16)
            sp.dma_start(early[:, 0:4096], a["w13"]).then_inc(s["w0"], 16)
            sp.dma_start(xT[:, :, :], a["xT"]).then_inc(s["x"], 16)
            for dst, name in ((small1, "small1"), (b1s, "b1"), (small3, "small3"), (adapt_i, "adapt"),
                              (adapt_s, "adapt_s")):
                sp.dma_start(dst if dst is adapt_i else dst[:], a[name]).then_inc(s["small1"], 16)
            for dst, name in ((gain, "gain"), (wr, "wr"), (b21, "b21"), (b22, "b22"), (br, "br")):
                sp.dma_start(dst[:], a[name]).then_inc(s["small2"], 16)
            sp.wait_ge(s["tabst"], 1)
            sp.dma_start(tab_d, ix[0:B, 16:16 + WB]).then_inc(s["tabld"], 16)
            sp.wait_ge(s["tabld"], 16)
            with nc.allow_non_contiguous_dma(reason="704 words"):
                sp.dma_start(blkw[:, :], tab_d.rearrange("(g b) i -> (b i) g", b=BPT)).then_inc(s["tabld"], 16)
            sp.wait_ge(s["destst"], 1)
            for j in range(NEWB):
                src = dest[(j % 2) * B:(j % 2 + 1) * B, (j // 2) * BLOCK:(j // 2 + 1) * BLOCK]
                sp.dma_start(dest_d[:, j * BLOCK:(j + 1) * BLOCK], src).then_inc(s["destld"], 16)
            sp.wait_ge(s["destld"], 16 * NEWB)
            sp.dma_start(rest[0:B, 4402:4450], dest_d).then_inc(s["destld"], 16)
            sp.wait_ge(s["tokst"], 1)
            sp.dma_start(tok_d, rest[0:B, 4450:4482].bitcast(I32)).then_inc(s["tokld"], 16)
            sp.wait_ge(s["tokld"], 16)
            with nc.allow_non_contiguous_dma(reason="2048 words"):
                sp.dma_start(tok_i[:, :], tok_d.rearrange("(i b) t -> (b t) i", b=BPT)).then_inc(s["tokld"], 16)
            sp.wait_ge(s["seggot"], 32)
            sp.dma_start(newblk[0:P, :], stage[:, 0, :]).then_inc(s["segst"], 16)
            sp.dma_start(newblk[P:SEGS, :], stage[0:B, 1, :]).then_inc(s["segst"], 16)
            sp.wait_ge(s["segst"], 32)
            sp.wait_ge(s["tokst"], 1)
            sp.dma_start(l1_gate, a["gate1"]).then_inc(s["big1"], 16)
            sp.dma_start(l1_up, a["up1"]).then_inc(s["big1"], 16)
            sp.wait_ge(s["acc_used"], NCH)
            sp.dma_start(l1_down, a["down1"]).then_inc(s["down1"], 16)
            sp.wait_ge(s["acc_used"], 2 * NCH)
            sp.dma_start(mid[:, 0:1024], a["l2w"][:, 0:1024]).then_inc(s["wqkv"], 16)
            k0 = first_at["key"][0]
            assert first_at["keyless"][0] == k0 + WK
            sp.dma_start(early[:, 7168:7168 + 2 * WK], a["first"][:, k0:k0 + 2 * WK]).then_inc(s["keys"], 16)
            sp.dma_start(mid[:, 1024:5632], a["l2w"][:, 1024:5632]).then_inc(s["l2w"], 16)
            sp.dma_start(big[:, 0:2 * KD * N3], a["gu3"]).then_inc(s["big3"], 16)
            with sp.Fori(0, NCH) as tc:
                for t in range(TPC):
                    slot = t % 2
                    sp.wait_ge(s["gnew0" if slot == 0 else "gnew1"], (tc * 2 + t // 2 + 1) * 16)
                    nc.sync.sem_inc(s["passed"], 1)
                    sp.wait_ge(s["o_ps"], tc * BPC + (O_CREDIT - BPC + BPT * (t + 1)))
                    for q in range(BPT):
                        for h, (i0, i1) in enumerate(((0, 6), (6, WB))):
                            sp.dma_start(kv2[t][0:(i1 - i0) * BLOCK, h, q, :],
                                         kvw[slot * 64 + q * WB + i0:slot * 64 + q * WB + i1, :, :])\
                                .then_inc(s["shuf0" if slot == 0 else "shuf1"], 16)
            sp.wait_ge(s["acc_used"], 3 * NCH)
            sp.dma_start(raw3, a["raw3"]).then_inc(s["raw3"], 16)
            sp.dma_start(l3_down, a["down3"]).then_inc(s["big3"], 16)
            with sp.Fori(0, NCH) as tc:
                sp.wait_ge(s["acc_used"], tc + 3 * NCH + 1)
                sp.dma_start(a["out"][:, :, bass.ds(tc * CH, CH)], xT[:, :, bass.ds(tc * CH, CH)])\
                    .then_inc(s["s_out"], 16)
            sp.wait_ge(s["s_out"], 16 * NCH)

        @block.gpsimd
        def _(pool):
            def gather(out, src, idx, signal, **kw):
                nc.gpsimd.indirect_dma_start(
                    out=out, out_offset=None, in_=src, in_offset=bass.IndirectOffsetOnAxis(ap=idx, axis=0), **kw
                ).then_inc(signal, 16)

            nc.gpsimd.memset(work[:, 0:2048], 0.0).then_inc(s["wzero"], 1)
            pool.wait_ge(s["condx"], 1)
            for i in range(NT):
                gather(wrows[:, i, :], a["cond_w"], cond_x[:, i:i + 1], s["wrows"])
            o1, o2 = cast_at["identb"][0], cast_at["sel1"][0]
            pool.dma_start(identb[:, :], a["cast"][:, o1:o1 + P]).then_inc(s["castb"], 16)
            pool.dma_start(tselb[:, :, :], a["cast"][:, o1 + P:o2].rearrange("p (q n) -> p q n", q=BPT))\
                .then_inc(s["castb"], 16)
            pool.dma_start(selb[:, :], a["cast"][:, o2:o2 + L1.M * P]).then_inc(s["castb"], 16)
            pool.wait_ge(s["condidx"], 1)
            gather(stage[:, 0, :], a["cache"], seg_i[:, 0:1], s["seggot"])
            gather(stage[0:B, 1, :], a["cache"], seg_i[0:B, 1:2], s["seggot"])

            pool.wait_ge(s["segst"], 32)
            pool.wait_ge(s["tokld"], 32)
            with pool.Fori(0, NCH) as tc:
                nc.gpsimd.tensor_copy(cur_i[:, 0:TPC], tok_i[:, bass.ds(tc * TPC, TPC)]).then_inc(s["curidx"], 1)
                pool.wait_ge(s["curidx"], tc + 1)
                pool.wait_ge(s["roped"], tc + 1)
                pool.wait_ge(s["v_ready"], tc + 1)
                nc.gpsimd.sem_inc(s["passed"], 1)
                for t in range(TPC):
                    nc.gpsimd.indirect_dma_start(
                        out=rows16, out_offset=bass.IndirectOffsetOnAxis(ap=cur_i[:, t:t + 1], axis=0),
                        in_=kvrow[:, t, :], in_offset=None, bounds_check=SEGS * BLOCK - 1, oob_is_err=False,
                    ).then_inc(s["scattered"], 16)
                pool.wait_ge(s["scattered"], (tc + 1) * (16 * TPC))
                nc.gpsimd.sem_inc(s["passed"], 1)

            pool.wait_ge(s["scattered"], 16 * NT)
            pool.wait_ge(s["masked"], 1)
            pool.wait_ge(s["qkv_end"], 1)
            nc.gpsimd.memset(Qbd, 0.0).then_inc(s["qzero"], 1)
            pool.wait_ge(s["qzero"], 1)
            o3 = cast_at["sel3"][0]
            pool.dma_start(selb[:, 0:L3.M * P], a["cast"][:, o3:o3 + L3.M * P]).then_inc(s["sel3"], 16)

            def old_blocks(t):
                slot = t % 2
                gather(early[slot * 64:slot * 64 + BPT * WB, 0:ROW], a["cache"], cur_i[0:BPT * WB, 4 + t:5 + t],
                       s["gold0" if slot == 0 else "gold1"])

            def new_blocks(tc, t):
                slot = t % 2
                pool.wait_ge(s["gold0" if slot == 0 else "gold1"], (tc * 2 + t // 2 + 1) * 16)
                nc.gpsimd.sem_inc(s["passed"], 1)
                gather(early[slot * 64:slot * 64 + BPT * WB, 0:ROW], newblk, cur_i[0:BPT * WB, 8 + t:9 + t],
                       s["gnew0" if slot == 0 else "gnew1"], bounds_check=SEGS - 1, oob_is_err=False)

            with pool.Fori(0, NCH) as tc:
                nc.gpsimd.tensor_copy(cur_i[0:BPT * WB, 4:8], win_i[:, bass.ds(tc * TPC, TPC)])
                nc.gpsimd.tensor_copy(cur_i[0:BPT * WB, 8:12], new_i[:, bass.ds(tc * TPC, TPC)])\
                    .then_inc(s["curidx2"], 1)
                pool.wait_ge(s["curidx2"], tc + 1)
                nc.gpsimd.sem_inc(s["passed"], 1)
                for t in range(TPC):
                    if t >= 2:
                        pool.wait_ge(s["shuf0" if t % 2 == 0 else "shuf1"], (tc * 2 + t // 2) * (16 * 2 * BPT))
                        nc.gpsimd.sem_inc(s["passed"], 1)
                    old_blocks(t)
                    if t >= 1:
                        new_blocks(tc, t - 1)
                new_blocks(tc, TPC - 1)
                pool.wait_ge(s["shuf0"], (tc * 2 + 2) * (16 * 2 * BPT))
                pool.wait_ge(s["shuf1"], (tc * 2 + 2) * (16 * 2 * BPT))
                nc.gpsimd.sem_inc(s["passed"], 1)

        @block.scalar
        def _(act):
            act.wait_ge(s["folds"], 1)
            nc.scalar.activation(sinb[:], sinb[:], ACT.Sin)
            nc.scalar.activation(cosb[:], cosb[:], ACT.Sin).then_inc(s["trig"], 1)
            for g in range(0, 8, 2):
                act.wait_ge(s["y0"], g + 1)
                nc.scalar.activation(yT[:, g % 2, (g // 2) * CH:(g // 2 + 1) * CH], ps[:, g, :], ACT.Copy)\
                    .then_inc(s["y0s"], 1)
            act.wait_ge(s["y0"], 8)
            act.wait_ge(s["w0"], 16)
            nc.scalar.activation(l0_high, early[:, 0:4096], ACT.Copy).then_inc(s["w0h"], 1)
            act.wait_ge(s["had"], 1)
            nc.scalar.activation(l0_down2[0], ps[:, 0:4, :].rearrange("p c (m n) -> p (c m) n", n=D), ACT.Copy).then_inc(s["down0"], 1)
            with act.Fori(0, NCH) as tc:
                act.wait_ge(s["gu_done"], tc + 1)
                nc.scalar.activation(yhigh, yT[:, :, bass.ds(tc * CH, CH)], ACT.Copy).then_inc(s["ycur_ready"], 1)
                for m in range(M0 + 1):
                    if m >= 1:
                        act_high(act, m - 1, P, tc * M0)
                    if m < M0:
                        act_silu(act, m, P, tc * M0)
            act.wait_ge(s["acc_used"], NCH)
            act.wait_ge(s["big1"], 32)
            act.wait_ge(s["tokst"], 1)
            for k in range(KD):
                nc.scalar.activation(l1_gateh[:, k, :], l1_gate[:, k, :], ACT.Copy).then_inc(s["w1h"], 1)
                nc.scalar.activation(l1_uph[k], l1_up[:, k, :], ACT.Copy).then_inc(s["w1h"], 1)
            with act.Fori(0, NCH) as tc:
                moe_act(act, L1, tc)

            with act.Fori(0, NCH) as tc:
                act.wait_ge(s["acc_used"], 2 * NCH)
                nc.scalar.activation(ycur[:, :, :], xT[:, :, bass.ds(tc * CH, CH)], ACT.Copy)\
                    .then_inc(s["xs_ready"], 1)
                act.wait_ge(s["qkv_ready"], tc + 1)
                nc.scalar.activation(sqr.rearrange("p (t n) -> p t n", t=TPC), ps[:, 0:4, 0:384], ACT.Square)\
                    .then_inc(s["squared"], 1)
                nc.scalar.activation(kvrow[:, :, KW:2 * KW], ps[:, 0:4, 384:512], ACT.Copy).then_inc(s["v_ready"], 1)
                act.wait_ge(s["ssq_ready"], tc + 1)
                nc.scalar.activation(kcol[:, 0, :], kcol[:, 1, :], ACT.Sqrt).then_inc(s["root_ready"], 1)
                act.wait_ge(s["qps_ready"], tc + 1)
                nc.scalar.activation(qT[:, :, bass.ds(tc * CH, CH)], ps[:, 4:6, :], ACT.Copy)\
                    .then_inc(s["qsb_ready"], 1)
                act.wait_ge(s["scattered"], (tc + 1) * (16 * TPC))
            act.wait_ge(s["qsb_ready"], NCH)
            nc.scalar.activation(rcol[:, 3, :], rcol[:, 1, :], ACT.Copy).then_inc(s["qkv_end"], 1)

            def keys_out(tc, n):
                act.wait_ge(s["kt_ps"], tc * BPC + (n + 1))
                nc.scalar.activation(KTs[:, n % 2, :], ps[:, n % 2, 0:WK], ACT.Copy).then_inc(s["kt_sb"], 1)

            def exponentials(tc, n):
                act.wait_ge(s["nb_ready"], tc * BPC + (n + 1))
                for h in range(2):
                    last = nc.scalar.activation(Pex[:, n % 2, h, :], ps[:, 2 + n % 2, h * WK:(h + 1) * WK], ACT.Exp,
                                                bias=acol[:, 1, n % 2, h:h + 1], scale=SC,
                                                accum_out=acol[:, 2, n % 2, h:h + 1])
                last.then_inc(s["p_ready"], 1)

            def probs_out(tc, n):
                act.wait_ge(s["pt_ps"], tc * BPC + (n + 1))
                nc.scalar.activation(PTs[0:96, n % 2, 0, :], ps[0:96, 4 + n % 2, 0:256], ACT.Copy)
                nc.scalar.activation(PTs[0:80, n % 2, 1, :], ps[0:80, 4 + n % 2, 256:512], ACT.Copy)\
                    .then_inc(s["pt_sb"], 1)

            with act.Fori(0, NCH) as tc:
                for n in range(BPC + 2):
                    if n < BPC:
                        keys_out(tc, n)
                    if 1 <= n <= BPC:
                        exponentials(tc, n - 1)
                    if n >= 2:
                        probs_out(tc, n - 2)
                act.wait_ge(s["ytok_ps"], tc + 1)
                nc.scalar.activation(ytok.rearrange("p (a b) n -> p a (b n)", a=2), ps[:, 0:2, :], ACT.Copy)\
                    .then_inc(s["ytok_sb"], 1)
                act.wait_ge(s["lex_ready"], tc + 1)
                nc.scalar.activation(lexe, lex, ACT.Exp).then_inc(s["lexe_ready"], 1)
                act.wait_ge(s["fx_ps"], tc + 1)
                nc.scalar.activation(fx, ps[:, 3, 0:128].rearrange("p (d n) -> p d n", d=KD), ACT.Copy)\
                    .then_inc(s["fx_sb"], 1)
                act.wait_ge(s["pwt_ps"], tc + 1)
                nc.scalar.activation(pwT[0:64, :], ps[0:64, 4, :], ACT.Copy).then_inc(s["pwt_sb"], 1)
                act.wait_ge(s["h_ps"], tc + 1)
                for m in range(H2 // P):
                    last = nc.scalar.activation(hT2[:, m, :], ps[:, 5, m * 64:(m + 1) * 64], ACT.Gelu,
                                                bias=b21[:, m:m + 1])
                last.then_inc(s["h_sb"], 1)
                act.wait_ge(s["outl_ps"], tc + 1)
                nc.scalar.activation(outl[0:64, :], ps[0:64, 0, 0:256], ACT.Copy).then_inc(s["outl_sb"], 1)

            act.wait_ge(s["fin_ready"], 1)
            nc.scalar.activation(awt[:, :, :], ps[:, 0, 0:128].rearrange("p (k n) -> p k n", k=KD), ACT.Copy)
            nc.scalar.activation(wpb[:, :], ps[0:64, 1, 0:256], ACT.Copy).then_inc(s["fint_sb"], 1)
            act.wait_ge(s["acc_used"], 3 * NCH)
            act.wait_ge(s["big3"], 16)
            for k in range(KD):
                nc.scalar.activation(l3_gateh[:, k, :], l3_gate[:, k, :], ACT.Copy).then_inc(s["w3h"], 1)
                nc.scalar.activation(l3_uph[:, k, :], l3_up[:, k, :], ACT.Copy).then_inc(s["w3h"], 1)
            act.wait_ge(s["big3"], 32)
            nc.scalar.activation(l3_down2[0], l3_down, ACT.Copy).then_inc(s["w3h"], 1)
            with act.Fori(0, NCH) as tc:
                moe_act(act, L3, tc)

        @block.vector
        def _(dve):
            ch = Chain(dve, s["chain1"])
            dve.wait_ge(s["cond"], 16)
            ch.link(nc.vector.tensor_copy(cond_f[:, :], cond_i[:, :]))
            dve.wait_ge(s["late"], 16)
            nc.vector.tensor_scalar(cond_x[:, :], cond_f[:, :], float(S), C["rowt"], ALU.mult, ALU.add)\
                .then_inc(s["condx"], 1)

            dve.wait_ge(s["ints"], 32)
            dve.wait_ge(s["first"], 16)
            kv, off0, hi, slot0 = (kv_f[:, j, :] for j in range(4))
            ch.link(nc.vector.tensor_copy(kv, kv_i[:, :]))
            ch.link(nc.vector.tensor_scalar(off0, kv, 1.0 / BLOCK, -0.5 + 0.5 / BLOCK, ALU.mult, ALU.add))
            ch.link(nc.vector.tensor_scalar(hi, off0, MAGIC, None, ALU.add))
            ch.link(nc.vector.tensor_scalar(slot0, hi, MAGIC, None, ALU.subtract))
            ch.link(nc.vector.scalar_tensor_tensor(off0, slot0, -float(BLOCK), kv, ALU.mult, ALU.add))
            ang, turns, fold, wrap = (ycur[:, j // 2, (j % 2) * 256:(j % 2 + 1) * 256] for j in range(4))
            pos = kv_f[:, 2, 0:NT]
            ch.link(nc.vector.tensor_scalar(pos, kv[:, 0:NT], C["rowt"], None, ALU.add))
            ch.link(nc.vector.tensor_tensor(ang.rearrange("p (i f) -> p i f", i=NT),
                                            pos.unsqueeze(2).broadcast_to([P, NT, HD // 2]),
                                            F["inv"].unsqueeze(1).broadcast_to([P, NT, HD // 2]), ALU.mult))
            ch.link(nc.vector.tensor_scalar(turns, ang, float(1 / (2 * np.pi)), None, ALU.mult))
            ch.link(nc.vector.tensor_scalar(turns, turns, MAGIC, None, ALU.add))
            ch.link(nc.vector.tensor_scalar(turns, turns, MAGIC, None, ALU.subtract))
            ch.link(nc.vector.scalar_tensor_tensor(fold, turns, -TWO_PI_HI, ang, ALU.mult, ALU.add))
            ch.link(nc.vector.scalar_tensor_tensor(ang, turns, -TWO_PI_LO, fold, ALU.mult, ALU.add))
            edge = 3.1415925
            sin_f = sinb[:].rearrange("p i f -> p (i f)")
            cos_f = cosb[:].rearrange("p i f -> p (i f)")
            ch.link(nc.vector.tensor_scalar(sin_f, ang, edge, -edge, ALU.min, ALU.max))
            ch.link(nc.vector.tensor_scalar(wrap, ang, float(np.pi / 2), -float(2 * np.pi), ALU.is_gt, ALU.mult))
            ch.link(nc.vector.scalar_tensor_tensor(fold, ang, float(np.pi / 2), wrap, ALU.add, ALU.add))
            nc.vector.tensor_scalar(cos_f, fold, edge, -edge, ALU.min, ALU.max).then_inc(s["folds"], 1)

            slots, tab = ix[0:B, 0:WB], ix[0:B, 16:16 + WB]
            ch.link(nc.vector.tensor_copy(bt_f[0:B, :], bt_i[0:B, :]))
            ch.link(nc.vector.tensor_scalar(slots, F["win"][0:B, :], slot0[0:B, NT:NT + 1], 0.0, ALU.add, ALU.max))
            ch.link(nc.vector.tensor_scalar(slots, slots, float(NBLK - 1), None, ALU.min))
            for i in range(WB):
                ch.link(nc.vector.scalar_tensor_tensor(cmpt[0:B, i * NBLK:(i + 1) * NBLK], F["slots"][0:B, :],
                                                       slots[:, i:i + 1], bt_f[0:B, :], ALU.is_equal, ALU.mult,
                                                       accum_out=tab[:, i:i + 1]))
            i0 = WINDOW // BLOCK
            segf = ix[:, 32:34]
            nc.vector.tensor_copy(segf[0:B, 0:1], tab[:, i0:i0 + 1]).then_inc(s["tabst"], 1)
            nc.vector.tensor_copy(segf[B:P, 0:1], tab[:, i0 + 1:i0 + 2])
            ch.link(nc.vector.tensor_copy(segf[0:B, 1:2], tab[:, i0 + 2:i0 + 3]))
            nc.vector.tensor_copy(seg_i[:, 0:1], segf[:, 0:1])
            nc.vector.tensor_copy(seg_i[0:B, 1:2], segf[0:B, 1:2]).then_inc(s["condidx"], 1)
            idB = ident[0:B, 0:B]
            ch.link(nc.vector.tensor_tensor(diag4[0:B, 0:NEWB, :], idB.unsqueeze(1).broadcast_to([B, NEWB, B]),
                                            tab[:, i0:i0 + NEWB].unsqueeze(2).broadcast_to([B, NEWB, B]), ALU.mult))
            nc.vector.tensor_scalar(diag4[0:B, NEWB, :], idB, off0[0:B, NT:NT + 1], None, ALU.mult)\
                .then_inc(s["rowps"], 1)
            dve.wait_ge(s["wrows"], 16 * NT)
            dve.wait_ge(s["wzero"], 1)
            for q in range(BPT):
                r = slice(q * S, (q + 1) * S)
                last = nc.vector.tensor_copy(wdiag[r, :, r], wrows[r, :, :])
            last.then_inc(s["wdiag"], 1)
            dve.wait_ge(s["rowsb"], 1)
            ch.link(nc.vector.tensor_copy(rowinfo, ps[:, 7, 0:256]))
            nc.vector.sem_inc(s["rowused"], 1)
            dve.wait_ge(s["w2"], 16)
            for step, (src, dst) in enumerate(((l0_down, w2mix), (w2mix, l0_down), (l0_down, w2mix))):
                r = 4 >> step
                si, di = (z.rearrange("p (a h r) n -> p a h (r n)", h=2, r=r) for z in (src, dst))
                nc.vector.tensor_tensor(di[:, :, 0, :], si[:, :, 0, :], si[:, :, 1, :], ALU.add)
                last = nc.vector.tensor_tensor(di[:, :, 1, :], si[:, :, 0, :], si[:, :, 1, :], ALU.subtract)
                if step < 2:
                    ch.link(last)
            last.then_inc(s["mix"], 1)
            segblk, offrow = rowinfo[:, 0:SEGS], rowinfo[:, SEGS:SEGS + B]
            v = seen.rearrange("p (o j b) -> p o j b", o=BLOCK, j=NEWB)
            prio = F["prio"].rearrange("p (j b) -> p j b", j=NEWB)

            def over_o(x):
                return x.unsqueeze(1).broadcast_to([P, BLOCK, B])

            offs = F["off"].unsqueeze(2).broadcast_to([P, BLOCK, B])
            ch.link(nc.vector.tensor_copy(v[:, :, 1, :], over_o(prio[:, 1, :])))
            ch.link(nc.vector.tensor_tensor(v[:, :, 0, :], over_o(offrow), offs, ALU.is_le))
            ch.link(nc.vector.tensor_tensor(v[:, :, 2, :], over_o(offrow), offs, ALU.is_gt))
            ch.link(nc.vector.tensor_tensor(v[:, :, 0, :], v[:, :, 0, :], over_o(prio[:, 0, :]), ALU.mult))
            ch.link(nc.vector.tensor_tensor(v[:, :, 2, :], v[:, :, 2, :], over_o(prio[:, 2, :]), ALU.mult))
            for g in range(1, 8, 2):
                dve.wait_ge(s["y0"], g + 1)
                nc.vector.tensor_copy(yT[:, g % 2, (g // 2) * CH:(g // 2 + 1) * CH], ps[:, g, :])\
                    .then_inc(s["y0s"], 1)
            win, last_seg, col = ix[:, 40:56], ix[:, 56:57], ix[:, 57:58]
            for st, rows in enumerate((P, B)):
                ch.link(nc.vector.tensor_scalar(eqt[0:rows, :], segblk[0:rows, :], segf[0:rows, st:st + 1], None,
                                                ALU.is_equal))
                ch.link(nc.vector.tensor_tensor(cmpt[0:rows, :].rearrange("p (o n) -> p o n", o=BLOCK),
                                                seen[0:rows, :].rearrange("p (o n) -> p o n", o=BLOCK),
                                                eqt[0:rows, :].unsqueeze(1).broadcast_to([rows, BLOCK, SEGS]),
                                                ALU.mult))
                ch.link(nc.vector.tensor_reduce(win[0:rows, :], cmpt[0:rows, :].rearrange("p (o n) -> p o n", o=BLOCK),
                                                X, ALU.max))
                ch.link(nc.vector.tensor_tensor(cmpt[0:rows, 0:SEGS], eqt[0:rows, :], F["segid"][0:rows, :], ALU.mult))
                ch.link(nc.vector.tensor_reduce(last_seg[0:rows, :], cmpt[0:rows, 0:SEGS], X, ALU.max))
                ch.link(nc.vector.tensor_scalar(col[0:rows, :], last_seg[0:rows, :], float(BLOCK), -BLOCK - FAR,
                                                ALU.mult, ALU.add))
                ch.link(nc.vector.tensor_scalar(eqt[0:rows, 0:BLOCK], F["off"][0:rows, :], col[0:rows, :], None,
                                                ALU.add))
                ch.link(nc.vector.scalar_tensor_tensor(cmpt[0:rows, 0:BLOCK], win[0:rows, :],
                                                       F["myprio"][0:rows, st:st + 1], eqt[0:rows, 0:BLOCK],
                                                       ALU.is_equal, ALU.mult))
                ch.link(nc.vector.tensor_scalar(dest[0:rows, st * BLOCK:(st + 1) * BLOCK], cmpt[0:rows, 0:BLOCK], FAR,
                                                None, ALU.add))
            nc.vector.tensor_copy(ix[:, 58:59], ix[:, 56:57]).then_inc(s["destst"], 1)
            dve.wait_ge(s["w0h"], 1)
            nc.vector.tensor_tensor(l0_low, early[:, 0:4096], l0_high, ALU.subtract).then_inc(s["w0l"], 1)
            dve.wait_ge(s["down0"], 1)
            nc.vector.tensor_tensor(l0_down2[1], ps[:, 0:4, :].rearrange("p c (m n) -> p (c m) n", n=D), l0_down2[0],
                                    ALU.subtract).then_inc(s["w0l"], 1)
            dve.wait_ge(s["tabld"], 32)
            WR = BPT * WB
            nc.vector.tensor_copy(win_i[:, :], blkw[:, :])
            wide = cmpt[0:WR, :].rearrange("p (g n) -> p g n", g=NT)
            ch.link(nc.vector.tensor_tensor(wide, segblk[0:WR, :].unsqueeze(1).broadcast_to([WR, NT, SEGS]),
                                            blkw[:, :].unsqueeze(2).broadcast_to([WR, NT, SEGS]), ALU.is_equal))
            ch.link(nc.vector.tensor_tensor(wide, wide, F["segid"][0:WR, :].unsqueeze(1).broadcast_to([WR, NT, SEGS]),
                                            ALU.mult))
            ch.link(nc.vector.tensor_reduce(ix[0:WR, 0:NT], wide, X, ALU.max))
            ch.link(nc.vector.tensor_scalar(ix[0:WR, 16:32], ix[0:WR, 0:NT], 0.0, FAR, ALU.is_equal, ALU.mult))
            ch.link(nc.vector.scalar_tensor_tensor(new_i[:, :], ix[0:WR, 0:NT], -1.0, ix[0:WR, 16:32], ALU.add,
                                                   ALU.add))
            dve.wait_ge(s["destld"], 16 * (NEWB + 1))
            toks = cmpt[0:B, 0:S * NEWB * BLOCK].rearrange("p (t u) -> p t u", t=S)
            ch.link(nc.vector.scalar_tensor_tensor(
                toks, F["shift"][0:B, :].rearrange("p (t u) -> p t u", t=S), off0[0:B, NT:NT + 1],
                rest[0:B, 4402:4450].unsqueeze(1).broadcast_to([B, S, NEWB * BLOCK]), ALU.is_equal, ALU.mult))
            ch.link(nc.vector.tensor_reduce(eqt[0:B, 0:S], toks, X, ALU.add))
            nc.vector.tensor_copy(rest[0:B, 4450:4482].bitcast(I32), eqt[0:B, 0:S]).then_inc(s["tokst"], 1)
            dve.wait_ge(s["small1"], 80)
            ch.link(nc.vector.tensor_copy(adapt_f, adapt_i))
            for li in range(2):
                ch.link(nc.vector.tensor_scalar(amask[:, li, :], adapt_f[:, li, :], adapt_s[:, 2 * li + 1:2 * li + 2],
                                                adapt_s[:, 2 * li:2 * li + 1], ALU.is_equal, ALU.mult))

            dve.wait_ge(s["x"], 16)
            with dve.Fori(0, NCH) as tc:
                dve.wait_ge(s["ycur_ready"], tc + 1)
                nc.vector.tensor_tensor(ylow1, yT[:, :, bass.ds(tc * CH, CH)], yhigh, ALU.subtract).then_inc(s["ylow_ready"], 1)
                for m in range(M0):
                    dve.wait_ge(s["silu_ready"], tc * M0 + (m + 1))
                    nc.vector.tensor_tensor(silu[:, m % SLOTS, :], silu[:, m % SLOTS, :], ps[:, 2 + m % 2, :], ALU.mult)\
                        .then_inc(s["hfull_ready"], 1)
                    dve_low(dve, m, P, tc * M0)
                dve_residual(dve, tc, 0)
            router = small1[:, :, D + P:]
            high, low = (x[:, 0:KD * E1].rearrange("p (k e) -> p k e", k=KD) for x in (routerh, routerl))
            ch.link(nc.vector.tensor_copy(high, router))
            nc.vector.tensor_tensor(low, router, high, ALU.subtract).then_inc(s["w1l"], 1)
            for k in range(KD):
                dve.wait_ge(s["w1h"], 2 * k + 1)
                nc.vector.tensor_tensor(l1_gatel[:, k, :], l1_gate[:, k, :], l1_gateh[:, k, :],
                                        ALU.subtract).then_inc(s["w1l"], 1)
                dve.wait_ge(s["w1h"], 2 * k + 2)
                nc.vector.tensor_tensor(l1_upl[:, k, :], l1_up[:, k, :], l1_uph[k],
                                        ALU.subtract).then_inc(s["w1l"], 1)
            with dve.Fori(0, NCH) as tc:
                moe_dve(dve, L1, 0, tc, s["stdlinks"])
                dve_residual(dve, tc, L1.acc0)

            dve.wait_ge(s["trig"], 1)
            dve.wait_ge(s["small2"], 80)
            nc.vector.tensor_scalar(gain[:, :], gain[:, :], 1.0, None, ALU.add).then_inc(s["gained"], 1)
            dve.wait_ge(s["gained"], 1)
            NH = G * GS + G

            dve.wait_ge(s["keys"], 16)
            keynum, keyless = (early[:, 7168 + j * WK:7168 + (j + 1) * WK] for j in range(2))
            hi, least = kv_f[:, 2, :], kv_f[:, 3, :]
            ch.link(nc.vector.tensor_scalar(hi, off0, float(WINDOW), None, ALU.add))
            ch.link(nc.vector.tensor_tensor(least, hi, kv, ALU.subtract))

            def per_tile(x):
                return x[:, 0:NT].unsqueeze(2).broadcast_to([P, NT, WK])

            def per_key(x):
                return x.unsqueeze(1).broadcast_to([P, NT, WK])

            ma = early[:, 0:NT * WK].rearrange("p (i c) -> p i c", i=NT)
            mb = early[:, ROW:ROW + NT * WK].rearrange("p (i c) -> p i c", i=NT)
            ch.link(nc.vector.tensor_tensor(ma, per_key(keyless), per_tile(off0), ALU.is_gt))
            ch.link(nc.vector.tensor_tensor(mb, per_key(keyless), per_tile(hi), ALU.is_le))
            ch.link(nc.vector.tensor_tensor(ma, ma, mb, ALU.mult))
            ch.link(nc.vector.tensor_tensor(mb, per_key(keynum), per_tile(least), ALU.is_ge))
            ch.link(nc.vector.tensor_tensor(ma, ma, mb, ALU.mult))
            nc.vector.tensor_scalar(maskb[:, :], early[:, 0:NT * WK], -MASKED, MASKED, ALU.mult, ALU.add)\
                .then_inc(s["masked"], 1)

            with dve.Fori(0, NCH) as tc:
                ch = Chain(dve, s["qklinks"], tc * 7)
                dve.wait_ge(s["squared"], tc + 1)
                ch.link(nc.vector.tensor_reduce(kcol[:, 0, :], sqr.rearrange("p (h d) -> p h d", d=HD), X, ALU.add))
                nc.vector.tensor_scalar(kcol[:, 1, :], kcol[:, 0, :], 1.0 / HD, EPS, ALU.mult, ALU.add)\
                    .then_inc(s["ssq_ready"], 1)
                dve.wait_ge(s["root_ready"], tc + 1)
                ch.link(nc.vector.reciprocal(kcol[:, 1, :], kcol[:, 0, :]))
                qk4 = qkn.rearrange("p (t h d) -> p t h d", t=TPC, d=HD)
                for t in range(TPC):
                    last = nc.vector.tensor_tensor(
                        qk4[:, t, :, :], ps[:, t, 0:384].rearrange("p (h d) -> p h d", d=HD),
                        kcol[:, 1, t * NH:(t + 1) * NH].unsqueeze(2).broadcast_to([P, NH, HD]), ALU.mult)
                ch.link(last)
                qk3 = qkn.rearrange("p (t n) -> p t n", t=TPC)
                ch.link(nc.vector.tensor_tensor(qk3, qk3, gain[:, :].unsqueeze(1).broadcast_to([P, TPC, NH * HD]),
                                                ALU.mult))

                def trig(table):
                    return table[:, bass.ds(tc * TPC, TPC), :].unsqueeze(2).broadcast_to([P, TPC, NH, HD // 2])

                def temp(x):
                    return x.rearrange("p (t h d) -> p t h d", t=TPC, d=HD // 2)

                low, high = qk4[:, :, :, 0:HD // 2], qk4[:, :, :, HD // 2:HD]
                tmp = [temp(sqr[:, 0:768]), temp(sqr[:, 768:1536]), temp(work[:, 0:768]), temp(work[:, 1024:1792])]
                nc.vector.tensor_tensor(tmp[0], low, trig(cosb), ALU.mult)
                nc.vector.tensor_tensor(tmp[1], high, trig(sinb), ALU.mult)
                nc.vector.tensor_tensor(tmp[2], high, trig(cosb), ALU.mult)
                ch.link(nc.vector.tensor_tensor(tmp[3], low, trig(sinb), ALU.mult))
                k4 = kvrow[:, :, 0:KW].rearrange("p t (g d) -> p t g d", g=G)
                nq = G * GS
                nc.vector.tensor_tensor(low[:, :, 0:nq, :], tmp[0][:, :, 0:nq, :], tmp[1][:, :, 0:nq, :], ALU.subtract)
                nc.vector.tensor_tensor(high[:, :, 0:nq, :], tmp[2][:, :, 0:nq, :], tmp[3][:, :, 0:nq, :], ALU.add)
                ch.link(nc.vector.tensor_tensor(k4[:, :, :, 0:HD // 2], tmp[0][:, :, nq:, :], tmp[1][:, :, nq:, :],
                                                ALU.subtract))
                ch.link(nc.vector.tensor_tensor(k4[:, :, :, HD // 2:], tmp[2][:, :, nq:, :], tmp[3][:, :, nq:, :],
                                                ALU.add))
                nc.vector.tensor_copy(kcol[:, 0, 0:1], kcol[:, 1, 0:1]).then_inc(s["roped"], 1)
                assert ch.n == 7

            def block_diagonals(tc, n):
                if n >= 4:
                    dve.wait_ge(s["s_ps"], tc * BPC + (n - 2))
                q = Qbd[:, (n // 2) % 2, :, :].rearrange("p b (g h t) -> p b g h t", g=G, h=GS)
                for g in range(G):
                    rows = slice(g * HD, (g + 1) * HD)
                    src = qT[rows, :, bass.ds(tc * CH + n * S, 2 * S)].rearrange("p h (b t) -> p b h t", b=2)
                    last = nc.vector.tensor_copy(q[rows, :, g, :, :], src)
                last.then_inc(s["qbd_ready"], 2)

            def normalise(tc, n):
                dve.wait_ge(s["rr_ready"], tc * BPC + (n + 1))
                for h in range(2):
                    last = nc.vector.tensor_scalar(Pn[:, n % 2, h, :], Pex[:, n % 2, h, :],
                                                   acol[:, 3, n % 2, h:h + 1], None, ALU.mult)
                last.then_inc(s["pn_ready"], 1)

            def maxima(tc, n):
                dve.wait_ge(s["s_ps"], tc * BPC + (n + 1))
                nc.vector.tensor_reduce(acol[:, 0, n % 2, :],
                                        ps[:, 2 + n % 2, 0:2 * WK].rearrange("p (h c) -> p h c", h=2), X, ALU.max)\
                    .then_inc(s["mlinks"], 1)
                dve.wait_ge(s["mlinks"], tc * BPC + (n + 1))
                nc.vector.tensor_scalar(acol[:, 1, n % 2, :], acol[:, 0, n % 2, :], -SC, None, ALU.mult)\
                    .then_inc(s["nb_ready"], 1)

            def sums(tc, n):
                dve.wait_ge(s["p_ready"], tc * BPC + (n + 1))
                nc.vector.reciprocal(acol[:, 3, n % 2, :], acol[:, 2, n % 2, :]).then_inc(s["rr_ready"], 1)

            def values_out(tc, n):
                dve.wait_ge(s["o_ps"], tc * BPC + (O_CREDIT + n + 1))
                nc.vector.tensor_copy(oT[:, :, n * S:(n + 1) * S],
                                      ps[:, 6 + n % 2, 0:GS * S].rearrange("p (h t) -> p h t", h=GS))\
                    .then_inc(s["o_sb"], 1)

            dve.wait_ge(s["qzero"], 1)
            with dve.Fori(0, NCH) as tc:
                block_diagonals(tc, 0)
                for n in range(1, BPC + 3):
                    if n <= BPC:
                        maxima(tc, n - 1)
                    if n >= 3:
                        values_out(tc, n - 3)
                    if n % 2 == 1 and n + 1 < BPC:
                        block_diagonals(tc, n + 1)
                    if n <= BPC:
                        sums(tc, n - 1)
                        normalise(tc, n - 1)
                ch = Chain(dve, s["chain2"], tc * TAIL_LINKS)
                dve.wait_ge(s["ytok_sb"], tc + 1)
                ch.link(nc.vector.tensor_tensor(ywr, ytok, wr[:, :].unsqueeze(1).broadcast_to([P, TPC, D]), ALU.mult))
                ch.link(nc.vector.tensor_reduce(lcol[:, 0, :], ywr, X, ALU.add))
                ch.link(nc.vector.tensor_scalar(lcol[:, 1, :], lcol[:, 0, :], br[:, 0:1], None, ALU.add))

                def r3(x):
                    return x[:, 0:P].rearrange("p (t e) -> p t e", t=TPC)

                def const(x):
                    return x.unsqueeze(1).broadcast_to([P, TPC, S])

                def over(x, n=S):
                    return x.unsqueeze(2).broadcast_to([P, TPC, n])

                nc.vector.tensor_tensor(r3(rt[0]), const(C["own"]), over(lcol[:, 1, :]), ALU.mult)\
                    .then_inc(s["ldiag_ready"], 1)
                dve.wait_ge(s["lrow_ps"], tc + 1)
                nc.vector.sem_inc(s["passed"], 1)
                lrow = ps[:, 2, 0:P]
                for t in range(TPC):
                    nc.vector.max(top8[:, t, :], lrow[:, t * S:(t + 1) * S])
                ch.link(nc.vector.tensor_tensor(r3(rt[1]), r3(lrow), const(C["own"]), ALU.mult))
                ch.link(nc.vector.tensor_reduce(lcol[:, 2, :], r3(rt[1]), X, ALU.add))
                nc.vector.tensor_tensor(lex[:, :, 0:SEL], top8[:, :, 0:SEL],
                                        top8[:, :, 0:1].broadcast_to([P, TPC, SEL]), ALU.subtract)
                nc.vector.tensor_tensor(lex[:, :, SEL:SEL + 1], lcol[:, 2, :].unsqueeze(2), top8[:, :, 0:1],
                                        ALU.subtract).then_inc(s["lex_ready"], 1)
                ch.link(nc.vector.tensor_tensor(r3(rt[2]), r3(lrow), over(lcol[:, 2, :]), ALU.is_gt))
                ch.link(nc.vector.tensor_tensor(r3(rt[3]), r3(lrow), over(lcol[:, 2, :]), ALU.is_equal))
                ch.link(nc.vector.tensor_tensor(r3(rt[4]), r3(rt[3]), const(C["before"]), ALU.mult))
                ch.link(nc.vector.tensor_tensor(r3(rt[3]), r3(rt[4]), r3(rt[2]), ALU.add))
                ch.link(nc.vector.tensor_reduce(lcol[:, 3, :], r3(rt[3]), X, ALU.add))
                NP = TPC * BPT * SEL
                pk = pick[:, :, :]
                rank3 = C["rank"].unsqueeze(1).broadcast_to([P, TPC, NP])
                place3 = C["place"].rearrange("p (t n) -> p t n", t=TPC)
                ch.link(nc.vector.tensor_tensor(pickw, rank3, over(lcol[:, 3, :], NP), ALU.is_equal))
                ch.link(nc.vector.tensor_tensor(pk, pickw, place3, ALU.mult))
                dve.wait_ge(s["lexe_ready"], tc + 1)
                ch.link(nc.vector.tensor_reduce(lcol[:, 4, :], lexe[:, :, 0:SEL], X, ALU.add))
                ch.link(nc.vector.reciprocal(lcol[:, 5, :], lcol[:, 4, :]))
                ch.link(nc.vector.tensor_tensor(lcol[:, 6, :], lcol[:, 5, :], lexe[:, :, SEL], ALU.mult))
                ch.link(nc.vector.tensor_tensor(pickw, pk, over(lcol[:, 6, :], NP), ALU.mult))
                ch.link(nc.vector.tensor_copy(lcol[:, 7, :], lcol[:, 6, :]))
                nc.vector.tensor_copy(lcol[:, 7, :], lcol[:, 6, :]).then_inc(s["pick_ready"], 1)
                assert ch.n == TAIL_LINKS, ch.n
                dve_residual(dve, tc, 2 * NCH)

            router = small3[:, :, D:]
            high, low = (x[:, 0:KD * L3.RW].rearrange("p (k e) -> p k e", k=KD) for x in (routerh, routerl))
            nc.vector.tensor_copy(high, router).then_inc(s["routed3"], 1)
            dve.wait_ge(s["routed3"], 1)
            nc.vector.tensor_tensor(low, router, high, ALU.subtract).then_inc(s["w3l"], 1)
            split = [x for k in range(KD) for x in ((l3_gatel[:, k, :], l3_gate[:, k, :], l3_gateh[:, k, :]),
                                                    (l3_upl[:, k, :], l3_up[:, k, :], l3_uph[:, k, :]))]
            for i, (low, full, high) in enumerate(split + [(l3_down2[1], l3_down, l3_down2[0])]):
                dve.wait_ge(s["w3h"], i + 1)
                nc.vector.tensor_tensor(low, full, high, ALU.subtract).then_inc(s["w3l"], 1)
            with dve.Fori(0, NCH) as tc:
                moe_dve(dve, L3, 1, tc, s["chain3"])
                dve_residual(dve, tc, L3.acc0)

        @block.tensor
        def _(pe):
            nc.tensor.sem_inc(s["o_ps"], O_CREDIT)
            pe.wait_ge(s["rowps"], 1)
            nc.tensor.matmul(ps[:, 7, 0:256], C["ones"][0:B, :], diag4[0:B, :, :], start=True, stop=True)\
                .then_inc(s["rowsb"], 1)
            pe.wait_ge(s["rowused"], 1)
            pe.wait_ge(s["xrows"], 16)
            pe.wait_ge(s["wdiag"], 1)
            for c in range(NCH):
                for d in range(KD):
                    for t in range(TPC):
                        i = c * TPC + t
                        last = nc.tensor.matmul(ps[:, 2 * c + d, t * P:(t + 1) * P],
                                                xrows[:, i, d * P:(d + 1) * P], wdiag[:, i, :], start=True, stop=True)
                    last.then_inc(s["y0"], 1)
            pe.wait_ge(s["mix"], 1)
            pe.wait_ge(s["y0s"], 8)
            for c in range(4):
                last = nc.tensor.matmul(ps[:, c, :], C["had"], w2mix[:, 2 * c:2 * c + 2, :], start=True, stop=True)
            last.then_inc(s["had"], 1)
            pe.wait_ge(s["w0l"], 2)
            nc.tensor.sem_inc(s["gu_done"], 1)
            with pe.Fori(0, NCH) as tc:
                pe.wait_ge(s["ylow_ready"], tc + 1)
                for m in range(M0):
                    if m >= 2:
                        pe.wait_ge(s["hfull_ready"], tc * M0 + (m - 1))
                    pe_gate_up(m, P, *parts0)
                    if m == M0 - 1:
                        nc.tensor.sem_inc(s["gu_done"], 1)
                    if m >= 2:
                        pe_down(pe, m - 2, P, l0_down2, True, tc * M0, M0 - 1)
                for m in (M0 - 2, M0 - 1):
                    pe_down(pe, m, P, l0_down2, True, tc * M0, M0 - 1)
                pe.wait_ge(s["acc_used"], tc + 1)
            pe.wait_ge(s["small1"], 80)
            pe.wait_ge(s["castb"], 48)
            pe.wait_ge(s["down1"], 16)
            pe.wait_ge(s["w1l"], 1 + 2 * KD)
            with pe.Fori(0, NCH) as tc:
                moe_pe(pe, L1, tc, small1[:, :, 0:D], small1[:, :, D:D + P], b1s,
                       [(l1_gateh[:, k, :], l1_gatel[:, k, :]) for k in range(KD)],
                       [(l1_uph[k], l1_upl[:, k, :]) for k in range(KD)], l1_down)
            pe.wait_ge(s["wqkv"], 16)
            with pe.Fori(0, NCH) as tc:
                pe.wait_ge(s["xs_ready"], tc + 1)
                for t in range(TPC):
                    for k in range(KD):
                        last = nc.tensor.matmul(ps[:, t, :], ycur[:, k, t * P:(t + 1) * P], wqkv[:, k, :],
                                                start=(k == 0), stop=(k == KD - 1))
                last.then_inc(s["qkv_ready"], 1)
                pe.wait_ge(s["roped"], tc + 1)
                pe.wait_ge(s["v_ready"], tc + 1)
                for t in range(TPC):
                    for h in range(GS):
                        last = nc.tensor.transpose(ps[:, 4 + h, t * P:(t + 1) * P],
                                                   qkn.rearrange("p (t n) -> p t n", t=TPC)[:, t, h * P:(h + 1) * P],
                                                   ident)
                last.then_inc(s["qps_ready"], 1)
            pe.wait_ge(s["qsb_ready"], NCH)
            pe.wait_ge(s["l2w"], 16)
            pe.wait_ge(s["masked"], 1)

            def keys(tc, n):
                t, q = n // BPT, n % BPT
                if q == 0:
                    pe.wait_ge(s["shuf0" if t % 2 == 0 else "shuf1"], (tc * 2 + t // 2 + 1) * (16 * 2 * BPT))
                nc.tensor.transpose(ps[:, n % 2, 0:96], kv2[t][0:96, 0, q, 0:KW], ident[0:96, 0:96])
                nc.tensor.transpose(ps[:, n % 2, 96:WK], kv2[t][0:80, 1, q, 0:KW], ident[0:80, 0:80])\
                    .then_inc(s["kt_ps"], 1)

            def scores(tc, n):
                pe.wait_ge(s["kt_sb"], tc * BPC + (n + 1))
                pe.wait_ge(s["qbd_ready"], tc * BPC + (n + 1))
                for h in range(2):
                    out = ps[:, 2 + n % 2, h * WK:(h + 1) * WK]
                    nc.tensor.matmul(out, Qbd[:, (n // 2) % 2, n % 2, h * P:(h + 1) * P], KTs[:, n % 2, :], start=True, stop=False)
                    last = nc.tensor.matmul(out, tselb[:, n % BPT, :],
                                            maskb[:, bass.ds(tc * (TPC * WK) + (n // BPT) * WK, WK)],
                                            start=False, stop=True)
                last.then_inc(s["s_ps"], 1)

            def probs(tc, n):
                pe.wait_ge(s["pn_ready"], tc * BPC + (n + 1))
                bank = ps[:, 4 + n % 2, :]
                for h in range(2):
                    nc.tensor.transpose(bank[0:96, h * P:(h + 1) * P], Pn[:, n % 2, h, 0:96], ident)
                for h in range(2):
                    last = nc.tensor.transpose(bank[0:80, 256 + h * P:256 + (h + 1) * P], Pn[:, n % 2, h, 96:WK],
                                               ident)
                last.then_inc(s["pt_ps"], 1)

            def values(tc, n):
                t, q = n // BPT, n % BPT
                pe.wait_ge(s["pt_sb"], tc * BPC + (n + 1))
                if n >= 2:
                    pe.wait_ge(s["o_sb"], tc * BPC + (n - 1))
                for g in range(G):
                    for h, r in ((0, 96), (1, 80)):
                        last = nc.tensor.matmul(ps[g * HD:(g + 1) * HD, 6 + n % 2, 0:GS * S],
                                                kv2[t][0:r, h, q, KW + g * HD:KW + (g + 1) * HD],
                                                PTs[0:r, n % 2, h, g * GS * S:(g + 1) * GS * S],
                                                start=(h == 0), stop=(h == 1))
                last.then_inc(s["o_ps"], 1)

            with pe.Fori(0, NCH) as tc:
                for n in range(BPC + 3):
                    if n < BPC:
                        keys(tc, n)
                    if 1 <= n <= BPC:
                        scores(tc, n - 1)
                    if 2 <= n < BPC + 2:
                        probs(tc, n - 2)
                    if n >= 3:
                        values(tc, n - 3)
                pe.wait_ge(s["o_sb"], tc * BPC + BPC)
                for t in range(TPC):
                    for h in range(GS):
                        last = nc.tensor.matmul(ps[:, t // 2, (t % 2) * D:(t % 2 + 1) * D],
                                                oT[:, h, t * P:(t + 1) * P], wo[:, h, :],
                                                start=(h == 0), stop=(h == GS - 1))
                last.then_inc(s["ytok_ps"], 1)
                for d in range(KD):
                    for h in range(GS):
                        nc.tensor.matmul(ps[:, 6 + d, :], wo[:, h, d * P:(d + 1) * P], oT[:, h, :],
                                         start=(h == 0), stop=False)
                pe.wait_ge(s["ldiag_ready"], tc + 1)
                nc.tensor.matmul(ps[:, 2, 0:P], C["samebatch"], rt[0][:, 0:P], start=True, stop=True)\
                    .then_inc(s["lrow_ps"], 1)
                pe.wait_ge(s["pick_ready"], tc + 1)
                NP = TPC * BPT * SEL
                for d in range(KD):
                    for t in range(TPC):
                        last = nc.tensor.matmul(ps[:, 3, d * NP:(d + 1) * NP], ytok[:, t, d * P:(d + 1) * P],
                                                pick[:, t, :], start=(t == 0), stop=(t == TPC - 1))
                last.then_inc(s["fx_ps"], 1)
                for t in range(TPC):
                    last = nc.tensor.transpose(ps[0:NP, 4, t * P:(t + 1) * P], pickw[:, t, :], ident)
                last.then_inc(s["pwt_ps"], 1)
                pe.wait_ge(s["fx_sb"], tc + 1)
                for m in range(H2 // P):
                    for k in range(KD):
                        last = nc.tensor.matmul(ps[:, 5, m * NP:(m + 1) * NP], w21[:, k, m * P:(m + 1) * P],
                                                fx[:, k, :], start=(k == 0), stop=(k == KD - 1))
                last.then_inc(s["h_ps"], 1)
                pe.wait_ge(s["h_sb"], tc + 1)
                for m in range(H2 // P):
                    nc.tensor.matmul(ps[0:NP, 0, 0:D], hT2[:, m, :], w22[:, m, :], start=(m == 0), stop=False)
                nc.tensor.matmul(ps[0:NP, 0, 0:D], C["ones"][0:1, 0:NP], b22[0:1, :], start=False, stop=True)\
                    .then_inc(s["outl_ps"], 1)
                pe.wait_ge(s["outl_sb"], tc + 1)
                pe.wait_ge(s["pwt_sb"], tc + 1)
                for d in range(KD):
                    last = nc.tensor.matmul(ps[:, 6 + d, :], outl[0:NP, d * P:(d + 1) * P], pwT[0:NP, :],
                                            start=False, stop=True)
                last.then_inc(s["acc_ready"], 1)
                pe.wait_ge(s["acc_used"], tc + 2 * NCH + 1)

            pe.wait_ge(s["raw3"], 16)
            aT, wt, bn, wpT = raw3[:, :, 0:64], raw3[:, :, 64:320], raw3[:, :, 320:384], raw3[:, :, 384:640]
            for i in range(KD):
                for k in range(KD):
                    nc.tensor.matmul(ps[:, 0, i * 64:(i + 1) * 64], wt[:, k, i * P:(i + 1) * P], aT[:, k, :],
                                     start=(k == 0), stop=(k == KD - 1))
            for k in range(KD):
                last = nc.tensor.matmul(ps[0:64, 1, 0:D], bn[:, k, :], wpT[:, k, :], start=(k == 0),
                                        stop=(k == KD - 1))
            last.then_inc(s["fin_ready"], 1)
            pe.wait_ge(s["fint_sb"], 1)
            pe.wait_ge(s["w3l"], 2 + 2 * KD)
            pe.wait_ge(s["sel3"], 16)
            with pe.Fori(0, NCH) as tc:
                moe_pe(pe, L3, tc, small3[:, :, 0:D], awt, wpb,
                       [(l3_gateh[:, k, :], l3_gatel[:, k, :]) for k in range(KD)],
                       [(l3_uph[:, k, :], l3_upl[:, k, :]) for k in range(KD)], l3_down2)


def kernel(**inputs):
    import numpy as _np
    import concourse.bacc as _bacc
    from concourse import mybir as _mybir
    from concourse.bass_utils import run_bass_kernel_spmd as _run

    v = {k: _np.asarray(x) for k, x in inputs.items()}

    def fold(w):
        return w.reshape(KD, P, -1).transpose(1, 0, 2)

    def tokens(x):
        return _np.repeat(x, S).reshape(NT, P).T

    x = v["x"].reshape(T, D)
    qkv = _np.concatenate([v["L2_cond_Wq"].T.reshape(D, G, GS, HD).transpose(0, 2, 1, 3).reshape(D, -1),
                           v["L2_cond_Wk"].T, v["L2_cond_Wv"].T], axis=1)
    wo = v["L2_cond_Wo"].T.reshape(G, GS, HD, D).transpose(0, 2, 1, 3).reshape(P, GS, D)
    up1 = v["L1_ffn_gate_up_proj"].transpose(1, 0, 2)
    w1 = v["L3_ffn_w1"].transpose(2, 0, 1)
    gu = v["L3_ffn_shared_gate_up_w"].T
    down3 = _np.concatenate([v["L3_ffn_w2"].transpose(0, 2, 1).reshape(E3 * F3, D), v["L3_ffn_shared_down_w"].T,
                             _np.zeros((L3.M * P - N3, D), _np.float32)])
    scal1 = _np.repeat(v["L1_cond_scalings"], R)
    scal3 = _np.tile(_np.repeat(v["L3_cond_scaling"], R), 2)
    row = _np.arange(P) // R
    (_, late), (_, first), (_, cast) = constants()
    kvlen = v["itok_B_37_3939"]
    arrays = {
        "cond": tokens(v["itok_B_1_198"]),
        "kv": _np.concatenate([tokens(kvlen), _np.tile(kvlen, 2)[:, None]], axis=1),
        "tables": v["itok_Bx257_0_4111"],
        "adapt": _np.broadcast_to(_np.stack([v["itok_B_0_6"], v["itok_B_0_3"]])[None], (P, 2, B)),
        "adapt_s": _np.stack([scal1, row.astype(_np.float32), scal3, (row % 4).astype(_np.float32)], axis=1),
        "late": late, "first": first, "cast": cast,
        "xrows": x.reshape(NT, P, D).transpose(1, 0, 2),
        "xT": fold(x.T),
        "cond_w": v["L0_cond_weights"].reshape(-1, S),
        "w13": _np.concatenate([fold(v["L0_ffn_W1"].T).reshape(P, -1), fold(v["L0_ffn_W3"].T).reshape(P, -1)], 1),
        "w2": v["L0_ffn_W2"].T.reshape(M0, P, D).transpose(1, 0, 2),
        "small1": fold(_np.concatenate([v["L1_cond_W"].T, v["L1_cond_A"].reshape(P, D).T, v["L1_ffn_gate"]], 1)),
        "b1": v["L1_cond_Bm"].transpose(0, 2, 1).reshape(P, D),
        "gate1": fold(up1[:, :, :F1].reshape(D, N1)),
        "up1": fold(up1[:, :, F1:].reshape(D, N1)),
        "down1": v["L1_ffn_down_proj"].reshape(L1.M, P, D).transpose(1, 0, 2),
        "cache": _np.concatenate([v["L2_cond_k_blocks"].transpose(0, 2, 1, 3).reshape(NROWS, BLOCK, KW),
                                  v["L2_cond_v_blocks"].transpose(0, 2, 1, 3).reshape(NROWS, BLOCK, KW)],
                                 axis=2).reshape(NROWS, ROW),
        "l2w": _np.concatenate([fold(qkv).reshape(P, -1), wo.reshape(P, -1), fold(v["L2_ffn_W1"]).reshape(P, -1),
                                v["L2_ffn_W2"].reshape(H2 // P, P, D).transpose(1, 0, 2).reshape(P, -1)], axis=1),
        "gq": v["L2_cond_q_norm_scale"], "gk": v["L2_cond_k_norm_scale"],
        "wr": _np.broadcast_to(v["L2_ffn_Wr"].reshape(1, D), (P, D)),
        "b21": v["L2_ffn_b1"].reshape(H2 // P, P).T,
        "b22": v["L2_ffn_b2"].reshape(1, D),
        "br": _np.broadcast_to(v["L2_ffn_br"].reshape(1, 1), (P, 1)),
        "small3": fold(_np.concatenate([v["L3_cond_W_base"].T, v["L3_ffn_gate_w"].T, v["L3_ffn_shared_gate_w"].T,
                                     _np.zeros((D, L3.RW - L3.EW), _np.float32)], 1)),
        "raw3": fold(_np.concatenate([v["L3_cond_A"].reshape(64, D).T, v["L3_cond_Wt"],
                                      v["L3_cond_B_w"].transpose(1, 0, 2).reshape(D, 64), v["L3_cond_Wp"].T], 1)),
        "gu3": _np.concatenate([
            fold(_np.concatenate([w1[:, :, :F3].reshape(D, -1), gu[:, :FS]], axis=1)).reshape(P, -1),
            fold(_np.concatenate([w1[:, :, F3:].reshape(D, -1), gu[:, FS:]], axis=1)).reshape(P, -1)], axis=1),
        "down3": down3.reshape(L3.M, P, D).transpose(1, 0, 2),
    }
    arrays["gain"] = _np.broadcast_to(_np.concatenate([_np.tile(arrays.pop("gq"), G * GS),
                                                       _np.tile(arrays.pop("gk"), G)])[None], (P, 384))
    nc = _bacc.Bacc("TRN2", target_bir_lowering=False, num_devices=1)
    sent, a = {}, {}
    for name, x in arrays.items():
        x = _np.ascontiguousarray(x)
        sent[f"in_{name}"] = x
        a[name] = nc.dram_tensor(f"in_{name}", x.shape, _mybir.dt.from_np(x.dtype), kind="ExternalInput").ap()
    a["out"] = nc.dram_tensor("out_x", (P, KD, T), _mybir.dt.float32, kind="ExternalOutput").ap()
    build(nc, a)
    r = _run(nc, [sent], core_ids=[0])
    got = r.results[0]["out_x"]
    return got.transpose(1, 0, 2).reshape(D, T).T.reshape(B, S, D)
```

```python
from contextlib import ExitStack

import numpy as np

import concourse.bass as bass
from concourse import mybir

ALU = mybir.AluOpType
ACT = mybir.ActivationFunctionType
F32 = mybir.dt.float32
BF16 = mybir.dt.bfloat16
FR = mybir.dt.float32r
I32 = mybir.dt.int32
X = mybir.AxisListType.X

P = 128
B, S, D = 64, 32, 256
T = B * S
KD = D // P
NT = T // P
CH = 512
NCH = T // CH
TPC = CH // P
BPT, BPC = P // S, CH // S
H0 = 1024
E1, K1, F1 = 32, 4, 96
E3, K3, F3, FS = 8, 2, 176, 704
R = 16
G, GS, HD = 4, 2, 32
BLOCK, WINDOW, NBLK, NROWS = 16, 128, 257, 4112
WB = WINDOW // BLOCK + S // BLOCK + 1
WK = WB * BLOCK
NEWB = S // BLOCK + 1
SEGS = NEWB * B
ROW = BLOCK * 2 * G * HD
KW = G * HD
SEL = 4
H2 = 1024
EPS = 1e-6
FAR = float(2 ** 17)
MASKED = -1e30


def pieces(total):
    return [min(P, total - a) for a in range(0, total, P)]


class Moe:

    def __init__(self, experts, chosen, shared, rank, total, step0, chunk0, acc0, piece0, split_down, high0):
        self.E, self.K, self.Z = experts, chosen, rank
        self.EW = experts + shared
        self.RW = self.EW + self.EW % 2
        self.shared = shared
        self.total = total
        self.widths = pieces(total)
        self.M = len(self.widths)
        self.step0, self.chunk0, self.acc0, self.piece0 = step0, chunk0, acc0, piece0
        self.split_down, self.high0 = split_down, high0
        self.links = 16 if shared else 14


M0 = H0 // P
SLOTS = 3
L1 = Moe(E1, K1, 0, 8 * R, E1 * F1, NCH * M0, 0, NCH, 0, False, 0)
L3 = Moe(E3, K3, 1, 4 * R, E3 * F3 + FS, NCH * (M0 + L1.M), NCH, 3 * NCH, NCH * L1.M, True,
         NCH * M0)
N1, N3 = L1.total, L3.total
TAIL_LINKS = 17
O_CREDIT = 16
MAGIC = 1.5 * 2 ** 23
TWO_PI_HI = 6.28125
TWO_PI_LO = float(2 * np.pi - 6.28125)


def constants():
    p = np.arange(P)
    t = p % S
    had = np.array([[1.0]])
    while had.shape[0] < P:
        had = np.block([[had, had], [had, -had]])
    half = HD // 2
    inv = (np.float32(1.0) / (np.float32(10000.0) ** (np.arange(half, dtype=np.float32) / np.float32(half))))
    seg_j, seg_b = np.repeat(np.arange(NEWB), B), np.tile(np.arange(B), NEWB)
    c = np.arange(WK)
    sel_t, sel_b = np.repeat(np.arange(TPC), BPT * SEL), np.tile(np.repeat(np.arange(BPT), SEL), TPC)

    def rows(x):
        return np.broadcast_to(np.asarray(x, np.float32).reshape(1, -1), (P, np.size(x)))

    late = {
        "ident": np.eye(P),
        "had": had / 32.0,
        "restart32": rows((np.arange(TPC * E1) % E1) != 0),
        "restart8": rows((np.arange(TPC * E3) % E3) != 0),
        "samebatch": (p[:, None] // S) == (p[None, :] // S),
        "own": t[:, None] == np.arange(S)[None, :],
        "before": np.arange(S)[None, :] < t[:, None],
        "place": (sel_b[None, None, :] == (p // S)[:, None, None])
        & (sel_t[None, None, :] == np.arange(TPC)[None, :, None]),
        "rank": rows(np.tile(np.arange(SEL), TPC * BPT)),
        "rowt": t[:, None],
        "ones": np.ones((P, P)),
    }
    first = {
        "slots": rows(np.arange(NBLK)),
        "segid": rows(1 + np.arange(SEGS)),
        "prio": rows(seg_b * 4 + seg_j + 1),
        "off": rows(np.arange(BLOCK)),
        "win": rows(np.arange(WB) - WINDOW // BLOCK),
        "myprio": np.stack([(p % B) * 4 + p // B + 1, (p % B) * 4 + 3], axis=1),
        "shift": rows(np.arange(NEWB * BLOCK)[None, :] - np.arange(S)[:, None]),
        "key": rows(c),
        "keyless": c[None, :] - t[:, None],
        "inv": rows(inv),
    }

    def sels(L, owner):
        x = np.zeros((P, L.M * P), np.float32)
        for j in range(3):
            x[j * L.EW + owner, np.arange(L.total)] = 1
        return x

    tsel = np.stack([((p[:, None] // S) == q) & ((p[:, None] % S) == (p[None, :] % S)) for q in range(BPT)], 1)
    cast = {
        "identb": np.eye(P),
        "tselb": tsel,
        "sel1": sels(L1, np.arange(N1) // F1),
        "sel3": sels(L3, np.minimum(np.arange(N3) // F3, E3)),
    }

    def pack(d):
        at, out, o = {}, [], 0
        for name, x in d.items():
            x = np.asarray(x, np.float32).reshape(P, -1)
            at[name] = (o, x.shape[1])
            o += x.shape[1]
            out.append(x)
        return at, np.ascontiguousarray(np.concatenate(out, axis=1))

    return pack(late), pack(first), pack(cast)


class Chain:

    def __init__(self, eng, sem, base=0):
        self.eng, self.sem, self.base, self.n = eng, sem, base, 0

    def link(self, ins):
        self.n += 1
        ins.then_inc(self.sem, 1)
        self.eng.wait_ge(self.sem, self.base + self.n)


def build(nc, a):
    (late_at, _), (first_at, _), (cast_at, _) = constants()
    with ExitStack() as ctx:
        base = {}

        def sb(name, shape, dt=F32):
            base[name] = -(-nc.sbuf_base // 32) * 32
            return ctx.enter_context(nc.sbuf_tensor(name, shape, dt))

        def rounded(name, host, word, shape):
            assert word % 8 == 0
            return nc.alloc_sbuf_tensor_at(name, [P] + shape, FR, offset=base[host] + 4 * word).ap()

        def sem(name):
            return ctx.enter_context(nc.semaphore(name))

        ps = ctx.enter_context(nc.psum_tensor("ps", [P, 8, 512], F32))

        newblk = nc.dram_tensor("newblk", (SEGS, ROW), F32).ap()
        tab_d = nc.dram_tensor("tab_d", (B, WB), F32).ap()
        dest_d = nc.dram_tensor("dest_d", (B, NEWB * BLOCK), F32).ap()
        tok_d = nc.dram_tensor("tok_d", (B, S), I32).ap()

        xT = sb("xT", [P, KD, T])
        yT = sb("yT", [P, KD, T])
        qT = yT
        big = sb("big", [P, 2 * KD * N3 + L3.M * D])
        l1_gate = big[:, 0:KD * N1].rearrange("p (k n) -> p k n", k=KD)
        l1_up = big[:, KD * N1:2 * KD * N1].rearrange("p (k n) -> p k n", k=KD)
        l3_gate = big[:, 0:KD * N3].rearrange("p (k n) -> p k n", k=KD)
        l3_up = big[:, KD * N3:2 * KD * N3].rearrange("p (k n) -> p k n", k=KD)
        l3_down = big[:, 2 * KD * N3:].rearrange("p (m n) -> p m n", n=D)
        stage = big[:, 0:2 * ROW].rearrange("p (j n) -> p j n", j=2)
        rest = big[:, 2 * ROW:]
        early = sb("early", [P, 12288])
        l0_w1 = early[:, 0:2048].rearrange("p (k n) -> p k n", k=KD)
        l0_w3 = early[:, 2048:4096].rearrange("p (k n) -> p k n", k=KD)
        l0_down = early[:, 4096:6144].rearrange("p (m n) -> p m n", n=D)
        w2mix = early[:, 6144:8192].rearrange("p (c n) -> p c n", n=D)
        xrows = early[:, 8192:12288].rearrange("p (i n) -> p i n", n=D)
        l1_down = early[:, 6144:12288].rearrange("p (m n) -> p m n", n=D)
        kvw = early[:, 0:ROW].rearrange("p (o n) -> p o n", o=BLOCK)
        halves = [early[:, ROW:2 * ROW], big[:, 2 * KD * N3:2 * KD * N3 + ROW]]
        kv2 = [x[:, j * (ROW // 2):(j + 1) * (ROW // 2)].rearrange("p (h b n) -> p h b n", h=2, b=BPT)
               for x in halves for j in range(2)]
        scr = early[:, 2 * ROW:3 * ROW]
        qkvs = [scr, halves[1]]
        qkn = [x[:, 0:1536] for x in qkvs]
        sqr = [x[:, 1536:3072] for x in qkvs]
        kvrow = [x[:, 3072:4096].rearrange("p (t n) -> p t n", t=TPC) for x in qkvs]
        KTs = scr[:, 0:352].rearrange("p (s n) -> p s n", s=2)
        Pex = scr[:, 352:1056].rearrange("p (s h n) -> p s h n", s=2, h=2)
        PTs = scr[:, 1760:2784].rearrange("p (s h n) -> p s h n", s=2, h=2)
        Qbd = scr[:, 3072:4096].rearrange("p (s b n) -> p s b n", s=2, b=2)
        acol = scr[:, 2784:2800].rearrange("p (a s h) -> p a s h", a=4, s=2)
        mid = sb("mid", [P, 6144])
        F = {n: mid[:, 3072 + o:3072 + o + w] for n, (o, w) in first_at.items()}
        first_n = sum(w for _, w in first_at.values())
        assert 3072 + first_n <= 6144
        seen = mid[:, 0:3072]
        wqkv = mid[:, 0:1024].rearrange("p (k n) -> p k n", k=KD)
        wo = mid[:, 1024:1536].rearrange("p (g n) -> p g n", g=GS)
        w21 = mid[:, 1536:3584].rearrange("p (k n) -> p k n", k=KD)
        w22 = mid[:, 3584:5632].rearrange("p (m n) -> p m n", n=D)
        l0_high = rounded("l0_high", "early", 8192, [4096])
        l0_low = rounded("l0_low", "early", 0, [4096])
        parts0 = [[[x[:, (2 * i + k) * H0:(2 * i + k + 1) * H0] for x in (l0_high, l0_low)] for k in range(KD)]
                  for i in range(2)]
        l0_down2 = [rounded("l0_downh", "early", 4096, [M0, D]), rounded("l0_downl", "early", 6144, [M0, D])]
        l1_gateh, l1_gatel = rounded("l1_gateh", "early", 0, [KD, N1]), rounded("l1_gatel", "big", 0, [KD, N1])
        l1_uph = [rounded("l1_uph0", "yT", 0, [N1]), rounded("l1_uph1", "mid", 0, [N1])]
        l1_upl = rounded("l1_upl", "big", KD * N1, [KD, N1])
        l3_gateh, l3_gatel = rounded("l3_gateh", "early", 0, [KD, N3]), rounded("l3_gatel", "big", 0, [KD, N3])
        l3_uph, l3_upl = rounded("l3_uph", "early", KD * N3, [KD, N3]), rounded("l3_upl", "big", KD * N3, [KD, N3])
        l3_down2 = [rounded("l3_downh", "mid", 0, [L3.M, D]), rounded("l3_downl", "big", 2 * KD * N3, [L3.M, D])]

        late = sb("late", [P, sum(w for _, w in late_at.values())])
        C = {n: late[:, o:o + w] for n, (o, w) in late_at.items()}
        ident = C["ident"]
        identb = sb("identb", [P, P], BF16)
        tselb = sb("tselb", [P, BPT, P], BF16)
        selb = sb("selb", [P, L1.M * P], BF16)
        maskb = sb("maskb", [P, NT * WK], BF16)
        cosb = sb("cosb", [P, NT, HD // 2])
        sinb = sb("sinb", [P, NT, HD // 2])
        gain = sb("gain", [P, (G * GS + G) * HD])
        wr = sb("wr", [P, D])
        b21 = sb("b21", [P, H2 // P])
        b22 = sb("b22", [1, D])
        br = sb("br", [P, 1])
        small1 = sb("small1", [P, KD, D + P + L1.EW])
        b1s = sb("b1s", [P, D])
        small3 = sb("small3", [P, KD, D + L3.RW])
        work = sb("work", [P, 2560])
        silu = work[:, 0:1536].rearrange("p (s n) -> p s n", s=SLOTS)
        hid = [work[:, 1536:2048], work[:, 2048:2560], mid[:, 4096:4608]]
        hidh = [rounded("hidh0", "work", 1536, [CH]), rounded("hidh1", "work", 2048, [CH]),
                rounded("hidh2", "mid", 4096, [CH])]
        hidh3 = hidh[0:2] + [rounded("hidh3", "yT", 1024, [CH])]
        hidl = rounded("hidl", "mid", 4608, [SLOTS, CH])
        prod = work[:, 2048:2560]
        wdiag = work[:, 0:2048].rearrange("p (i n) -> p i n", n=P)
        raw3 = early[:, ROW:ROW + 1280].rearrange("p (k n) -> p k n", k=KD)
        Pn = work[:, 0:3 * 2 * WK].rearrange("p (s h n) -> p s h n", s=3, h=2)
        ycur = sb("ycur", [P, KD, CH])
        yhigh = rounded("yhigh", "ycur", 0, [KD, CH])
        ylow1 = rounded("ylow1", "mid", 3072, [KD, CH])
        ylow3 = rounded("ylow3", "yT", 0, [KD, CH])
        routerh = sb("routerh", [P, KD * L1.EW], FR)
        routerl = sb("routerl", [P, KD * L1.EW], FR)
        oT = ycur
        ytok = work[:, 0:1024].rearrange("p (t n) -> p t n", t=TPC)
        ywr = scr[:, 0:1024].rearrange("p (t n) -> p t n", t=TPC)
        hT2 = work[:, 1024:1536].rearrange("p (m n) -> p m n", n=TPC * BPT * SEL)
        pwT = prod
        fx = scr[:, 1024:1152].rearrange("p (d n) -> p d n", d=KD)
        outl = scr[:, 1152:1408]
        pick = scr[:, 1408:1664].rearrange("p (t n) -> p t n", t=TPC)
        pickw = scr[:, 1664:1920].rearrange("p (t n) -> p t n", t=TPC)
        lcol = scr[:, 2800:2864].rearrange("p (a t) -> p a t", t=TPC)
        lex = scr[:, 2864:2884].rearrange("p (t n) -> p t n", t=TPC)
        lexe = scr[:, 2884:2904].rearrange("p (t n) -> p t n", t=TPC)
        zm = sb("zm", [P, CH])
        awt = sb("awt", [P, KD, 64])
        wpb = sb("wpb", [64, D])
        top8 = sb("top8", [P, TPC, 8])
        rt = [sb(f"rt{i}", [P, TPC * L1.EW]) for i in range(6)]
        rcol = sb("rcol", [P, 5, TPC])
        parts = sb("parts", [P, TPC * 3 * L1.EW], BF16)
        partsT = sb("partsT", [3 * L1.EW, CH], BF16)
        kcol = sb("kcol", [P, 2, TPC * 12])

        wrows = prod.rearrange("p (i n) -> p i n", i=NT)
        cond_i = sb("cond_i", [P, NT], I32)
        cond_f = sb("cond_f", [P, NT])
        cond_x = sb("cond_x", [P, NT], I32)
        adapt_i = zm[:, 0:2 * B].bitcast(I32).rearrange("p (l b) -> p l b", l=2)
        adapt_f = zm[:, 2 * B:4 * B].rearrange("p (l b) -> p l b", l=2)
        adapt_s = sb("adapt_s", [P, 4])
        amask = sb("amask", [P, 2, B])
        bt_i = rest[:, 0:257].bitcast(I32)
        bt_f = rest[:, 257:514]
        diag4 = rest[:, 514:770].rearrange("p (j b) -> p j b", j=4)
        rowinfo = rest[:, 770:1026]
        ix = rest[:, 1026:1090]
        cmpt = rest[:, 1090:1090 + 3072]
        eqt = rest[:, 4162:4354]
        dest = rest[:, 4354:4402]
        kv_i = sb("kv_i", [P, NT + 1], I32)
        kv_f = sb("kv_f", [P, 4, NT + 1])
        win_i = sb("win_i", [BPT * WB, NT + 1], I32)
        new_i = sb("new_i", [BPT * WB, NT], I32)
        tok_i = sb("tok_i", [P, NT], I32)
        seg_i = sb("seg_i", [P, 2], I32)
        cur_i = sb("cur_i", [P, 3 * TPC], I32)
        blkw = sb("blkw", [BPT * WB, NT])

        names = ("late cast x xrows cond w0 w2 small1 big1 down1 ints first small2 l2w raw3 big3 sel3 "
                 "condidx condx wrows wzero wdiag y0 y0s mix had down0 castb gu_ready w_ready silu_ready "
                 "prod_ready hid_ready acc_ready acc_used z_ready zm_ready y_ready ycur_ready lg_ready "
                 "shifted exp_ready parts_ready partsT_ready partsT_used chain1 chain3 chain2 amask tabst "
                 "tabld destst destld tokst tokld seggot segst rowps rowsb trig folds xs_ready qkv_ready "
                 "squared ssq_ready root_ready v_ready gained roped qps_ready qsb_ready scattered qklinks "
                 "curidx2 gold0 gold1 gnew0 gnew1 shuf0 shuf1 kt_ps kt_sb qbd_ready s_ps nb_ready p_ready "
                 "rr_ready pn_ready pt_ps pt_sb o_ps o_sb qzero ytok_ps ytok_sb ldiag_ready lrow_ps "
                 "lex_ready lexe_ready pick_ready fx_ps fx_sb pwt_ps pwt_sb h_ps h_sb outl_ps outl_sb "
                 "fin_ready fint_sb s_out stdlinks mlinks qkv_end passed ylow_ready hfull_ready "
                 "hhigh_ready w0h w0l w1h w1l w3h w3l wqkv gu_done routed3 rowused masked keys poolhigh "
                 "down3").split()
        s = {n: sem(n) for n in names}


        def split_matmul(out, weights, rows, start, stop):
            (wh, wl), (xh, xl) = weights, rows
            for n, (w, x) in enumerate(((wh, xh), (wh, xl), (wl, xh))):
                last = nc.tensor.matmul(out, w, x, start=start and n == 0,
                                        stop=stop and n == 2)
            return last

        def pe_gate_up(m, w, gate, up, ylow=ylow1):
            cols = slice(m * P, m * P + w)
            for bank, weights in ((m % 2, gate), (2 + m % 2, up)):
                for k in range(KD):
                    last = split_matmul(ps[0:w, bank, :], [x[:, cols] for x in weights[k]],
                                        (yhigh[:, k, :], ylow[:, k, :]), k == 0, k == KD - 1)
            last.then_inc(s["gu_ready"], 1)

        def pe_down(pe, m, w, down, split, step, last_m, high=hidh):
            pe.wait_ge(s["hid_ready"], step + m + 1)
            for d in range(KD):
                cols = slice(d * P, (d + 1) * P)
                if not split:
                    last = nc.tensor.matmul(ps[:, 6 + d, :], down[0:w, m, cols], hid[m % SLOTS][0:w, :],
                                            start=(m == 0), stop=(m == last_m))
                else:
                    last = split_matmul(ps[:, 6 + d, :], [x[0:w, m, cols] for x in down],
                                        (high[m % SLOTS][0:w, :], hidl[0:w, m % SLOTS, :]), m == 0, m == last_m)
            if m == last_m:
                last.then_inc(s["acc_ready"], 1)

        def act_high(act, m, w, step, high=hidh):
            act.wait_ge(s["hfull_ready"], step + m + 1)
            nc.scalar.activation(high[m % SLOTS][0:w, :], silu[0:w, m % SLOTS, :], ACT.Copy)\
                .then_inc(s["hhigh_ready"], 1)

        def dve_low(dve, m, w, step, high=hidh):
            dve.wait_ge(s["hhigh_ready"], step + m + 1)
            nc.vector.tensor_tensor(hidl[0:w, m % SLOTS, :], silu[0:w, m % SLOTS, :], high[m % SLOTS][0:w, :],
                                    ALU.subtract).then_inc(s["hid_ready"], 1)

        def act_silu(act, m, w, step):
            act.wait_ge(s["gu_ready"], step + m + 1)
            nc.scalar.activation(silu[0:w, m % SLOTS, :], ps[0:w, m % 2, :], ACT.Silu).then_inc(s["silu_ready"], 1)

        def dve_residual(dve, tc, acc0):
            dve.wait_ge(s["acc_ready"], tc + acc0 + 1)
            for d in range(KD):
                cols = xT[:, d, bass.ds(tc * CH, CH)]
                last = nc.vector.tensor_tensor(cols, ps[:, 6 + d, :], cols, ALU.add)
            last.then_inc(s["acc_used"], 1)


        def moe_pe(pe, L, tc, wbase, wa, wb, gate, up, down, ready, down_ready):
            step, n, piece = tc * L.M + L.step0, tc + L.chunk0, tc * L.M + L.piece0
            ylow = ylow3 if L.shared else ylow1
            xc = [xT[:, k, bass.ds(tc * CH, CH)] for k in range(KD)]
            for k in range(KD):
                last = nc.tensor.matmul(ps[0:L.Z, 0, :], wa[:, k, :], xc[k], start=(k == 0), stop=(k == KD - 1))
            last.then_inc(s["z_ready"], 1)
            for d in range(KD):
                for k in range(KD):
                    nc.tensor.matmul(ps[:, 2 + d, :], wbase[:, k, d * P:(d + 1) * P], xc[k],
                                     start=(k == 0), stop=False)
            pe.wait_ge(s["zm_ready"], n + 1)
            for d in range(KD):
                last = nc.tensor.matmul(ps[:, 2 + d, :], wb[0:L.Z, d * P:(d + 1) * P], zm[0:L.Z, :],
                                        start=False, stop=True)
            last.then_inc(s["y_ready"], 1)
            pe.wait_ge(s["ylow_ready"], NCH + n + 1)
            pe.wait_ge(s[ready[0]], ready[1])
            for t in range(TPC):
                cols = slice(t * P, (t + 1) * P)
                for k in range(KD):
                    last = split_matmul(ps[:, 4, t * L.RW:(t + 1) * L.RW], (yhigh[:, k, cols], ylow[:, k, cols]),
                                        [x[:, k * L.RW:(k + 1) * L.RW] for x in (routerh, routerl)], k == 0, k == KD - 1)
            last.then_inc(s["lg_ready"], 1)

            def spread(m):
                w = L.widths[m]
                nc.tensor.matmul(ps[0:w, 4 + m % 2, :], selb[0:3 * L.EW, m * P:m * P + w], partsT[0:3 * L.EW, :],
                                 start=True, stop=True).then_inc(s["w_ready"], 1)

            high = hidh3 if L.shared else hidh
            for m in range(L.M):
                if m >= 2:
                    pe.wait_ge(s["prod_ready"], piece + m - 1)
                pe_gate_up(m, L.widths[m], gate, up, ylow)
                if m == 1:
                    pe.wait_ge(s["parts_ready"], n + 1)
                    half = ps[:, 5, :].bitcast(BF16)
                    for t in range(TPC):
                        last = nc.tensor.transpose(half[0:3 * L.EW, t * P:(t + 1) * P],
                                                   parts[:, t * 3 * L.EW:(t + 1) * 3 * L.EW], identb[:, :])
                    last.then_inc(s["partsT_ready"], 1)
                    pe.wait_ge(s["partsT_used"], n + 1)
                    spread(0)
                    spread(1)
                    pe.wait_ge(s["acc_used"], tc + L.acc0)
                    pe.wait_ge(s[down_ready[0]], down_ready[1])
                if m >= 2:
                    if L.split_down:
                        pe.wait_ge(s["hfull_ready"], tc * L.M + (L.high0 + m - 1))
                    else:
                        pe.wait_ge(s["hid_ready"], step + m - 1)
                    spread(m)
                    pe_down(pe, m - 2, L.widths[m - 2], down, L.split_down, step, L.M - 1, high)
            for m in (L.M - 2, L.M - 1):
                pe_down(pe, m, L.widths[m], down, L.split_down, step, L.M - 1, high)

        def moe_act(act, L, tc):
            step, n = tc * L.M + L.step0, tc + L.chunk0
            act.wait_ge(s["y_ready"], n + 1)
            for d in range(KD):
                last = nc.scalar.activation(yhigh[:, d, :], ps[:, 2 + d, :], ACT.Copy)
            last.then_inc(s["ycur_ready"], 1)
            act.wait_ge(s["shifted"], n + 1)
            last = nc.scalar.activation(rt[1][:, 0:TPC * L.E], rt[0][:, 0:TPC * L.E], ACT.Exp)
            if L.shared:
                last = nc.scalar.activation(rcol[:, 3, :], rcol[:, 4, :], ACT.Exp, scale=-1.0)
            last.then_inc(s["exp_ready"], 1)
            act_silu(act, 0, L.widths[0], step)
            act_silu(act, 1, L.widths[1], step)
            act.wait_ge(s["partsT_ready"], n + 1)
            nc.scalar.activation(partsT[0:3 * L.EW, :], ps[:, 5, :].bitcast(BF16)[0:3 * L.EW, 0:CH],
                                 ACT.Copy).then_inc(s["partsT_used"], 1)
            for m in range(2, L.M):
                if L.split_down:
                    for h in range(0 if m == 2 else m - 1, m):
                        act_high(act, h, L.widths[h], tc * L.M + L.high0, hidh3)
                act_silu(act, m, L.widths[m], step)
            if L.split_down:
                act_high(act, L.M - 1, L.widths[-1], tc * L.M + L.high0, hidh3)

        def moe_dve(dve, L, li, tc, chain_sem):
            step, n, piece = tc * L.M + L.step0, tc + L.chunk0, tc * L.M + L.piece0
            dve.wait_ge(s["z_ready"], n + 1)
            nc.vector.tensor_tensor(
                zm[0:L.Z, :].rearrange("p (b s) -> p b s", s=S),
                ps[0:L.Z, 0, :].rearrange("p (b s) -> p b s", s=S),
                amask[0:L.Z, li, bass.ds(tc * BPC, BPC)].unsqueeze(2).broadcast_to([L.Z, BPC, S]),
                ALU.mult).then_inc(s["zm_ready"], 1)
            dve.wait_ge(s["ycur_ready"], NCH + n + 1)
            ylow = ylow3 if L.shared else ylow1
            for d in range(KD):
                last = nc.vector.tensor_tensor(ylow[:, d, :], ps[:, 2 + d, :], yhigh[:, d, :],
                                               ALU.subtract)
            last.then_inc(s["ylow_ready"], 1)
            E, EW = L.E, L.EW
            flat = TPC * E

            def tiles(x, e=E):
                return x[:, 0:TPC * e].rearrange("p (t e) -> p t e", t=TPC)

            def over(col, e=E):
                return col.broadcast_to([P, TPC, e])

            ch = Chain(dve, chain_sem, tc * L.links)
            lg = tiles(ps[:, 4, :], L.RW)[:, :, 0:E]
            dve.wait_ge(s["lg_ready"], n + 1)
            nc.vector.sem_inc(s["passed"], 1)
            for t in range(TPC):
                last = nc.vector.max(top8[:, t, :], lg[:, t, :])
            ch.link(last)
            if L.shared:
                nc.vector.tensor_copy(rcol[:, 4, :], tiles(ps[:, 4, :], L.RW)[:, :, E])
            nc.vector.tensor_tensor(tiles(rt[0]), lg, over(top8[:, :, 0:1]), ALU.subtract)\
                .then_inc(s["shifted"], 1)
            nc.vector.tensor_tensor(tiles(rt[2]), lg, over(top8[:, :, L.K - 1:L.K]), ALU.is_gt)
            ch.link(nc.vector.tensor_tensor(tiles(rt[3]), lg, over(top8[:, :, L.K - 1:L.K]), ALU.is_equal))
            nc.vector.tensor_reduce(rcol[:, 0, :], tiles(rt[2]), X, ALU.add)
            ch.link(nc.vector.tensor_tensor_scan(rt[4][:, 0:flat], C["restart%d" % E][:, 0:flat], rt[3][:, 0:flat],
                                                 0.0, ALU.mult, ALU.add))
            ch.link(nc.vector.tensor_tensor(tiles(rt[5]), tiles(rt[4]), over(rcol[:, 0, :].unsqueeze(2)), ALU.add))
            ch.link(nc.vector.scalar_tensor_tensor(rt[4][:, 0:flat], rt[5][:, 0:flat], float(L.K), rt[3][:, 0:flat],
                                                   ALU.is_le, ALU.mult))
            ch.link(nc.vector.tensor_tensor(rt[3][:, 0:flat], rt[2][:, 0:flat], rt[4][:, 0:flat], ALU.add))
            dve.wait_ge(s["exp_ready"], n + 1)
            ch.link(nc.vector.tensor_tensor(rt[2][:, 0:flat], rt[1][:, 0:flat], rt[3][:, 0:flat], ALU.mult))
            ch.link(nc.vector.tensor_reduce(rcol[:, 1, :], tiles(rt[2]), X, ALU.add))
            ch.link(nc.vector.reciprocal(rcol[:, 2, :], rcol[:, 1, :]))
            weights = tiles(rt[5], EW)
            ch.link(nc.vector.tensor_tensor(weights[:, :, 0:E], tiles(rt[2]), over(rcol[:, 2, :].unsqueeze(2)),
                                            ALU.mult))
            if L.shared:
                ch.link(nc.vector.tensor_scalar(rcol[:, 0, :], rcol[:, 3, :], 1.0, None, ALU.add))
                ch.link(nc.vector.reciprocal(weights[:, :, E:EW], rcol[:, 0, :].unsqueeze(2)))
            part = [parts[:, 0:TPC * 3 * EW].rearrange("p (t j e) -> p t j e", t=TPC, j=3)[:, :, j, :]
                    for j in range(3)]
            ch.link(nc.vector.tensor_copy(part[0], weights))
            ch.link(nc.vector.tensor_tensor(tiles(rt[0], EW), weights, part[0], ALU.subtract))
            ch.link(nc.vector.tensor_copy(part[1], tiles(rt[0], EW)))
            ch.link(nc.vector.tensor_tensor(tiles(rt[2], EW), tiles(rt[0], EW), part[1], ALU.subtract))
            nc.vector.tensor_copy(part[2], tiles(rt[2], EW)).then_inc(s["parts_ready"], 1)
            assert ch.n == L.links, ch.n

            for m, w in enumerate(L.widths):
                dve.wait_ge(s["silu_ready"], step + m + 1)
                row = silu[0:w, m % SLOTS, :]
                nc.vector.tensor_tensor(row, row, ps[0:w, 2 + m % 2, :],
                                        ALU.mult).then_inc(s["prod_ready"], 1)
                dve.wait_ge(s["prod_ready"], piece + m + 1)
                dve.wait_ge(s["w_ready"], piece + m + 1)
                if L.split_down:
                    nc.vector.tensor_tensor(row, row, ps[0:w, 4 + m % 2, :], ALU.mult).then_inc(s["hfull_ready"], 1)
                    dve_low(dve, m, w, tc * L.M + L.high0, hidh3)
                else:
                    nc.vector.tensor_tensor(hid[m % SLOTS][0:w, :], row, ps[0:w, 4 + m % 2, :], ALU.mult)\
                        .then_inc(s["hid_ready"], 1)

        rows16 = newblk.rearrange("s (o n) -> (s o) n", n=2 * KW)
        SC = 1.0 / 16.0
        block = ctx.enter_context(nc.Block())

        TURNED = 16 * 2 * BPT
        @block.sync
        def _(sp):
            nc.sync.sem_inc(s["shuf1"], TURNED)
            sp.dma_start(cond_i[:, :], a["cond"]).then_inc(s["cond"], 16)
            sp.dma_start(late[:, :], a["late"]).then_inc(s["late"], 16)
            sp.dma_start(kv_i[:, :], a["kv"]).then_inc(s["ints"], 16)
            sp.dma_start(bt_i[0:B, :], a["tables"]).then_inc(s["ints"], 16)
            sp.dma_start(mid[:, 3072:3072 + first_n], a["first"]).then_inc(s["first"], 16)
            sp.dma_start(l0_down, a["w2"]).then_inc(s["w2"], 16)
            sp.dma_start(xrows, a["xrows"]).then_inc(s["xrows"], 16)
            sp.dma_start(early[:, 0:4096], a["w13"]).then_inc(s["w0"], 16)
            sp.dma_start(xT[:, :, :], a["xT"]).then_inc(s["x"], 16)
            for dst, name in ((small1, "small1"), (b1s, "b1"), (small3, "small3"), (adapt_i, "adapt"),
                              (adapt_s, "adapt_s")):
                sp.dma_start(dst if dst is adapt_i else dst[:], a[name]).then_inc(s["small1"], 16)
            for dst, name in ((gain, "gain"), (wr, "wr"), (b21, "b21"), (b22, "b22"), (br, "br")):
                sp.dma_start(dst[:], a[name]).then_inc(s["small2"], 16)
            sp.wait_ge(s["tabst"], 1)
            sp.dma_start(tab_d, ix[0:B, 16:16 + WB]).then_inc(s["tabld"], 16)
            sp.wait_ge(s["tabld"], 16)
            with nc.allow_non_contiguous_dma(reason="704 words"):
                sp.dma_start(blkw[:, :], tab_d.rearrange("(g b) i -> (b i) g", b=BPT)).then_inc(s["tabld"], 16)
            sp.wait_ge(s["destst"], 1)
            for j in range(NEWB):
                src = dest[(j % 2) * B:(j % 2 + 1) * B, (j // 2) * BLOCK:(j // 2 + 1) * BLOCK]
                sp.dma_start(dest_d[:, j * BLOCK:(j + 1) * BLOCK], src).then_inc(s["destld"], 16)
            sp.wait_ge(s["destld"], 16 * NEWB)
            sp.dma_start(rest[0:B, 4402:4450], dest_d).then_inc(s["destld"], 16)
            sp.wait_ge(s["tokst"], 1)
            sp.dma_start(tok_d, rest[0:B, 4450:4482].bitcast(I32)).then_inc(s["tokld"], 16)
            sp.wait_ge(s["tokld"], 16)
            with nc.allow_non_contiguous_dma(reason="2048 words"):
                sp.dma_start(tok_i[:, :], tok_d.rearrange("(i b) t -> (b t) i", b=BPT)).then_inc(s["tokld"], 16)
            sp.wait_ge(s["seggot"], 32)
            sp.dma_start(newblk[0:P, :], stage[:, 0, :]).then_inc(s["segst"], 16)
            sp.dma_start(newblk[P:SEGS, :], stage[0:B, 1, :]).then_inc(s["segst"], 16)
            sp.wait_ge(s["segst"], 32)
            sp.wait_ge(s["tokst"], 1)
            sp.dma_start(l1_gate, a["gate1"]).then_inc(s["big1"], 16)
            sp.dma_start(l1_up, a["up1"]).then_inc(s["big1"], 16)
            sp.wait_ge(s["acc_used"], NCH)
            sp.dma_start(l1_down, a["down1"]).then_inc(s["down1"], 16)
            sp.wait_ge(s["acc_used"], 2 * NCH)
            k0 = first_at["key"][0]
            assert first_at["keyless"][0] == k0 + WK
            sp.dma_start(zm[:, 0:2 * WK], a["first"][:, k0:k0 + 2 * WK]).then_inc(s["keys"], 16)
            sp.dma_start(mid[:, 0:1024], a["l2w"][:, 0:1024]).then_inc(s["wqkv"], 16)
            sp.dma_start(raw3, a["raw3"]).then_inc(s["raw3"], 16)
            sp.dma_start(mid[:, 1024:5632], a["l2w"][:, 1024:5632]).then_inc(s["l2w"], 16)
            sp.dma_start(big[:, 0:2 * KD * N3], a["gu3"]).then_inc(s["big3"], 16)
            sp.wait_ge(s["masked"], 1)
            with sp.Fori(0, NCH) as tc:
                for t in range(TPC):
                    slot = t % 2
                    sp.wait_ge(s["gnew0" if slot == 0 else "gnew1"], (tc * 2 + t // 2 + 1) * 16)
                    nc.sync.sem_inc(s["passed"], 1)
                    sp.wait_ge(s["o_ps"], tc * BPC + (O_CREDIT - BPC + BPT * (t + 1)))
                    for q in range(BPT):
                        for h, (i0, i1) in enumerate(((0, 6), (6, WB))):
                            sp.dma_start(kv2[t][0:(i1 - i0) * BLOCK, h, q, :],
                                         kvw[slot * 64 + q * WB + i0:slot * 64 + q * WB + i1, :, :])\
                                .then_inc(s["shuf0" if slot == 0 else "shuf1"], 16)
            sp.wait_ge(s["o_ps"], O_CREDIT + B)
            sp.dma_start(l3_down, a["down3"]).then_inc(s["down3"], 16)
            with sp.Fori(0, NCH) as tc:
                sp.wait_ge(s["acc_used"], tc + 3 * NCH + 1)
                sp.dma_start(a["out"][:, :, bass.ds(tc * CH, CH)], xT[:, :, bass.ds(tc * CH, CH)])\
                    .then_inc(s["s_out"], 16)
            sp.wait_ge(s["s_out"], 16 * NCH)

        @block.gpsimd
        def _(pool):
            def gather(out, src, idx, signal, **kw):
                nc.gpsimd.indirect_dma_start(
                    out=out, out_offset=None, in_=src, in_offset=bass.IndirectOffsetOnAxis(ap=idx, axis=0), **kw
                ).then_inc(signal, 16)

            nc.gpsimd.memset(work[:, 0:2048], 0.0).then_inc(s["wzero"], 1)
            pool.wait_ge(s["condx"], 1)
            for i in range(NT):
                gather(wrows[:, i, :], a["cond_w"], cond_x[:, i:i + 1], s["wrows"])
            o1, o2 = cast_at["identb"][0], cast_at["sel1"][0]
            pool.dma_start(identb[:, :], a["cast"][:, o1:o1 + P]).then_inc(s["castb"], 16)
            pool.dma_start(tselb[:, :, :], a["cast"][:, o1 + P:o2].rearrange("p (q n) -> p q n", q=BPT))\
                .then_inc(s["castb"], 16)
            pool.dma_start(selb[:, :], a["cast"][:, o2:o2 + L1.M * P]).then_inc(s["castb"], 16)
            pool.wait_ge(s["condidx"], 1)
            gather(stage[:, 0, :], a["cache"], seg_i[:, 0:1], s["seggot"])
            gather(stage[0:B, 1, :], a["cache"], seg_i[0:B, 1:2], s["seggot"])

            pool.wait_ge(s["big1"], 32)
            pool.wait_ge(s["tokst"], 1)
            nc.gpsimd.tensor_copy(l1_uph[1], l1_up[:, 1, :]).then_inc(s["poolhigh"], 1)
            pool.wait_ge(s["poolhigh"], 1)
            nc.gpsimd.tensor_tensor(l1_upl[:, 1, :], l1_up[:, 1, :], l1_uph[1], ALU.subtract).then_inc(s["w1l"], 1)

            pool.wait_ge(s["acc_used"], 2 * NCH)
            o3 = cast_at["sel3"][0]
            pool.dma_start(selb[:, 0:L3.M * P], a["cast"][:, o3:o3 + L3.M * P]).then_inc(s["sel3"], 16)

            gold = ("gold0", "gold1")
            pool.wait_ge(s["masked"], 1)
            gather(early[0:BPT * WB, 0:ROW], a["cache"], win_i[:, 0:1], s["gold0"])

            pool.wait_ge(s["segst"], 32)
            pool.wait_ge(s["tokld"], 32)
            for c in range(NCH):
                pool.wait_ge(s["roped"], c + 1)
                pool.wait_ge(s["v_ready"], c + 1)
                for t in range(TPC):
                    i = c * TPC + t
                    nc.gpsimd.indirect_dma_start(
                        out=rows16, out_offset=bass.IndirectOffsetOnAxis(ap=tok_i[:, i:i + 1], axis=0),
                        in_=kvrow[c % 2][:, t, :], in_offset=None, bounds_check=SEGS * BLOCK - 1, oob_is_err=False,
                    ).then_inc(s["scattered"], 16)
                pool.wait_ge(s["scattered"], (c + 1) * (16 * TPC))

            pool.wait_ge(s["scattered"], 16 * NT)
            pool.wait_ge(s["qkv_end"], 1)
            nc.gpsimd.memset(Qbd, 0.0).then_inc(s["qzero"], 1)
            pool.wait_ge(s["qzero"], 1)
            with pool.Fori(0, NCH) as tc:
                nc.gpsimd.tensor_copy(cur_i[0:BPT * WB, 4:8], win_i[:, bass.ds(tc * TPC + 1, TPC)])
                nc.gpsimd.tensor_copy(cur_i[0:BPT * WB, 8:12], new_i[:, bass.ds(tc * TPC, TPC)])\
                    .then_inc(s["curidx2"], 1)
                pool.wait_ge(s["curidx2"], tc + 1)
                nc.gpsimd.sem_inc(s["passed"], 1)
                for t in range(TPC):
                    rows, ahead = (early[x * 64:x * 64 + BPT * WB, 0:ROW] for x in (t % 2, 1 - t % 2))
                    pool.wait_ge(s[gold[t % 2]], (tc * 2 + t // 2 + 1) * 16)
                    nc.gpsimd.sem_inc(s["passed"], 1)
                    gather(rows, newblk, cur_i[0:BPT * WB, 8 + t:9 + t], s["gnew0" if t % 2 == 0 else "gnew1"],
                           bounds_check=SEGS - 1, oob_is_err=False)
                    if t % 2 == 0:
                        pool.wait_ge(s["shuf1"], (tc * 2 + t // 2 + 1) * TURNED)
                    else:
                        pool.wait_ge(s["shuf0"], (tc * 2 + t // 2 + 1) * TURNED)
                    nc.gpsimd.sem_inc(s["passed"], 1)
                    gather(ahead, a["cache"], cur_i[0:BPT * WB, 4 + t:5 + t], s[gold[1 - t % 2]])
                pool.wait_ge(s["gold0"], (tc * 2 + 3) * 16)
                pool.wait_ge(s["gold1"], (tc * 2 + 2) * 16)
                nc.gpsimd.sem_inc(s["passed"], 1)

            pool.wait_ge(s["big3"], 16)
            pool.wait_ge(s["gold0"], (2 * NCH + 1) * 16)
            pool.wait_ge(s["shuf1"], (2 * NCH + 1) * TURNED)
            for i, (low, full, high) in enumerate(((l3_gatel[:, 0, :], l3_gate[:, 0, :], l3_gateh[:, 0, :]),
                                                   (l3_gatel[:, 1, :], l3_gate[:, 1, :], l3_gateh[:, 1, :]),
                                                   (l3_upl[:, 0, :], l3_up[:, 0, :], l3_uph[:, 0, :]))):
                pool.wait_ge(s["o_ps"], O_CREDIT + B - BPC + BPT * (2 if i == 2 else 1))
                nc.gpsimd.tensor_copy(high, full).then_inc(s["poolhigh"], 1)
                pool.wait_ge(s["poolhigh"], i + 2)
                nc.gpsimd.tensor_tensor(low, full, high, ALU.subtract).then_inc(s["w3l"], 1)

        @block.scalar
        def _(act):
            act.wait_ge(s["folds"], 1)
            nc.scalar.activation(sinb[:], sinb[:], ACT.Sin)
            nc.scalar.activation(cosb[:], cosb[:], ACT.Sin).then_inc(s["trig"], 1)
            for g in range(0, 8, 2):
                act.wait_ge(s["y0"], g + 1)
                nc.scalar.activation(yT[:, g % 2, (g // 2) * CH:(g // 2 + 1) * CH], ps[:, g, :], ACT.Copy)\
                    .then_inc(s["y0s"], 1)
            act.wait_ge(s["y0"], 8)
            act.wait_ge(s["w0"], 16)
            nc.scalar.activation(l0_high, early[:, 0:4096], ACT.Copy).then_inc(s["w0h"], 1)
            act.wait_ge(s["had"], 1)
            nc.scalar.activation(l0_down2[0], ps[:, 0:4, :].rearrange("p c (m n) -> p (c m) n", n=D), ACT.Copy).then_inc(s["down0"], 1)
            with act.Fori(0, NCH) as tc:
                act.wait_ge(s["gu_done"], tc + 1)
                nc.scalar.activation(yhigh, yT[:, :, bass.ds(tc * CH, CH)], ACT.Copy).then_inc(s["ycur_ready"], 1)
                for m in range(M0 + 1):
                    if m >= 1:
                        act_high(act, m - 1, P, tc * M0)
                    if m < M0:
                        act_silu(act, m, P, tc * M0)
            act.wait_ge(s["acc_used"], NCH)
            act.wait_ge(s["big1"], 32)
            act.wait_ge(s["tokst"], 1)
            nc.scalar.activation(l1_gateh[:, 0, :], l1_gate[:, 0, :], ACT.Copy).then_inc(s["w1h"], 1)
            nc.scalar.activation(l1_uph[0], l1_up[:, 0, :], ACT.Copy).then_inc(s["w1h"], 1)
            nc.scalar.activation(l1_gateh[:, 1, :], l1_gate[:, 1, :], ACT.Copy).then_inc(s["w1h"], 1)
            with act.Fori(0, NCH) as tc:
                moe_act(act, L1, tc)

            def rows_in(c):
                nc.scalar.activation(ycur[:, :, :], xT[:, :, c * CH:(c + 1) * CH], ACT.Copy).then_inc(s["xs_ready"], 1)

            def queries_out(c):
                act.wait_ge(s["qps_ready"], c + 1)
                nc.scalar.activation(qT[:, :, c * CH:(c + 1) * CH], ps[:, 4:6, :], ACT.Copy)\
                    .then_inc(s["qsb_ready"], 1)

            act.wait_ge(s["acc_used"], 2 * NCH)
            rows_in(0)
            for c in range(NCH):
                act.wait_ge(s["qkv_ready"], c + 1)
                nc.scalar.activation(sqr[c % 2].rearrange("p (t n) -> p t n", t=TPC), ps[:, 0:4, 0:384], ACT.Square)\
                    .then_inc(s["squared"], 1)
                if c >= 2:
                    act.wait_ge(s["scattered"], (c - 1) * (16 * TPC))
                nc.scalar.activation(kvrow[c % 2][:, :, KW:2 * KW], ps[:, 0:4, 384:512], ACT.Copy)\
                    .then_inc(s["v_ready"], 1)
                if c + 1 < NCH:
                    rows_in(c + 1)
                if c == 0:
                    act.wait_ge(s["fin_ready"], 1)
                    nc.scalar.activation(awt[:, :, :], ps[:, 6, 0:128].rearrange("p (k n) -> p k n", k=KD), ACT.Copy)
                    nc.scalar.activation(wpb[:, :], ps[0:64, 7, 0:256], ACT.Copy).then_inc(s["fint_sb"], 1)
                if c >= 1:
                    queries_out(c - 1)
                act.wait_ge(s["ssq_ready"], c + 1)
                nc.scalar.activation(kcol[:, 0, :], kcol[:, 1, :], ACT.Sqrt).then_inc(s["root_ready"], 1)
            queries_out(NCH - 1)
            act.wait_ge(s["qsb_ready"], NCH)
            nc.scalar.activation(rcol[:, 3, :], rcol[:, 1, :], ACT.Copy).then_inc(s["qkv_end"], 1)

            act.wait_ge(s["masked"], 1)

            def keys_out(tc, n):
                act.wait_ge(s["kt_ps"], tc * BPC + (n + 1))
                nc.scalar.activation(KTs[:, n % 2, :], ps[:, n % 2, 0:WK], ACT.Copy).then_inc(s["kt_sb"], 1)

            def exponentials(tc, n):
                act.wait_ge(s["nb_ready"], tc * BPC + (n + 1))
                for h in range(2):
                    last = nc.scalar.activation(Pex[:, n % 2, h, :], ps[:, 2 + n % 2, h * WK:(h + 1) * WK], ACT.Exp,
                                                bias=acol[:, 1, n % 2, h:h + 1], scale=SC,
                                                accum_out=acol[:, 2, n % 2, h:h + 1])
                last.then_inc(s["p_ready"], 1)

            def probs_out(tc, n):
                act.wait_ge(s["pt_ps"], tc * BPC + (n + 1))
                nc.scalar.activation(PTs[0:96, n % 2, 0, :], ps[0:96, 4 + n % 2, 0:256], ACT.Copy)
                nc.scalar.activation(PTs[0:80, n % 2, 1, :], ps[0:80, 4 + n % 2, 256:512], ACT.Copy)\
                    .then_inc(s["pt_sb"], 1)

            with act.Fori(0, NCH) as tc:
                for n in range(BPC + 3):
                    if n < BPC:
                        keys_out(tc, n)
                    if n >= 3:
                        probs_out(tc, n - 3)
                    if 1 <= n <= BPC:
                        exponentials(tc, n - 1)
                act.wait_ge(s["ytok_ps"], tc + 1)
                nc.scalar.activation(ytok.rearrange("p (a b) n -> p a (b n)", a=2), ps[:, 0:2, :], ACT.Copy)\
                    .then_inc(s["ytok_sb"], 1)
                act.wait_ge(s["lex_ready"], tc + 1)
                nc.scalar.activation(lexe, lex, ACT.Exp).then_inc(s["lexe_ready"], 1)
                act.wait_ge(s["fx_ps"], tc + 1)
                nc.scalar.activation(fx, ps[:, 3, 0:128].rearrange("p (d n) -> p d n", d=KD), ACT.Copy)\
                    .then_inc(s["fx_sb"], 1)
                act.wait_ge(s["pwt_ps"], tc + 1)
                nc.scalar.activation(pwT[0:64, :], ps[0:64, 4, :], ACT.Copy).then_inc(s["pwt_sb"], 1)
                act.wait_ge(s["h_ps"], tc + 1)
                for m in range(H2 // P):
                    last = nc.scalar.activation(hT2[:, m, :], ps[:, 5, m * 64:(m + 1) * 64], ACT.Gelu,
                                                bias=b21[:, m:m + 1])
                last.then_inc(s["h_sb"], 1)
                act.wait_ge(s["outl_ps"], tc + 1)
                nc.scalar.activation(outl[0:64, :], ps[0:64, 0, 0:256], ACT.Copy).then_inc(s["outl_sb"], 1)

            act.wait_ge(s["acc_used"], 3 * NCH)
            act.wait_ge(s["big3"], 16)
            nc.scalar.activation(l3_uph[:, 1, :], l3_up[:, 1, :], ACT.Copy).then_inc(s["w3h"], 1)
            act.wait_ge(s["down3"], 16)
            nc.scalar.activation(l3_down2[0], l3_down, ACT.Copy).then_inc(s["w3h"], 1)
            with act.Fori(0, NCH) as tc:
                moe_act(act, L3, tc)

        @block.vector
        def _(dve):
            ch = Chain(dve, s["chain1"])
            dve.wait_ge(s["cond"], 16)
            ch.link(nc.vector.tensor_copy(cond_f[:, :], cond_i[:, :]))
            dve.wait_ge(s["late"], 16)
            nc.vector.tensor_scalar(cond_x[:, :], cond_f[:, :], float(S), C["rowt"], ALU.mult, ALU.add)\
                .then_inc(s["condx"], 1)

            dve.wait_ge(s["ints"], 32)
            dve.wait_ge(s["first"], 16)
            kv, off0, hi, slot0 = (kv_f[:, j, :] for j in range(4))
            ch.link(nc.vector.tensor_copy(kv, kv_i[:, :]))
            ch.link(nc.vector.tensor_scalar(off0, kv, 1.0 / BLOCK, -0.5 + 0.5 / BLOCK, ALU.mult, ALU.add))
            ch.link(nc.vector.tensor_scalar(hi, off0, MAGIC, None, ALU.add))
            ch.link(nc.vector.tensor_scalar(slot0, hi, MAGIC, None, ALU.subtract))
            ch.link(nc.vector.scalar_tensor_tensor(off0, slot0, -float(BLOCK), kv, ALU.mult, ALU.add))
            ang, turns, fold, wrap = (ycur[:, j // 2, (j % 2) * 256:(j % 2 + 1) * 256] for j in range(4))
            pos = kv_f[:, 2, 0:NT]
            ch.link(nc.vector.tensor_scalar(pos, kv[:, 0:NT], C["rowt"], None, ALU.add))
            ch.link(nc.vector.tensor_tensor(ang.rearrange("p (i f) -> p i f", i=NT),
                                            pos.unsqueeze(2).broadcast_to([P, NT, HD // 2]),
                                            F["inv"].unsqueeze(1).broadcast_to([P, NT, HD // 2]), ALU.mult))
            ch.link(nc.vector.tensor_scalar(turns, ang, float(1 / (2 * np.pi)), None, ALU.mult))
            ch.link(nc.vector.tensor_scalar(turns, turns, MAGIC, None, ALU.add))
            ch.link(nc.vector.tensor_scalar(turns, turns, MAGIC, None, ALU.subtract))
            ch.link(nc.vector.scalar_tensor_tensor(fold, turns, -TWO_PI_HI, ang, ALU.mult, ALU.add))
            ch.link(nc.vector.scalar_tensor_tensor(ang, turns, -TWO_PI_LO, fold, ALU.mult, ALU.add))
            edge = 3.1415925
            sin_f = sinb[:].rearrange("p i f -> p (i f)")
            cos_f = cosb[:].rearrange("p i f -> p (i f)")
            ch.link(nc.vector.tensor_scalar(sin_f, ang, edge, -edge, ALU.min, ALU.max))
            ch.link(nc.vector.tensor_scalar(wrap, ang, float(np.pi / 2), -float(2 * np.pi), ALU.is_gt, ALU.mult))
            ch.link(nc.vector.scalar_tensor_tensor(fold, ang, float(np.pi / 2), wrap, ALU.add, ALU.add))
            nc.vector.tensor_scalar(cos_f, fold, edge, -edge, ALU.min, ALU.max).then_inc(s["folds"], 1)

            slots, tab = ix[0:B, 0:WB], ix[0:B, 16:16 + WB]
            ch.link(nc.vector.tensor_copy(bt_f[0:B, :], bt_i[0:B, :]))
            ch.link(nc.vector.tensor_scalar(slots, F["win"][0:B, :], slot0[0:B, NT:NT + 1], 0.0, ALU.add, ALU.max))
            ch.link(nc.vector.tensor_scalar(slots, slots, float(NBLK - 1), None, ALU.min))
            for i in range(WB):
                ch.link(nc.vector.scalar_tensor_tensor(cmpt[0:B, i * NBLK:(i + 1) * NBLK], F["slots"][0:B, :],
                                                       slots[:, i:i + 1], bt_f[0:B, :], ALU.is_equal, ALU.mult,
                                                       accum_out=tab[:, i:i + 1]))
            i0 = WINDOW // BLOCK
            segf = ix[:, 32:34]
            nc.vector.tensor_copy(segf[0:B, 0:1], tab[:, i0:i0 + 1]).then_inc(s["tabst"], 1)
            nc.vector.tensor_copy(segf[B:P, 0:1], tab[:, i0 + 1:i0 + 2])
            ch.link(nc.vector.tensor_copy(segf[0:B, 1:2], tab[:, i0 + 2:i0 + 3]))
            nc.vector.tensor_copy(seg_i[:, 0:1], segf[:, 0:1])
            nc.vector.tensor_copy(seg_i[0:B, 1:2], segf[0:B, 1:2]).then_inc(s["condidx"], 1)
            idB = ident[0:B, 0:B]
            ch.link(nc.vector.tensor_tensor(diag4[0:B, 0:NEWB, :], idB.unsqueeze(1).broadcast_to([B, NEWB, B]),
                                            tab[:, i0:i0 + NEWB].unsqueeze(2).broadcast_to([B, NEWB, B]), ALU.mult))
            nc.vector.tensor_scalar(diag4[0:B, NEWB, :], idB, off0[0:B, NT:NT + 1], None, ALU.mult)\
                .then_inc(s["rowps"], 1)
            dve.wait_ge(s["wrows"], 16 * NT)
            dve.wait_ge(s["wzero"], 1)
            for q in range(BPT):
                r = slice(q * S, (q + 1) * S)
                last = nc.vector.tensor_copy(wdiag[r, :, r], wrows[r, :, :])
            last.then_inc(s["wdiag"], 1)
            dve.wait_ge(s["rowsb"], 1)
            ch.link(nc.vector.tensor_copy(rowinfo, ps[:, 7, 0:256]))
            nc.vector.sem_inc(s["rowused"], 1)
            dve.wait_ge(s["w2"], 16)
            for step, (src, dst) in enumerate(((l0_down, w2mix), (w2mix, l0_down), (l0_down, w2mix))):
                r = 4 >> step
                si, di = (z.rearrange("p (a h r) n -> p a h (r n)", h=2, r=r) for z in (src, dst))
                nc.vector.tensor_tensor(di[:, :, 0, :], si[:, :, 0, :], si[:, :, 1, :], ALU.add)
                last = nc.vector.tensor_tensor(di[:, :, 1, :], si[:, :, 0, :], si[:, :, 1, :], ALU.subtract)
                if step < 2:
                    ch.link(last)
            last.then_inc(s["mix"], 1)
            segblk, offrow = rowinfo[:, 0:SEGS], rowinfo[:, SEGS:SEGS + B]
            v = seen.rearrange("p (o j b) -> p o j b", o=BLOCK, j=NEWB)
            prio = F["prio"].rearrange("p (j b) -> p j b", j=NEWB)

            def over_o(x):
                return x.unsqueeze(1).broadcast_to([P, BLOCK, B])

            offs = F["off"].unsqueeze(2).broadcast_to([P, BLOCK, B])
            ch.link(nc.vector.tensor_copy(v[:, :, 1, :], over_o(prio[:, 1, :])))
            ch.link(nc.vector.tensor_tensor(v[:, :, 0, :], over_o(offrow), offs, ALU.is_le))
            ch.link(nc.vector.tensor_tensor(v[:, :, 2, :], over_o(offrow), offs, ALU.is_gt))
            ch.link(nc.vector.tensor_tensor(v[:, :, 0, :], v[:, :, 0, :], over_o(prio[:, 0, :]), ALU.mult))
            ch.link(nc.vector.tensor_tensor(v[:, :, 2, :], v[:, :, 2, :], over_o(prio[:, 2, :]), ALU.mult))
            for g in range(1, 8, 2):
                dve.wait_ge(s["y0"], g + 1)
                nc.vector.tensor_copy(yT[:, g % 2, (g // 2) * CH:(g // 2 + 1) * CH], ps[:, g, :])\
                    .then_inc(s["y0s"], 1)
            win, last_seg, col = ix[:, 40:56], ix[:, 56:57], ix[:, 57:58]
            for st, rows in enumerate((P, B)):
                ch.link(nc.vector.tensor_scalar(eqt[0:rows, :], segblk[0:rows, :], segf[0:rows, st:st + 1], None,
                                                ALU.is_equal))
                ch.link(nc.vector.tensor_tensor(cmpt[0:rows, :].rearrange("p (o n) -> p o n", o=BLOCK),
                                                seen[0:rows, :].rearrange("p (o n) -> p o n", o=BLOCK),
                                                eqt[0:rows, :].unsqueeze(1).broadcast_to([rows, BLOCK, SEGS]),
                                                ALU.mult))
                ch.link(nc.vector.tensor_reduce(win[0:rows, :], cmpt[0:rows, :].rearrange("p (o n) -> p o n", o=BLOCK),
                                                X, ALU.max))
                ch.link(nc.vector.tensor_tensor(cmpt[0:rows, 0:SEGS], eqt[0:rows, :], F["segid"][0:rows, :], ALU.mult))
                ch.link(nc.vector.tensor_reduce(last_seg[0:rows, :], cmpt[0:rows, 0:SEGS], X, ALU.max))
                ch.link(nc.vector.tensor_scalar(col[0:rows, :], last_seg[0:rows, :], float(BLOCK), -BLOCK - FAR,
                                                ALU.mult, ALU.add))
                ch.link(nc.vector.tensor_scalar(eqt[0:rows, 0:BLOCK], F["off"][0:rows, :], col[0:rows, :], None,
                                                ALU.add))
                ch.link(nc.vector.scalar_tensor_tensor(cmpt[0:rows, 0:BLOCK], win[0:rows, :],
                                                       F["myprio"][0:rows, st:st + 1], eqt[0:rows, 0:BLOCK],
                                                       ALU.is_equal, ALU.mult))
                ch.link(nc.vector.tensor_scalar(dest[0:rows, st * BLOCK:(st + 1) * BLOCK], cmpt[0:rows, 0:BLOCK], FAR,
                                                None, ALU.add))
            nc.vector.tensor_copy(ix[:, 58:59], ix[:, 56:57]).then_inc(s["destst"], 1)
            dve.wait_ge(s["w0h"], 1)
            nc.vector.tensor_tensor(l0_low, early[:, 0:4096], l0_high, ALU.subtract).then_inc(s["w0l"], 1)
            dve.wait_ge(s["down0"], 1)
            nc.vector.tensor_tensor(l0_down2[1], ps[:, 0:4, :].rearrange("p c (m n) -> p (c m) n", n=D), l0_down2[0],
                                    ALU.subtract).then_inc(s["w0l"], 1)
            dve.wait_ge(s["tabld"], 32)
            WR = BPT * WB
            nc.vector.tensor_copy(win_i[:, 0:NT], blkw[:, :])
            nc.vector.tensor_copy(win_i[:, NT:NT + 1], blkw[:, 0:1])
            wide = cmpt[0:WR, :].rearrange("p (g n) -> p g n", g=NT)
            ch.link(nc.vector.tensor_tensor(wide, segblk[0:WR, :].unsqueeze(1).broadcast_to([WR, NT, SEGS]),
                                            blkw[:, :].unsqueeze(2).broadcast_to([WR, NT, SEGS]), ALU.is_equal))
            ch.link(nc.vector.tensor_tensor(wide, wide, F["segid"][0:WR, :].unsqueeze(1).broadcast_to([WR, NT, SEGS]),
                                            ALU.mult))
            ch.link(nc.vector.tensor_reduce(ix[0:WR, 0:NT], wide, X, ALU.max))
            ch.link(nc.vector.tensor_scalar(ix[0:WR, 16:32], ix[0:WR, 0:NT], 0.0, FAR, ALU.is_equal, ALU.mult))
            ch.link(nc.vector.scalar_tensor_tensor(new_i[:, :], ix[0:WR, 0:NT], -1.0, ix[0:WR, 16:32], ALU.add,
                                                   ALU.add))
            dve.wait_ge(s["destld"], 16 * (NEWB + 1))
            toks = cmpt[0:B, 0:S * NEWB * BLOCK].rearrange("p (t u) -> p t u", t=S)
            ch.link(nc.vector.scalar_tensor_tensor(
                toks, F["shift"][0:B, :].rearrange("p (t u) -> p t u", t=S), off0[0:B, NT:NT + 1],
                rest[0:B, 4402:4450].unsqueeze(1).broadcast_to([B, S, NEWB * BLOCK]), ALU.is_equal, ALU.mult))
            ch.link(nc.vector.tensor_reduce(eqt[0:B, 0:S], toks, X, ALU.add))
            nc.vector.tensor_copy(rest[0:B, 4450:4482].bitcast(I32), eqt[0:B, 0:S]).then_inc(s["tokst"], 1)
            dve.wait_ge(s["small1"], 80)
            ch.link(nc.vector.tensor_copy(adapt_f, adapt_i))
            for li in range(2):
                ch.link(nc.vector.tensor_scalar(amask[:, li, :], adapt_f[:, li, :], adapt_s[:, 2 * li + 1:2 * li + 2],
                                                adapt_s[:, 2 * li:2 * li + 1], ALU.is_equal, ALU.mult))

            dve.wait_ge(s["x"], 16)
            with dve.Fori(0, NCH) as tc:
                dve.wait_ge(s["ycur_ready"], tc + 1)
                nc.vector.tensor_tensor(ylow1, yT[:, :, bass.ds(tc * CH, CH)], yhigh, ALU.subtract).then_inc(s["ylow_ready"], 1)
                for m in range(M0):
                    dve.wait_ge(s["silu_ready"], tc * M0 + (m + 1))
                    nc.vector.tensor_tensor(silu[:, m % SLOTS, :], silu[:, m % SLOTS, :], ps[:, 2 + m % 2, :], ALU.mult)\
                        .then_inc(s["hfull_ready"], 1)
                    dve_low(dve, m, P, tc * M0)
                dve_residual(dve, tc, 0)
            router = small1[:, :, D + P:]
            high, low = (x[:, 0:KD * E1].rearrange("p (k e) -> p k e", k=KD) for x in (routerh, routerl))
            ch.link(nc.vector.tensor_copy(high, router))
            nc.vector.tensor_tensor(low, router, high, ALU.subtract).then_inc(s["w1l"], 1)
            for i, (low, full, high) in enumerate(((l1_gatel[:, 0, :], l1_gate[:, 0, :], l1_gateh[:, 0, :]),
                                                   (l1_upl[:, 0, :], l1_up[:, 0, :], l1_uph[0]),
                                                   (l1_gatel[:, 1, :], l1_gate[:, 1, :], l1_gateh[:, 1, :]))):
                dve.wait_ge(s["w1h"], i + 1)
                nc.vector.tensor_tensor(low, full, high, ALU.subtract).then_inc(s["w1l"], 1)
            with dve.Fori(0, NCH) as tc:
                moe_dve(dve, L1, 0, tc, s["stdlinks"])
                dve_residual(dve, tc, L1.acc0)

            dve.wait_ge(s["trig"], 1)
            dve.wait_ge(s["small2"], 80)
            nc.vector.tensor_scalar(gain[:, :], gain[:, :], 1.0, None, ALU.add).then_inc(s["gained"], 1)
            dve.wait_ge(s["gained"], 1)
            NH = G * GS + G

            dve.wait_ge(s["keys"], 16)
            keynum, keyless = (zm[:, j * WK:(j + 1) * WK] for j in range(2))
            hi, least = kv_f[:, 2, :], kv_f[:, 3, :]
            ch.link(nc.vector.tensor_scalar(hi, off0, float(WINDOW), None, ALU.add))
            ch.link(nc.vector.tensor_tensor(least, hi, kv, ALU.subtract))

            def per_tile(x):
                return x[:, 0:NT].unsqueeze(2).broadcast_to([P, NT, WK])

            def per_key(x):
                return x.unsqueeze(1).broadcast_to([P, NT, WK])

            ma = early[:, 0:NT * WK].rearrange("p (i c) -> p i c", i=NT)
            mb = early[:, 2 * ROW - NT * WK:2 * ROW].rearrange("p (i c) -> p i c", i=NT)
            ch.link(nc.vector.tensor_tensor(ma, per_key(keyless), per_tile(off0), ALU.is_gt))
            ch.link(nc.vector.tensor_tensor(mb, per_key(keyless), per_tile(hi), ALU.is_le))
            ch.link(nc.vector.tensor_tensor(ma, ma, mb, ALU.mult))
            ch.link(nc.vector.tensor_tensor(mb, per_key(keynum), per_tile(least), ALU.is_ge))
            ch.link(nc.vector.tensor_tensor(ma, ma, mb, ALU.mult))
            nc.vector.tensor_scalar(maskb[:, :], early[:, 0:NT * WK], -MASKED, MASKED, ALU.mult, ALU.add)\
                .then_inc(s["masked"], 1)

            for c in range(NCH):
                ch = Chain(dve, s["qklinks"], c * 6)
                dve.wait_ge(s["squared"], c + 1)
                ch.link(nc.vector.tensor_reduce(kcol[:, 0, :], sqr[c % 2].rearrange("p (h d) -> p h d", d=HD), X, ALU.add))
                nc.vector.tensor_scalar(kcol[:, 1, :], kcol[:, 0, :], 1.0 / HD, EPS, ALU.mult, ALU.add)\
                    .then_inc(s["ssq_ready"], 1)
                dve.wait_ge(s["root_ready"], c + 1)
                ch.link(nc.vector.reciprocal(kcol[:, 1, :], kcol[:, 0, :]))
                dve.wait_ge(s["v_ready"], c + 1)
                qk4 = qkn[c % 2].rearrange("p (t h d) -> p t h d", t=TPC, d=HD)
                for t in range(TPC):
                    last = nc.vector.tensor_tensor(
                        qk4[:, t, :, :], ps[:, t, 0:384].rearrange("p (h d) -> p h d", d=HD),
                        kcol[:, 1, t * NH:(t + 1) * NH].unsqueeze(2).broadcast_to([P, NH, HD]), ALU.mult)
                ch.link(last)
                qk3 = qkn[c % 2].rearrange("p (t n) -> p t n", t=TPC)
                ch.link(nc.vector.tensor_tensor(qk3, qk3, gain[:, :].unsqueeze(1).broadcast_to([P, TPC, NH * HD]),
                                                ALU.mult))

                def trig(table):
                    return table[:, c * TPC:(c + 1) * TPC, :].unsqueeze(2).broadcast_to([P, TPC, NH, HD // 2])

                def temp(x):
                    return x.rearrange("p (t h d) -> p t h d", t=TPC, d=HD // 2)

                low, high = qk4[:, :, :, 0:HD // 2], qk4[:, :, :, HD // 2:HD]
                tmp = [temp(work[:, j * 768:(j + 1) * 768]) for j in range(3)] + [temp(sqr[c % 2][:, 0:768])]
                nc.vector.tensor_tensor(tmp[0], low, trig(cosb), ALU.mult)
                nc.vector.tensor_tensor(tmp[1], high, trig(sinb), ALU.mult)
                nc.vector.tensor_tensor(tmp[2], high, trig(cosb), ALU.mult)
                ch.link(nc.vector.tensor_tensor(tmp[3], low, trig(sinb), ALU.mult))
                k4 = kvrow[c % 2][:, :, 0:KW].rearrange("p t (g d) -> p t g d", g=G)
                nq = G * GS
                nc.vector.tensor_tensor(low[:, :, 0:nq, :], tmp[0][:, :, 0:nq, :], tmp[1][:, :, 0:nq, :], ALU.subtract)
                nc.vector.tensor_tensor(high[:, :, 0:nq, :], tmp[2][:, :, 0:nq, :], tmp[3][:, :, 0:nq, :], ALU.add)
                ch.link(nc.vector.tensor_tensor(k4[:, :, :, 0:HD // 2], tmp[0][:, :, nq:, :], tmp[1][:, :, nq:, :],
                                                ALU.subtract))
                nc.vector.tensor_tensor(k4[:, :, :, HD // 2:], tmp[2][:, :, nq:, :], tmp[3][:, :, nq:, :], ALU.add)\
                    .then_inc(s["roped"], 1)
                dve.wait_ge(s["roped"], c + 1)
                assert ch.n == 6

            def block_diagonals(tc, n):
                if n >= 4:
                    dve.wait_ge(s["s_ps"], tc * BPC + (n - 2))
                q = Qbd[:, (n // 2) % 2, :, :].rearrange("p b (g h t) -> p b g h t", g=G, h=GS)
                for g in range(G):
                    rows = slice(g * HD, (g + 1) * HD)
                    src = qT[rows, :, bass.ds(tc * CH + n * S, 2 * S)].rearrange("p h (b t) -> p b h t", b=2)
                    last = nc.vector.tensor_copy(q[rows, :, g, :, :], src)
                last.then_inc(s["qbd_ready"], 2)

            def normalise(tc, n):
                dve.wait_ge(s["rr_ready"], tc * BPC + (n + 1))
                for h in range(2):
                    last = nc.vector.tensor_scalar(Pn[:, n % 3, h, :], Pex[:, n % 2, h, :],
                                                   acol[:, 3, n % 2, h:h + 1], None, ALU.mult)
                last.then_inc(s["pn_ready"], 1)

            def maxima(tc, n):
                dve.wait_ge(s["s_ps"], tc * BPC + (n + 1))
                nc.vector.tensor_reduce(acol[:, 0, n % 2, :],
                                        ps[:, 2 + n % 2, 0:2 * WK].rearrange("p (h c) -> p h c", h=2), X, ALU.max)\
                    .then_inc(s["mlinks"], 1)
                dve.wait_ge(s["mlinks"], tc * BPC + (n + 1))
                nc.vector.tensor_scalar(acol[:, 1, n % 2, :], acol[:, 0, n % 2, :], -SC, None, ALU.mult)\
                    .then_inc(s["nb_ready"], 1)

            def sums(tc, n):
                dve.wait_ge(s["p_ready"], tc * BPC + (n + 1))
                nc.vector.reciprocal(acol[:, 3, n % 2, :], acol[:, 2, n % 2, :]).then_inc(s["rr_ready"], 1)

            def values_out(tc, n):
                dve.wait_ge(s["o_ps"], tc * BPC + (O_CREDIT + n + 1))
                nc.vector.tensor_copy(oT[:, :, n * S:(n + 1) * S],
                                      ps[:, 6 + n % 2, 0:GS * S].rearrange("p (h t) -> p h t", h=GS))\
                    .then_inc(s["o_sb"], 1)

            dve.wait_ge(s["qzero"], 1)
            with dve.Fori(0, NCH) as tc:
                block_diagonals(tc, 0)
                for n in range(1, BPC + 4):
                    if n <= BPC:
                        maxima(tc, n - 1)
                    if n >= 4:
                        values_out(tc, n - 4)
                    if n % 2 == 1 and n + 1 < BPC:
                        block_diagonals(tc, n + 1)
                    if n <= BPC:
                        sums(tc, n - 1)
                        normalise(tc, n - 1)
                ch = Chain(dve, s["chain2"], tc * TAIL_LINKS)
                dve.wait_ge(s["ytok_sb"], tc + 1)
                ch.link(nc.vector.tensor_tensor(ywr, ytok, wr[:, :].unsqueeze(1).broadcast_to([P, TPC, D]), ALU.mult))
                ch.link(nc.vector.tensor_reduce(lcol[:, 0, :], ywr, X, ALU.add))
                ch.link(nc.vector.tensor_scalar(lcol[:, 1, :], lcol[:, 0, :], br[:, 0:1], None, ALU.add))

                def r3(x):
                    return x[:, 0:P].rearrange("p (t e) -> p t e", t=TPC)

                def const(x):
                    return x.unsqueeze(1).broadcast_to([P, TPC, S])

                def over(x, n=S):
                    return x.unsqueeze(2).broadcast_to([P, TPC, n])

                nc.vector.tensor_tensor(r3(rt[0]), const(C["own"]), over(lcol[:, 1, :]), ALU.mult)\
                    .then_inc(s["ldiag_ready"], 1)
                dve.wait_ge(s["lrow_ps"], tc + 1)
                nc.vector.sem_inc(s["passed"], 1)
                lrow = ps[:, 2, 0:P]
                for t in range(TPC):
                    nc.vector.max(top8[:, t, :], lrow[:, t * S:(t + 1) * S])
                ch.link(nc.vector.tensor_tensor(r3(rt[1]), r3(lrow), const(C["own"]), ALU.mult))
                ch.link(nc.vector.tensor_reduce(lcol[:, 2, :], r3(rt[1]), X, ALU.add))
                nc.vector.tensor_tensor(lex[:, :, 0:SEL], top8[:, :, 0:SEL],
                                        top8[:, :, 0:1].broadcast_to([P, TPC, SEL]), ALU.subtract)
                nc.vector.tensor_tensor(lex[:, :, SEL:SEL + 1], lcol[:, 2, :].unsqueeze(2), top8[:, :, 0:1],
                                        ALU.subtract).then_inc(s["lex_ready"], 1)
                ch.link(nc.vector.tensor_tensor(r3(rt[2]), r3(lrow), over(lcol[:, 2, :]), ALU.is_gt))
                ch.link(nc.vector.tensor_tensor(r3(rt[3]), r3(lrow), over(lcol[:, 2, :]), ALU.is_equal))
                ch.link(nc.vector.tensor_tensor(r3(rt[4]), r3(rt[3]), const(C["before"]), ALU.mult))
                ch.link(nc.vector.tensor_tensor(r3(rt[3]), r3(rt[4]), r3(rt[2]), ALU.add))
                ch.link(nc.vector.tensor_reduce(lcol[:, 3, :], r3(rt[3]), X, ALU.add))
                NP = TPC * BPT * SEL
                pk = pick[:, :, :]
                rank3 = C["rank"].unsqueeze(1).broadcast_to([P, TPC, NP])
                place3 = C["place"].rearrange("p (t n) -> p t n", t=TPC)
                ch.link(nc.vector.tensor_tensor(pickw, rank3, over(lcol[:, 3, :], NP), ALU.is_equal))
                ch.link(nc.vector.tensor_tensor(pk, pickw, place3, ALU.mult))
                dve.wait_ge(s["lexe_ready"], tc + 1)
                ch.link(nc.vector.tensor_reduce(lcol[:, 4, :], lexe[:, :, 0:SEL], X, ALU.add))
                ch.link(nc.vector.reciprocal(lcol[:, 5, :], lcol[:, 4, :]))
                ch.link(nc.vector.tensor_tensor(lcol[:, 6, :], lcol[:, 5, :], lexe[:, :, SEL], ALU.mult))
                ch.link(nc.vector.tensor_tensor(pickw, pk, over(lcol[:, 6, :], NP), ALU.mult))
                ch.link(nc.vector.tensor_copy(lcol[:, 7, :], lcol[:, 6, :]))
                nc.vector.tensor_copy(lcol[:, 7, :], lcol[:, 6, :]).then_inc(s["pick_ready"], 1)
                assert ch.n == TAIL_LINKS, ch.n
                dve_residual(dve, tc, 2 * NCH)

            router = small3[:, :, D:]
            high, low = (x[:, 0:KD * L3.RW].rearrange("p (k e) -> p k e", k=KD) for x in (routerh, routerl))
            nc.vector.tensor_copy(high, router).then_inc(s["routed3"], 1)
            dve.wait_ge(s["routed3"], 1)
            nc.vector.tensor_tensor(low, router, high, ALU.subtract).then_inc(s["w3l"], 1)
            for i, (low, full, high) in enumerate(((l3_upl[:, 1, :], l3_up[:, 1, :], l3_uph[:, 1, :]),
                                                   (l3_down2[1], l3_down, l3_down2[0]))):
                dve.wait_ge(s["w3h"], i + 1)
                nc.vector.tensor_tensor(low, full, high, ALU.subtract).then_inc(s["w3l"], 1)
            with dve.Fori(0, NCH) as tc:
                moe_dve(dve, L3, 1, tc, s["chain3"])
                dve_residual(dve, tc, L3.acc0)

        @block.tensor
        def _(pe):
            nc.tensor.sem_inc(s["o_ps"], O_CREDIT)
            pe.wait_ge(s["rowps"], 1)
            nc.tensor.matmul(ps[:, 7, 0:256], C["ones"][0:B, :], diag4[0:B, :, :], start=True, stop=True)\
                .then_inc(s["rowsb"], 1)
            pe.wait_ge(s["rowused"], 1)
            pe.wait_ge(s["xrows"], 16)
            pe.wait_ge(s["wdiag"], 1)
            for c in range(NCH):
                for d in range(KD):
                    for t in range(TPC):
                        i = c * TPC + t
                        last = nc.tensor.matmul(ps[:, 2 * c + d, t * P:(t + 1) * P],
                                                xrows[:, i, d * P:(d + 1) * P], wdiag[:, i, :], start=True, stop=True)
                    last.then_inc(s["y0"], 1)
            pe.wait_ge(s["mix"], 1)
            pe.wait_ge(s["y0s"], 8)
            for c in range(4):
                last = nc.tensor.matmul(ps[:, c, :], C["had"], w2mix[:, 2 * c:2 * c + 2, :], start=True, stop=True)
            last.then_inc(s["had"], 1)
            pe.wait_ge(s["w0l"], 2)
            nc.tensor.sem_inc(s["gu_done"], 1)
            with pe.Fori(0, NCH) as tc:
                pe.wait_ge(s["ylow_ready"], tc + 1)
                for m in range(M0):
                    if m >= 2:
                        pe.wait_ge(s["hfull_ready"], tc * M0 + (m - 1))
                    pe_gate_up(m, P, *parts0)
                    if m == M0 - 1:
                        nc.tensor.sem_inc(s["gu_done"], 1)
                    if m >= 2:
                        pe_down(pe, m - 2, P, l0_down2, True, tc * M0, M0 - 1)
                for m in (M0 - 2, M0 - 1):
                    pe_down(pe, m, P, l0_down2, True, tc * M0, M0 - 1)
                pe.wait_ge(s["acc_used"], tc + 1)
            pe.wait_ge(s["small1"], 80)
            pe.wait_ge(s["castb"], 48)
            with pe.Fori(0, NCH) as tc:
                moe_pe(pe, L1, tc, small1[:, :, 0:D], small1[:, :, D:D + P], b1s,
                       [(l1_gateh[:, k, :], l1_gatel[:, k, :]) for k in range(KD)],
                       [(l1_uph[k], l1_upl[:, k, :]) for k in range(KD)], l1_down,
                       ("w1l", 1 + 2 * KD), ("down1", 16))
            pe.wait_ge(s["wqkv"], 16)
            def projections(c):
                pe.wait_ge(s["xs_ready"], c + 1)
                if c >= 1:
                    pe.wait_ge(s["qklinks"], (c - 1) * 6 + 3)
                for t in range(TPC):
                    for k in range(KD):
                        last = nc.tensor.matmul(ps[:, t, :], ycur[:, k, t * P:(t + 1) * P], wqkv[:, k, :],
                                                start=(k == 0), stop=(k == KD - 1))
                last.then_inc(s["qkv_ready"], 1)

            def queries(c):
                pe.wait_ge(s["roped"], c + 1)
                for t in range(TPC):
                    for h in range(GS):
                        last = nc.tensor.transpose(
                            ps[:, 4 + h, t * P:(t + 1) * P],
                            qkn[c % 2].rearrange("p (t n) -> p t n", t=TPC)[:, t, h * P:(h + 1) * P], ident)
                last.then_inc(s["qps_ready"], 1)

            projections(0)
            pe.wait_ge(s["raw3"], 16)
            aT, wt, bn, wpT = raw3[:, :, 0:64], raw3[:, :, 64:320], raw3[:, :, 320:384], raw3[:, :, 384:640]
            for i in range(KD):
                for k in range(KD):
                    nc.tensor.matmul(ps[:, 6, i * 64:(i + 1) * 64], wt[:, k, i * P:(i + 1) * P], aT[:, k, :],
                                     start=(k == 0), stop=(k == KD - 1))
            for k in range(KD):
                last = nc.tensor.matmul(ps[0:64, 7, 0:D], bn[:, k, :], wpT[:, k, :], start=(k == 0),
                                        stop=(k == KD - 1))
            last.then_inc(s["fin_ready"], 1)
            for c in range(NCH):
                if c + 1 < NCH:
                    projections(c + 1)
                queries(c)
            pe.wait_ge(s["qsb_ready"], NCH)
            pe.wait_ge(s["fint_sb"], 1)
            pe.wait_ge(s["l2w"], 16)
            pe.wait_ge(s["masked"], 1)

            def keys(tc, n):
                t, q = n // BPT, n % BPT
                if q == 0:
                    pe.wait_ge(s["shuf0" if t % 2 == 0 else "shuf1"], (tc * 2 + t // 2 + 1 + t % 2) * TURNED)
                nc.tensor.transpose(ps[:, n % 2, 0:96], kv2[t][0:96, 0, q, 0:KW], ident[0:96, 0:96])
                nc.tensor.transpose(ps[:, n % 2, 96:WK], kv2[t][0:80, 1, q, 0:KW], ident[0:80, 0:80])\
                    .then_inc(s["kt_ps"], 1)

            def scores(tc, n):
                pe.wait_ge(s["kt_sb"], tc * BPC + (n + 1))
                pe.wait_ge(s["qbd_ready"], tc * BPC + (n + 1))
                for h in range(2):
                    out = ps[:, 2 + n % 2, h * WK:(h + 1) * WK]
                    nc.tensor.matmul(out, Qbd[:, (n // 2) % 2, n % 2, h * P:(h + 1) * P], KTs[:, n % 2, :], start=True, stop=False)
                    last = nc.tensor.matmul(out, tselb[:, n % BPT, :],
                                            maskb[:, bass.ds(tc * (TPC * WK) + (n // BPT) * WK, WK)],
                                            start=False, stop=True)
                last.then_inc(s["s_ps"], 1)

            def probs(tc, n):
                pe.wait_ge(s["pn_ready"], tc * BPC + (n + 1))
                bank = ps[:, 4 + n % 2, :]
                for h in range(2):
                    nc.tensor.transpose(bank[0:96, h * P:(h + 1) * P], Pn[:, n % 3, h, 0:96], ident)
                for h in range(2):
                    last = nc.tensor.transpose(bank[0:80, 256 + h * P:256 + (h + 1) * P], Pn[:, n % 3, h, 96:WK],
                                               ident)
                last.then_inc(s["pt_ps"], 1)

            def values(tc, n):
                t, q = n // BPT, n % BPT
                pe.wait_ge(s["pt_sb"], tc * BPC + (n + 1))
                if n >= 2:
                    pe.wait_ge(s["o_sb"], tc * BPC + (n - 1))
                for g in range(G):
                    for h, r in ((0, 96), (1, 80)):
                        last = nc.tensor.matmul(ps[g * HD:(g + 1) * HD, 6 + n % 2, 0:GS * S],
                                                kv2[t][0:r, h, q, KW + g * HD:KW + (g + 1) * HD],
                                                PTs[0:r, n % 2, h, g * GS * S:(g + 1) * GS * S],
                                                start=(h == 0), stop=(h == 1))
                last.then_inc(s["o_ps"], 1)

            with pe.Fori(0, NCH) as tc:
                for n in range(BPC + 4):
                    if n < BPC:
                        keys(tc, n)
                    if 3 <= n < BPC + 3:
                        probs(tc, n - 3)
                    if 1 <= n <= BPC:
                        scores(tc, n - 1)
                    if n >= 4:
                        values(tc, n - 4)
                pe.wait_ge(s["o_sb"], tc * BPC + BPC)
                for t in range(TPC):
                    for h in range(GS):
                        last = nc.tensor.matmul(ps[:, t // 2, (t % 2) * D:(t % 2 + 1) * D],
                                                oT[:, h, t * P:(t + 1) * P], wo[:, h, :],
                                                start=(h == 0), stop=(h == GS - 1))
                last.then_inc(s["ytok_ps"], 1)
                for d in range(KD):
                    for h in range(GS):
                        nc.tensor.matmul(ps[:, 6 + d, :], wo[:, h, d * P:(d + 1) * P], oT[:, h, :],
                                         start=(h == 0), stop=False)
                pe.wait_ge(s["ldiag_ready"], tc + 1)
                nc.tensor.matmul(ps[:, 2, 0:P], C["samebatch"], rt[0][:, 0:P], start=True, stop=True)\
                    .then_inc(s["lrow_ps"], 1)
                pe.wait_ge(s["pick_ready"], tc + 1)
                NP = TPC * BPT * SEL
                for d in range(KD):
                    for t in range(TPC):
                        last = nc.tensor.matmul(ps[:, 3, d * NP:(d + 1) * NP], ytok[:, t, d * P:(d + 1) * P],
                                                pick[:, t, :], start=(t == 0), stop=(t == TPC - 1))
                last.then_inc(s["fx_ps"], 1)
                for t in range(TPC):
                    last = nc.tensor.transpose(ps[0:NP, 4, t * P:(t + 1) * P], pickw[:, t, :], ident)
                last.then_inc(s["pwt_ps"], 1)
                pe.wait_ge(s["fx_sb"], tc + 1)
                for m in range(H2 // P):
                    for k in range(KD):
                        last = nc.tensor.matmul(ps[:, 5, m * NP:(m + 1) * NP], w21[:, k, m * P:(m + 1) * P],
                                                fx[:, k, :], start=(k == 0), stop=(k == KD - 1))
                last.then_inc(s["h_ps"], 1)
                pe.wait_ge(s["h_sb"], tc + 1)
                for m in range(H2 // P):
                    nc.tensor.matmul(ps[0:NP, 0, 0:D], hT2[:, m, :], w22[:, m, :], start=(m == 0), stop=False)
                nc.tensor.matmul(ps[0:NP, 0, 0:D], C["ones"][0:1, 0:NP], b22[0:1, :], start=False, stop=True)\
                    .then_inc(s["outl_ps"], 1)
                pe.wait_ge(s["outl_sb"], tc + 1)
                pe.wait_ge(s["pwt_sb"], tc + 1)
                for d in range(KD):
                    last = nc.tensor.matmul(ps[:, 6 + d, :], outl[0:NP, d * P:(d + 1) * P], pwT[0:NP, :],
                                            start=False, stop=True)
                last.then_inc(s["acc_ready"], 1)
                pe.wait_ge(s["acc_used"], tc + 2 * NCH + 1)

            pe.wait_ge(s["sel3"], 16)
            with pe.Fori(0, NCH) as tc:
                moe_pe(pe, L3, tc, small3[:, :, 0:D], awt, wpb,
                       [(l3_gateh[:, k, :], l3_gatel[:, k, :]) for k in range(KD)],
                       [(l3_uph[:, k, :], l3_upl[:, k, :]) for k in range(KD)], l3_down2,
                       ("w3l", 2 + 2 * KD), ("w3l", 2 + 2 * KD))


def kernel(**inputs):
    import numpy as _np
    import concourse.bacc as _bacc
    from concourse import mybir as _mybir
    from concourse.bass_utils import run_bass_kernel_spmd as _run

    v = {k: _np.asarray(x) for k, x in inputs.items()}

    def fold(w):
        return w.reshape(KD, P, -1).transpose(1, 0, 2)

    def tokens(x):
        return _np.repeat(x, S).reshape(NT, P).T

    x = v["x"].reshape(T, D)
    qkv = _np.concatenate([v["L2_cond_Wq"].T.reshape(D, G, GS, HD).transpose(0, 2, 1, 3).reshape(D, -1),
                           v["L2_cond_Wk"].T, v["L2_cond_Wv"].T], axis=1)
    wo = v["L2_cond_Wo"].T.reshape(G, GS, HD, D).transpose(0, 2, 1, 3).reshape(P, GS, D)
    up1 = v["L1_ffn_gate_up_proj"].transpose(1, 0, 2)
    w1 = v["L3_ffn_w1"].transpose(2, 0, 1)
    gu = v["L3_ffn_shared_gate_up_w"].T
    down3 = _np.concatenate([v["L3_ffn_w2"].transpose(0, 2, 1).reshape(E3 * F3, D), v["L3_ffn_shared_down_w"].T,
                             _np.zeros((L3.M * P - N3, D), _np.float32)])
    scal1 = _np.repeat(v["L1_cond_scalings"], R)
    scal3 = _np.tile(_np.repeat(v["L3_cond_scaling"], R), 2)
    row = _np.arange(P) // R
    (_, late), (_, first), (_, cast) = constants()
    kvlen = v["itok_B_37_3939"]
    arrays = {
        "cond": tokens(v["itok_B_1_198"]),
        "kv": _np.concatenate([tokens(kvlen), _np.tile(kvlen, 2)[:, None]], axis=1),
        "tables": v["itok_Bx257_0_4111"],
        "adapt": _np.broadcast_to(_np.stack([v["itok_B_0_6"], v["itok_B_0_3"]])[None], (P, 2, B)),
        "adapt_s": _np.stack([scal1, row.astype(_np.float32), scal3, (row % 4).astype(_np.float32)], axis=1),
        "late": late, "first": first, "cast": cast,
        "xrows": x.reshape(NT, P, D).transpose(1, 0, 2),
        "xT": fold(x.T),
        "cond_w": v["L0_cond_weights"].reshape(-1, S),
        "w13": _np.concatenate([fold(v["L0_ffn_W1"].T).reshape(P, -1), fold(v["L0_ffn_W3"].T).reshape(P, -1)], 1),
        "w2": v["L0_ffn_W2"].T.reshape(M0, P, D).transpose(1, 0, 2),
        "small1": fold(_np.concatenate([v["L1_cond_W"].T, v["L1_cond_A"].reshape(P, D).T, v["L1_ffn_gate"]], 1)),
        "b1": v["L1_cond_Bm"].transpose(0, 2, 1).reshape(P, D),
        "gate1": fold(up1[:, :, :F1].reshape(D, N1)),
        "up1": fold(up1[:, :, F1:].reshape(D, N1)),
        "down1": v["L1_ffn_down_proj"].reshape(L1.M, P, D).transpose(1, 0, 2),
        "cache": _np.concatenate([v["L2_cond_k_blocks"].transpose(0, 2, 1, 3).reshape(NROWS, BLOCK, KW),
                                  v["L2_cond_v_blocks"].transpose(0, 2, 1, 3).reshape(NROWS, BLOCK, KW)],
                                 axis=2).reshape(NROWS, ROW),
        "l2w": _np.concatenate([fold(qkv).reshape(P, -1), wo.reshape(P, -1), fold(v["L2_ffn_W1"]).reshape(P, -1),
                                v["L2_ffn_W2"].reshape(H2 // P, P, D).transpose(1, 0, 2).reshape(P, -1)], axis=1),
        "gq": v["L2_cond_q_norm_scale"], "gk": v["L2_cond_k_norm_scale"],
        "wr": _np.broadcast_to(v["L2_ffn_Wr"].reshape(1, D), (P, D)),
        "b21": v["L2_ffn_b1"].reshape(H2 // P, P).T,
        "b22": v["L2_ffn_b2"].reshape(1, D),
        "br": _np.broadcast_to(v["L2_ffn_br"].reshape(1, 1), (P, 1)),
        "small3": fold(_np.concatenate([v["L3_cond_W_base"].T, v["L3_ffn_gate_w"].T, v["L3_ffn_shared_gate_w"].T,
                                     _np.zeros((D, L3.RW - L3.EW), _np.float32)], 1)),
        "raw3": fold(_np.concatenate([v["L3_cond_A"].reshape(64, D).T, v["L3_cond_Wt"],
                                      v["L3_cond_B_w"].transpose(1, 0, 2).reshape(D, 64), v["L3_cond_Wp"].T], 1)),
        "gu3": _np.concatenate([
            fold(_np.concatenate([w1[:, :, :F3].reshape(D, -1), gu[:, :FS]], axis=1)).reshape(P, -1),
            fold(_np.concatenate([w1[:, :, F3:].reshape(D, -1), gu[:, FS:]], axis=1)).reshape(P, -1)], axis=1),
        "down3": down3.reshape(L3.M, P, D).transpose(1, 0, 2),
    }
    arrays["gain"] = _np.broadcast_to(_np.concatenate([_np.tile(arrays.pop("gq"), G * GS),
                                                       _np.tile(arrays.pop("gk"), G)])[None], (P, 384))
    nc = _bacc.Bacc("TRN2", target_bir_lowering=False, num_devices=1)
    sent, a = {}, {}
    for name, x in arrays.items():
        x = _np.ascontiguousarray(x)
        sent[f"in_{name}"] = x
        a[name] = nc.dram_tensor(f"in_{name}", x.shape, _mybir.dt.from_np(x.dtype), kind="ExternalInput").ap()
    a["out"] = nc.dram_tensor("out_x", (P, KD, T), _mybir.dt.float32, kind="ExternalOutput").ap()
    build(nc, a)
    r = _run(nc, [sent], core_ids=[0])
    got = r.results[0]["out_x"]
    return got.transpose(1, 0, 2).reshape(D, T).T.reshape(B, S, D)
```
